# Optimizing a Trainium2 kernel written in Bass

```python
import numpy as np
import jax
import jax.numpy as jnp

def _softmax(x, axis=-1):
    return jax.nn.softmax(x, axis=axis)

def _gelu(x):
    return jax.nn.gelu(x, approximate=True)

def _silu(x):
    return jax.nn.silu(x)

def _sigmoid(x):
    return jax.nn.sigmoid(x)

def _layernorm(x, axis=-1, eps=1e-05):
    m = jnp.mean(x, axis=axis, keepdims=True)
    v = jnp.var(x, axis=axis, keepdims=True)
    return (x - m) / jnp.sqrt(v + eps)

def _scatter_add(tgt, idx, src, axis=0):
    return tgt.at[idx].add(src)

def _segment_sum(src, seg, n):
    return jax.ops.segment_sum(src, seg, n)
kernel_name = 'mk_recurrent_d2_jaxref_r8_03f8a8'

def setup_inputs(seed: int=0):
    np.random.seed(seed)
    _w = jnp.asarray

    def _L0_attn_setup():
        import jax, jax.numpy as jnp
        import numpy as np
        key = jax.random.key(seed)
        B, L, D, N = (2, 256, 128, 16)
        ks = jax.random.split(key, 8)
        s = 1.0 / np.sqrt(D)
        A_log = jnp.log(jnp.broadcast_to(jnp.arange(1, N + 1, dtype=jnp.float32), (D, N)))
        return {'x': jax.random.normal(ks[0], (B, L, D), jnp.float32), 'Wz': jax.random.normal(ks[1], (D, D), jnp.float32) * s, 'bz': jnp.zeros((D,), jnp.float32), 'Wx': jax.random.normal(ks[2], (D, D), jnp.float32) * s, 'bx': jnp.zeros((D,), jnp.float32), 'WB': jax.random.normal(ks[3], (D, N), jnp.float32) * s, 'bB': jnp.zeros((N,), jnp.float32), 'WC': jax.random.normal(ks[4], (D, N), jnp.float32) * s, 'bC': jnp.zeros((N,), jnp.float32), 'Wdt': jax.random.normal(ks[5], (D, D), jnp.float32) * s, 'bdt': jnp.zeros((D,), jnp.float32), 'A_log': A_log, 'Wout': jax.random.normal(ks[6], (D, D), jnp.float32) * s, 'bout': jnp.zeros((D,), jnp.float32)}
    _L0_attn_in = _L0_attn_setup()

    def _L0_ffn_setup():
        import jax, jax.numpy as jnp
        import numpy as np
        B, S, D, F, E, K = (4, 256, 128, 512, 8, 2)
        key = jax.random.key(seed)
        ks = jax.random.split(key, 8)
        x = jax.random.normal(ks[0], (B, S, D), dtype=jnp.float32)
        router_w = jax.random.normal(ks[1], (E, D), dtype=jnp.float32) * 0.02
        w1_w = jax.random.normal(ks[2], (E, F, D), dtype=jnp.float32) * 0.02
        w1_b = jax.random.normal(ks[3], (E, F), dtype=jnp.float32) * 0.02
        w2_w = jax.random.normal(ks[4], (E, D, F), dtype=jnp.float32) * 0.02
        w2_b = jax.random.normal(ks[5], (E, D), dtype=jnp.float32) * 0.02
        wg_w = jax.random.normal(ks[6], (E, F, D), dtype=jnp.float32) * 0.02
        wg_b = jax.random.normal(ks[7], (E, F), dtype=jnp.float32) * 0.02
        return {'x': x, 'router_w': router_w, 'w1_w': w1_w, 'w1_b': w1_b, 'w2_w': w2_w, 'w2_b': w2_b, 'wg_w': wg_w, 'wg_b': wg_b}
    _L0_ffn_in = _L0_ffn_setup()

    def _L1_attn_setup():
        import jax, jax.numpy as jnp
        import numpy as np
        B, S, D = (4, 256, 128)
        key = jax.random.key(seed)
        kx, kq, kk, kv = jax.random.split(key, 4)
        bound = float(np.sqrt(6.0 / (D + D)))
        return {'x': jax.random.normal(kx, (B, S, D), dtype=jnp.float32), 'WQ': jax.random.uniform(kq, (D, D), jnp.float32, -bound, bound), 'WK': jax.random.uniform(kk, (D, D), jnp.float32, -bound, bound), 'WV': jax.random.uniform(kv, (D, D), jnp.float32, -bound, bound)}
    _L1_attn_in = _L1_attn_setup()

    def _L1_ffn_setup():
        import jax, jax.numpy as jnp
        import numpy as np
        B, T, C = (2, 256, 128)
        H, D = (16, 64)
        CR = 8
        R = C // CR
        ROPE = D // 2
        NOPE = D - ROPE
        E, K, I, S = (8, 2, 64, 1)
        THETA = 100000.0
        EPS = 1e-05

        def _rmsnorm(x, w):
            rms = jnp.sqrt(jnp.mean(x * x, axis=-1, keepdims=True) + EPS)
            return w * (x / rms)

        def _rope(xh):
            d = xh.shape[-1]
            t = jnp.arange(xh.shape[2], dtype=jnp.float32)
            freqs = 1.0 / THETA ** (jnp.arange(0, d, 2, dtype=jnp.float32) / d)
            ang = jnp.outer(t, freqs)
            cos, sin = (jnp.cos(ang), jnp.sin(ang))
            xr = xh.reshape(xh.shape[:-1] + (d // 2, 2))
            x0, x1 = (xr[..., 0], xr[..., 1])
            rot = jnp.stack([x0 * cos - x1 * sin, x0 * sin + x1 * cos], axis=-1)
            return rot.reshape(xh.shape)

        def _attention(x, Wq, Wkva, Wkvb, Wo):
            b, t, _ = x.shape
            q = (x @ Wq).reshape(b, t, H, D).transpose(0, 2, 1, 3)
            ckv = x @ Wkva
            kv_latent, k_rope = (ckv[:, :, :R], ckv[:, :, R:])
            kv = (kv_latent @ Wkvb).reshape(b, t, H, NOPE).transpose(0, 2, 1, 3)
            k_rope = jnp.broadcast_to(k_rope[:, None, :, :], (b, H, t, ROPE))
            q_nope, q_rope = (q[..., :NOPE], q[..., NOPE:])
            q = jnp.concatenate([q_nope, _rope(q_rope)], axis=-1)
            k = jnp.concatenate([kv, _rope(k_rope)], axis=-1)
            v = jnp.concatenate([kv, jnp.zeros_like(k_rope)], axis=-1)
            att = jnp.einsum('bhqd,bhkd->bhqk', q, k) / jnp.sqrt(jnp.float32(D))
            mask = jnp.tril(jnp.ones((t, t), dtype=bool))
            att = jnp.where(mask, att, jnp.float32(-jnp.inf))
            att = jax.nn.softmax(att, axis=-1)
            y = jnp.einsum('bhqk,bhkd->bhqd', att, v)
            y = y.transpose(0, 2, 1, 3).reshape(b, t, H * D)
            return y @ Wo

        def _experts(x_flat, Wg, Wu, Wd):
            g = jax.nn.silu(jnp.einsum('nc,eci->nei', x_flat, Wg))
            u = jnp.einsum('nc,eci->nei', x_flat, Wu)
            return jnp.einsum('nei,eic->nec', g * u, Wd)

        def _moe(x, Wgate, expert_bias, Wg, Wu, Wd, sWg, sWu, sWd):
            b, t, c = x.shape
            xf = x.reshape(-1, c)
            shared = jnp.mean(_experts(xf, sWg, sWu, sWd), axis=1)
            logits = xf @ Wgate + expert_bias
            probs = jax.nn.softmax(logits, axis=-1)
            topk_p, topk_i = jax.lax.top_k(probs, K)
            topk_p = topk_p / jnp.sum(topk_p, axis=-1, keepdims=True)
            comb = jnp.sum(jax.nn.one_hot(topk_i, E, dtype=xf.dtype) * topk_p[..., None], axis=1)
            routed = jnp.einsum('ne,nec->nc', comb, _experts(xf, Wg, Wu, Wd))
            return (shared + routed).reshape(b, t, c)
        key = jax.random.key(seed)
        ks = jax.random.split(key, 16)
        w = lambda k, shp: jax.random.normal(k, shp, dtype=jnp.float32) * 0.02
        return {'x': jax.random.normal(ks[0], (B, T, C), dtype=jnp.float32), 'w_ln1': jnp.ones((C,), jnp.float32), 'Wq': w(ks[1], (C, H * D)), 'Wkva': w(ks[2], (C, R + ROPE)), 'Wkvb': w(ks[3], (R, H * NOPE)), 'Wo': w(ks[4], (H * D, C)), 'w_ln2': jnp.ones((C,), jnp.float32), 'Wgate': w(ks[5], (C, E)), 'expert_bias': jnp.zeros((E,), jnp.float32), 'Wg': w(ks[6], (E, C, I)), 'Wu': w(ks[7], (E, C, I)), 'Wd': w(ks[8], (E, I, C)), 'sWg': w(ks[9], (S, C, I)), 'sWu': w(ks[10], (S, C, I)), 'sWd': w(ks[11], (S, I, C))}
    _L1_ffn_in = _L1_ffn_setup()
    _d = {'L0_attn_x': _L0_attn_in['x'], 'L0_attn_Wz': _L0_attn_in['Wz'], 'L0_attn_bz': _L0_attn_in['bz'], 'L0_attn_Wx': _L0_attn_in['Wx'], 'L0_attn_bx': _L0_attn_in['bx'], 'L0_attn_WB': _L0_attn_in['WB'], 'L0_attn_bB': _L0_attn_in['bB'], 'L0_attn_WC': _L0_attn_in['WC'], 'L0_attn_bC': _L0_attn_in['bC'], 'L0_attn_Wdt': _L0_attn_in['Wdt'], 'L0_attn_bdt': _L0_attn_in['bdt'], 'L0_attn_A_log': _L0_attn_in['A_log'], 'L0_attn_Wout': _L0_attn_in['Wout'], 'L0_attn_bout': _L0_attn_in['bout'], 'L0_ffn_router_w': _L0_ffn_in['router_w'], 'L0_ffn_w1_w': _L0_ffn_in['w1_w'], 'L0_ffn_w1_b': _L0_ffn_in['w1_b'], 'L0_ffn_w2_w': _L0_ffn_in['w2_w'], 'L0_ffn_w2_b': _L0_ffn_in['w2_b'], 'L0_ffn_wg_w': _L0_ffn_in['wg_w'], 'L0_ffn_wg_b': _L0_ffn_in['wg_b'], 'L1_attn_WQ': _L1_attn_in['WQ'], 'L1_attn_WK': _L1_attn_in['WK'], 'L1_attn_WV': _L1_attn_in['WV'], 'L1_ffn_w_ln1': _L1_ffn_in['w_ln1'], 'L1_ffn_Wq': _L1_ffn_in['Wq'], 'L1_ffn_Wkva': _L1_ffn_in['Wkva'], 'L1_ffn_Wkvb': _L1_ffn_in['Wkvb'], 'L1_ffn_Wo': _L1_ffn_in['Wo'], 'L1_ffn_w_ln2': _L1_ffn_in['w_ln2'], 'L1_ffn_Wgate': _L1_ffn_in['Wgate'], 'L1_ffn_expert_bias': _L1_ffn_in['expert_bias'], 'L1_ffn_Wg': _L1_ffn_in['Wg'], 'L1_ffn_Wu': _L1_ffn_in['Wu'], 'L1_ffn_Wd': _L1_ffn_in['Wd'], 'L1_ffn_sWg': _L1_ffn_in['sWg'], 'L1_ffn_sWu': _L1_ffn_in['sWu'], 'L1_ffn_sWd': _L1_ffn_in['sWd']}
    _x0 = _d['L0_attn_x']
    _d['L0_attn_x'] = jax.random.normal(jax.random.fold_in(jax.random.key(seed), 1), (8, 512, 128), dtype=_x0.dtype)
    del _x0
    return _d

def reference(L0_attn_x, L0_attn_Wz, L0_attn_bz, L0_attn_Wx, L0_attn_bx, L0_attn_WB, L0_attn_bB, L0_attn_WC, L0_attn_bC, L0_attn_Wdt, L0_attn_bdt, L0_attn_A_log, L0_attn_Wout, L0_attn_bout, L0_ffn_router_w, L0_ffn_w1_w, L0_ffn_w1_b, L0_ffn_w2_w, L0_ffn_w2_b, L0_ffn_wg_w, L0_ffn_wg_b, L1_attn_WQ, L1_attn_WK, L1_attn_WV, L1_ffn_w_ln1, L1_ffn_Wq, L1_ffn_Wkva, L1_ffn_Wkvb, L1_ffn_Wo, L1_ffn_w_ln2, L1_ffn_Wgate, L1_ffn_expert_bias, L1_ffn_Wg, L1_ffn_Wu, L1_ffn_Wd, L1_ffn_sWg, L1_ffn_sWu, L1_ffn_sWd):

    def _L0_attn_ref(x, Wz, bz, Wx, bx, WB, bB, WC, bC, Wdt, bdt, A_log, Wout, bout):
        import jax, jax.numpy as jnp
        import numpy as np
        B, L, D = x.shape
        N = A_log.shape[1]
        z = jax.nn.sigmoid(x @ Wz + bz)
        x_ssm = x @ Wx + bx
        Bm = x @ WB + bB
        C = x @ WC + bC
        dt = jax.nn.softplus(x @ Wdt + bdt)
        A = -jnp.exp(A_log)
        A_bar = jnp.exp(dt[..., None] * A)
        x_db = x_ssm[..., None] * (dt[..., None] * Bm[..., None, :])
        a_scan = jnp.transpose(A_bar, (1, 0, 2, 3))
        x_scan = jnp.transpose(x_db, (1, 0, 2, 3))
        c_scan = jnp.transpose(C, (1, 0, 2))

        def ssm_step(h, inp):
            a_t, x_t, c_t = inp
            h_new = a_t * h + x_t
            y_t = jnp.einsum('bdn,bn->bd', h_new, c_t)
            return (h_new, y_t)
        h0 = jnp.zeros((B, D, N), x.dtype)
        _, y_ssm = jax.lax.scan(ssm_step, h0, (a_scan, x_scan, c_scan))
        y_ssm = jnp.transpose(y_ssm, (1, 0, 2))
        y = y_ssm * z
        return y @ Wout + bout

    def _L0_ffn_ref(x, router_w, w1_w, w1_b, w2_w, w2_b, wg_w, wg_b):
        import jax, jax.numpy as jnp
        import numpy as np
        B, S, D, F, E, K = (4, 256, 128, 512, 8, 2)
        probs = jax.nn.softmax(jnp.einsum('bsd,ed->bse', x, router_w), axis=-1)
        token_probs, probs_idx = jax.lax.top_k(probs, K)
        gates = jnp.sum(token_probs[..., None] * jax.nn.one_hot(probs_idx, E, dtype=x.dtype), axis=-2)
        gates_e = jnp.moveaxis(gates, -1, 0)

        def body(acc, params):
            w1w, w1b, w2w, w2b, wgw, wgb, g = params
            y = jax.nn.gelu(jnp.einsum('bsd,fd->bsf', x, wgw) + wgb, approximate=False)
            h = y * (jnp.einsum('bsd,fd->bsf', x, w1w) + w1b)
            out = jnp.einsum('bsf,df->bsd', h, w2w) + w2b
            return (acc + out * g[..., None], None)
        acc0 = jnp.zeros_like(x)
        out, _ = jax.lax.scan(body, acc0, (w1_w, w1_b, w2_w, w2_b, wg_w, wg_b, gates_e))
        return out

    def _L1_attn_ref(x, WQ, WK, WV):
        import jax, jax.numpy as jnp
        import numpy as np
        B, S, D = (4, 256, 128)
        dk = WQ.shape[1]
        q = x @ WQ
        k = x @ WK
        v = x @ WV
        scores = jnp.einsum('bsd,btd->bst', q, k) / jnp.sqrt(jnp.asarray(dk, x.dtype))
        s = x.shape[1]
        causal = jnp.tril(jnp.ones((s, s), dtype=bool))
        scores = jnp.where(causal[None, :, :], scores, jnp.asarray(-jnp.inf, x.dtype))
        attention = jax.nn.softmax(scores, axis=-1)
        return jnp.einsum('bst,btd->bsd', attention, v)

    def _L1_ffn_ref(x, w_ln1, Wq, Wkva, Wkvb, Wo, w_ln2, Wgate, expert_bias, Wg, Wu, Wd, sWg, sWu, sWd):
        import jax, jax.numpy as jnp
        import numpy as np
        B, T, C = (2, 256, 128)
        H, D = (16, 64)
        CR = 8
        R = C // CR
        ROPE = D // 2
        NOPE = D - ROPE
        E, K, I, S = (8, 2, 64, 1)
        THETA = 100000.0
        EPS = 1e-05

        def _rmsnorm(x, w):
            rms = jnp.sqrt(jnp.mean(x * x, axis=-1, keepdims=True) + EPS)
            return w * (x / rms)

        def _rope(xh):
            d = xh.shape[-1]
            t = jnp.arange(xh.shape[2], dtype=jnp.float32)
            freqs = 1.0 / THETA ** (jnp.arange(0, d, 2, dtype=jnp.float32) / d)
            ang = jnp.outer(t, freqs)
            cos, sin = (jnp.cos(ang), jnp.sin(ang))
            xr = xh.reshape(xh.shape[:-1] + (d // 2, 2))
            x0, x1 = (xr[..., 0], xr[..., 1])
            rot = jnp.stack([x0 * cos - x1 * sin, x0 * sin + x1 * cos], axis=-1)
            return rot.reshape(xh.shape)

        def _attention(x, Wq, Wkva, Wkvb, Wo):
            b, t, _ = x.shape
            q = (x @ Wq).reshape(b, t, H, D).transpose(0, 2, 1, 3)
            ckv = x @ Wkva
            kv_latent, k_rope = (ckv[:, :, :R], ckv[:, :, R:])
            kv = (kv_latent @ Wkvb).reshape(b, t, H, NOPE).transpose(0, 2, 1, 3)
            k_rope = jnp.broadcast_to(k_rope[:, None, :, :], (b, H, t, ROPE))
            q_nope, q_rope = (q[..., :NOPE], q[..., NOPE:])
            q = jnp.concatenate([q_nope, _rope(q_rope)], axis=-1)
            k = jnp.concatenate([kv, _rope(k_rope)], axis=-1)
            v = jnp.concatenate([kv, jnp.zeros_like(k_rope)], axis=-1)
            att = jnp.einsum('bhqd,bhkd->bhqk', q, k) / jnp.sqrt(jnp.float32(D))
            mask = jnp.tril(jnp.ones((t, t), dtype=bool))
            att = jnp.where(mask, att, jnp.float32(-jnp.inf))
            att = jax.nn.softmax(att, axis=-1)
            y = jnp.einsum('bhqk,bhkd->bhqd', att, v)
            y = y.transpose(0, 2, 1, 3).reshape(b, t, H * D)
            return y @ Wo

        def _experts(x_flat, Wg, Wu, Wd):
            g = jax.nn.silu(jnp.einsum('nc,eci->nei', x_flat, Wg))
            u = jnp.einsum('nc,eci->nei', x_flat, Wu)
            return jnp.einsum('nei,eic->nec', g * u, Wd)

        def _moe(x, Wgate, expert_bias, Wg, Wu, Wd, sWg, sWu, sWd):
            b, t, c = x.shape
            xf = x.reshape(-1, c)
            shared = jnp.mean(_experts(xf, sWg, sWu, sWd), axis=1)
            logits = xf @ Wgate + expert_bias
            probs = jax.nn.softmax(logits, axis=-1)
            topk_p, topk_i = jax.lax.top_k(probs, K)
            topk_p = topk_p / jnp.sum(topk_p, axis=-1, keepdims=True)
            comb = jnp.sum(jax.nn.one_hot(topk_i, E, dtype=xf.dtype) * topk_p[..., None], axis=1)
            routed = jnp.einsum('ne,nec->nc', comb, _experts(xf, Wg, Wu, Wd))
            return (shared + routed).reshape(b, t, c)
        x = x + _attention(_rmsnorm(x, w_ln1), Wq, Wkva, Wkvb, Wo)
        residual = x
        xn = _rmsnorm(x, w_ln2)
        x_out = _moe(xn, Wgate, expert_bias, Wg, Wu, Wd, sWg, sWu, sWd)
        return residual + x_out
    x = L0_attn_x
    xn = _layernorm(x, axis=-1)
    s = _L0_attn_ref(xn, L0_attn_Wz, L0_attn_bz, L0_attn_Wx, L0_attn_bx, L0_attn_WB, L0_attn_bB, L0_attn_WC, L0_attn_bC, L0_attn_Wdt, L0_attn_bdt, L0_attn_A_log, L0_attn_Wout, L0_attn_bout)
    g = _silu(_L0_ffn_ref(xn, L0_ffn_router_w, L0_ffn_w1_w, L0_ffn_w1_b, L0_ffn_w2_w, L0_ffn_w2_b, L0_ffn_wg_w, L0_ffn_wg_b))
    x = x + s * g
    xn = _layernorm(x, axis=-1)
    s = _L1_attn_ref(xn, L1_attn_WQ, L1_attn_WK, L1_attn_WV)
    g = _silu(_L1_ffn_ref(xn, L1_ffn_w_ln1, L1_ffn_Wq, L1_ffn_Wkva, L1_ffn_Wkvb, L1_ffn_Wo, L1_ffn_w_ln2, L1_ffn_Wgate, L1_ffn_expert_bias, L1_ffn_Wg, L1_ffn_Wu, L1_ffn_Wd, L1_ffn_sWg, L1_ffn_sWu, L1_ffn_sWd))
    x = x + s * g
    return x

_drawn_inputs = setup_inputs


def setup_inputs(seed=0):
    import zlib

    import numpy as np

    out = dict(_drawn_inputs(seed))
    spreads = {'L0_attn_bz': (0.0, 0.1),
     'L0_attn_bx': (0.0, 0.1),
     'L0_attn_bB': (0.0, 0.1),
     'L0_attn_bC': (0.0, 0.1),
     'L0_attn_bdt': (0.0, 0.1),
     'L0_attn_bout': (0.0, 0.1),
     'L1_ffn_w_ln1': (1.0, 0.2),
     'L1_ffn_w_ln2': (1.0, 0.2),
     'L1_ffn_expert_bias': (0.0, 0.1)}
    factors = {}
    for name, (base, spread) in spreads.items():
        noise = np.random.default_rng([zlib.crc32(name.encode()), seed]).standard_normal(out[name].shape)
        drawn = base * np.exp(spread * noise) if base else spread * noise
        out[name] = jnp.asarray(drawn.astype(out[name].dtype))
    for name, factor in factors.items():
        out[name] = (out[name] * factor).astype(out[name].dtype)
    return out
```

```python
from contextlib import ExitStack

import numpy as np

import concourse.bass as bass
from concourse import mybir

ALU = mybir.AluOpType
ACT = mybir.ActivationFunctionType
AX = mybir.AxisListType.X
F32 = mybir.dt.float32
BF16 = mybir.dt.bfloat16

P = 128
B, L = 8, 512
J = L // P
NS = 16
E, FF = 8, 512
FT = FF // P
H, HP = 16, 8
ROPE, LAT = 32, 16
KD = ROPE + LAT + 1
I1 = 64
MT = E * I1 // P
EPS = 1e-5
MASKED = -1e30

WEIGHTS = [
    ("ident", [P, P]), ("sel_bc", [96, 32 * P]), ("mask", [P, P]), ("mask_t", [P, P]), ("cos", [P, L]), ("sin", [P, L]),
    ("one_row", [P, 1]), ("lower", [P, E * E]), ("sel_den", [P, P]), ("sel_comb", [E, MT * P]),
    ("wz", [P, P]), ("wx", [P, P]), ("wdt", [P, P]), ("wbc", [P, 96]), ("a_log", [P, NS]), ("wout", [P, P]),
    ("bz", [P, 1]), ("bx", [P, 1]), ("bdt", [P, 1]), ("bbc", [96, 1]), ("bout", [P, P]),
    ("router0", [P, E]), ("w1", [P, E * FF]), ("wg", [P, E * FF]), ("w2", [P, E * FT * P]),
    ("b1", [P, E * FT]), ("bg", [P, E * FT]), ("b2", [E, P]),
    ("wq1", [P, P]), ("wk1", [P, P]), ("wv1", [P, P]),
    ("ln1", [P, 1]), ("ln2", [P, 1]), ("wq", [P, HP * P]), ("wq_swap", [P, HP * P]), ("wk", [P, P]), ("wk_swap", [P, P]),
    ("wq_nope_t", [32, H * P]), ("wkvb_t", [32, H * LAT]), ("wo_nope", [32, H * P]), ("wlat", [P, LAT]),
    ("router1", [P, E]), ("bias1", [P, E]), ("wg1", [P, (MT + 1) * P]), ("wu1", [P, (MT + 1) * P]), ("wd1", [P, (MT + 1) * P]),
]
SETUP_ONLY = {"sel_bc", "mask", "mask_t", "wq_nope_t", "wkvb_t", "wo_nope", "a_log"}
LAYER0_ONLY = {"w1", "wg", "w2", "b1", "bg", "b2", "router0", "wz", "wx", "wdt", "wbc", "wout", "bz", "bx", "bdt", "bbc", "bout"}
BROADCAST = {"bout", "bias1"}


def two_layers(nc, x, w, out):
    with ExitStack() as ctx:
        def sb(name, shape, dt=F32):
            return ctx.enter_context(nc.sbuf_tensor(name, shape, dt))

        def sems(names):
            return [ctx.enter_context(nc.semaphore(n)) for n in names.split()]

        c = {name: sb("c_" + name, shape) for name, shape in WEIGHTS
             if name not in SETUP_ONLY | LAYER0_ONLY}
        bank = [ctx.enter_context(nc.psum_tensor(f"bank{i}", [P, 2, L], F32)) for i in range(4)]

        def bk(i):
            return bank[i // 2][:, i % 2, :]

        ident16 = sb("ident16", [P, P], BF16)
        mask16 = sb("mask16", [P, P], BF16)
        mask_t16 = sb("mask_t16", [P, P], BF16)
        neg_a = sb("neg_a", [P, NS])
        neg_bz = sb("neg_bz", [P, 1])
        eps = sb("eps", [P, 1])
        wvo = sb("wvo", [P, 4, P])
        vaug = sb("vaug", [P, J, 32])
        x1 = sb("x1", [P, B, J, P])

        xt = sb("xt", [P, J, P])
        stats = sb("stats", [P, J, 6])
        mv = sb("mv", [P, J, 2])
        std = sb("std", [P, J])
        rstd = sb("rstd", [P, J])
        xn = sb("xn", [P, J, P])
        xn_t = sb("xn_t", [P, L])
        prob = sb("prob", [P, J, E])
        small = sb("small", [P, J, 4])
        cmp_a = sb("cmp_a", [P, J, E, E])
        cmp_b = sb("cmp_b", [P, J, E, E])
        rank = sb("rank", [P, J, E])
        gates = sb("gates", [P, J, E])
        gates_t = sb("gates_t", [E, L])
        srow = sb("srow", [P, J, P])
        macc = sb("macc", [P, J, P])
        grow = sb("grow", [P, J, P])

        only0 = ctx.enter_context(ExitStack())
        sel_bc = only0.enter_context(nc.sbuf_tensor("sel_bc16", [96, 32, P], BF16))
        for name, shape in WEIGHTS:
            if name in LAYER0_ONLY:
                c[name] = only0.enter_context(nc.sbuf_tensor("c_" + name, shape, F32))
        (setup_in, setup_mm, setup_act, setup_dve, setup_done) = sems(
            "setup_in setup_mm setup_act setup_dve setup_done")

        with ExitStack() as own:
            for name, shape in WEIGHTS:
                if name in SETUP_ONLY:
                    c[name] = own.enter_context(nc.sbuf_tensor("c_" + name, shape, F32))
            with nc.Block() as block:
                @block.sync
                def _(sp):
                    for name, shape in WEIGHTS:
                        src = w[name]
                        if name in BROADCAST:
                            src = src.partition_broadcast(P)
                        sp.dma_start(c[name][:, :], src).then_inc(setup_in, 16)
    
                @block.vector
                def _(dve):
                    nc.vector.memset(eps[:], EPS)
                    nc.vector.memset(wvo[:], 0.0).then_inc(setup_dve, 1)
                    nc.vector.memset(vaug[:], 0.0).then_inc(setup_dve, 1)
                    dve.wait_ge(setup_dve, 2)
                    nc.vector.memset(vaug[:, :, LAT:LAT + 1], 1.0)
                    dve.wait_ge(setup_in, 16 * len(WEIGHTS))
                    nc.vector.tensor_copy(sel_bc[:].rearrange("p a b -> p (a b)"), c["sel_bc"][:, :])
                    nc.vector.tensor_copy(ident16[:], c["ident"][:])
                    nc.vector.tensor_copy(mask16[:], c["mask"][:])
                    nc.vector.tensor_copy(mask_t16[:], c["mask_t"][:])
                    nc.vector.tensor_scalar(neg_bz[:], c["bz"][:], -1.0, None, ALU.mult)
                    dve.wait_ge(setup_act, 1)
                    nc.vector.tensor_scalar(neg_a[:], neg_a[:], -1.0, None, ALU.mult)
                    dve.wait_ge(setup_mm, 1)
                    nc.vector.tensor_copy(
                        c["wq"][:].rearrange("p (h f) -> p h f", h=H)[:, :, ROPE:ROPE + LAT],
                        bk(0)[:, 0:H * LAT].rearrange("p (h f) -> p h f", h=H))
                    for s in range(4):
                        last = nc.vector.tensor_copy(wvo[32 * s:32 * s + LAT, :, :],
                                                     bk(2)[32 * s:32 * s + LAT, :].rearrange("p (g f) -> p g f", g=4))
                    last.then_inc(setup_done, 1)
                    dve.wait_ge(setup_done, 1)
    
                @block.scalar
                def _(act):
                    act.wait_ge(setup_in, 16 * len(WEIGHTS))
                    nc.scalar.activation(neg_a[:], c["a_log"][:], ACT.Exp).then_inc(setup_act, 1)
    
                @block.tensor
                def _(pe):
                    pe.wait_ge(setup_in, 16 * len(WEIGHTS))
                    for h in range(H):
                        nc.tensor.matmul(bk(0)[:, h * LAT:(h + 1) * LAT], c["wq_nope_t"][:, h * P:(h + 1) * P],
                                         c["wkvb_t"][:, h * LAT:(h + 1) * LAT], start=True, stop=True)
                    for h in range(H):
                        s, g = h % 4, h // 4
                        last = nc.tensor.matmul(bk(2)[32 * s:32 * s + LAT, g * P:(g + 1) * P],
                                                c["wkvb_t"][:, h * LAT:(h + 1) * LAT],
                                                c["wo_nope"][:, h * P:(h + 1) * P], start=True, stop=True)
                    last.then_inc(setup_mm, 1)
    
            nc.all_engine_barrier()

        layer0(nc, ctx, sb, sems, bk, c, x, locals())
        only0.close()
        nc.all_engine_barrier()
        layer1(nc, ctx, sb, sems, bk, bank, c, out, locals())


def chain_of(eng, sem):
    count = [0]

    def link(ins):
        count[0] += 1
        ins.then_inc(sem, 1)
        eng.wait_ge(sem, count[0])
    return link


def flat(t):
    return t.rearrange("p a b -> p (a b)")


def layer0(nc, ctx, sb, sems, bk, c, x, t):
    xt, stats, mv, std, rstd, xn, xn_t = (t[k] for k in "xt stats mv std rstd xn xn_t".split())
    prob, small, gates, gates_t = (t[k] for k in "prob small gates gates_t".split())
    srow, macc, grow, x1, eps = (t[k] for k in "srow macc grow x1 eps".split())
    with ExitStack() as own:
        def sb(name, shape, dt=F32):
            return own.enter_context(nc.sbuf_tensor(name, shape, dt))
        relu_dt = sb("relu_dt", [P, L])
        log_dt = sb("log_dt", [P, L])
        dt = sb("dt", [P, L])
        bc32 = sb("bc32", [96, L])
        bc_r1 = sb("bc_r1", [96, L])
        bc_r2 = sb("bc_r2", [96, L])
        bc_mid = sb("bc_mid", [96, L], BF16)
        bc16 = sb("bc16", [96, L], BF16)
        z = sb("z", [P, L])
        u = sb("u", [P, L])
        a_bar = sb("a_bar", [P, NS, L])
        ub = sb("ub", [P, L])
        state = sb("state", [P, L])
        hc = sb("hc", [P, 2, L])
        y = sb("y", [P, L])
        yz = sb("yz", [P, L])
        gel = sb("gel", [P, 2, L])
        hid = sb("hid", [P, 2, FT, L])

        names = ("x_in var_ready std_ready xn_ready xnt_psum xnt_ready proj_ready logits_ready dt_parts dt_ready "
                 "bc_ready_act bc16_ready xs_used ez_ready shifted exp_ready gates_ready gates_psum gates_t_ready b2_psum macc_init "
                 "a_ready bc_psum hc_ready y_added yz_ready s_psum gate_psum up_psum gel_ready hid_ready down_psum acc_done "
                 "silu_ready act_chain dve_chain x1_ready")
        s = dict(zip(names.split(), sems(names)))
        nums = [v.num for v in s.values()]

        with nc.Fori(0, B) as b:
            with nc.Block() as block:
                @block.sync
                def _(sp):
                    sp.dma_start(xt[:], x[bass.ds(b, 1)].rearrange("o (j p) d -> (o p) j d", p=P)).then_inc(s["x_in"], 16)

                @block.tensor
                def _(pe):
                    mm = nc.tensor.matmul
                    pe.wait_ge(s["xn_ready"], 1)
                    for j in range(J):
                        last = nc.tensor.transpose(bk(0)[:, j * P:(j + 1) * P], xn[:, j, :], c["ident"][:])
                    last.then_inc(s["xnt_psum"], 1)
                    pe.wait_ge(s["xnt_ready"], 1)
                    for w_, o, rows in ((c["wdt"], 4, P), (c["wbc"], 5, 96), (c["wx"], 3, P), (c["wz"], 2, P)):
                        mm(bk(o)[0:rows, :], w_[:], xn_t[:], start=True, stop=True).then_inc(s["proj_ready"], 1)
                    for j in range(J):
                        last = mm(bk(1)[:, j * E:(j + 1) * E], xn_t[:, j * P:(j + 1) * P], c["router0"][:],
                                  start=True, stop=True)
                    last.then_inc(s["logits_ready"], 1)

                    def up(k):
                        e, f = divmod(k, FT)
                        pair = 2 + 2 * (k % 2)
                        if k == 0:
                            pe.wait_ge(s["ez_ready"], 1)
                            pe.wait_ge(s["xs_used"], 1)
                        elif k == 1:
                            pe.wait_ge(s["dt_parts"], 1)
                            pe.wait_ge(s["bc_ready_act"], 1)
                        else:
                            pe.wait_ge(s["hid_ready"], k - 1)
                        cols = slice((e * FT + f) * P, (e * FT + f + 1) * P)
                        mm(bk(pair), c["wg"][:, cols], xn_t[:], start=True, stop=True).then_inc(s["gate_psum"], 1)
                        mm(bk(pair + 1), c["w1"][:, cols], xn_t[:], start=True, stop=True).then_inc(s["up_psum"], 1)

                    def spread(n):
                        if n == 0:
                            pe.wait_ge(s["bc16_ready"], 1)
                            pe.wait_ge(s["shifted"], 1)
                        else:
                            pe.wait_ge(s["hc_ready"], n)
                        mm(bk(0), t["sel_bc"][:, n, :], bc16[:], start=True, stop=True)
                        mm(bk(1), t["sel_bc"][:, NS + n, :], bc16[:], start=True, stop=True).then_inc(s["bc_psum"], 1)

                    def down(e):
                        pe.wait_ge(s["hid_ready"], FT * (e + 1))
                        if e == 0:
                            pe.wait_ge(s["gates_t_ready"], 1)
                        elif e == 1:
                            pe.wait_ge(s["macc_init"], 1)
                        else:
                            pe.wait_ge(s["acc_done"], e - 1)
                        for j in range(J):
                            for f in range(FT):
                                last = mm(bk(7 - e % 2)[:, j * P:(j + 1) * P], hid[:, e % 2, f, j * P:(j + 1) * P],
                                          c["w2"][:, (e * FT + f) * P:(e * FT + f + 1) * P],
                                          start=(f == 0), stop=(f == FT - 1))
                        last.then_inc(s["down_psum"], 1)

                    for e in range(E):
                        up(FT * e)
                        up(FT * e + 1)
                        if e == 1:
                            pe.wait_ge(s["gates_t_ready"], 1)
                            for j in range(J):
                                last = mm(bk(6)[:, j * P:(j + 1) * P], gates_t[:, j * P:(j + 1) * P], c["b2"][:],
                                          start=True, stop=True)
                            last.then_inc(s["b2_psum"], 1)
                        spread(2 * e)
                        up(FT * e + 2)
                        up(FT * e + 3)
                        spread(2 * e + 1)
                        if e == 0:
                            pe.wait_ge(s["gates_ready"], 1)
                            for j in range(J):
                                last = nc.tensor.transpose(bk(7)[0:E, j * P:(j + 1) * P], gates[:, j, :], c["ident"][:])
                            last.then_inc(s["gates_psum"], 1)
                        else:
                            down(e - 1)
                    down(E - 1)
                    pe.wait_ge(s["yz_ready"], 1)
                    for j in range(J):
                        last = mm(bk(0)[:, j * P:(j + 1) * P], yz[:, j * P:(j + 1) * P], c["wout"][:], start=True, stop=True)
                    last.then_inc(s["s_psum"], 1)

                @block.scalar
                def _(act):
                    link = chain_of(act, s["act_chain"])
                    af = nc.scalar.activation
                    act.wait_ge(s["var_ready"], 1)
                    af(std[:], mv[:, :, 1], ACT.Sqrt, bias=eps[:]).then_inc(s["std_ready"], 1)
                    act.wait_ge(s["xnt_psum"], 1)
                    af(xn_t[:], bk(0), ACT.Copy).then_inc(s["xnt_ready"], 1)
                    act.wait_ge(s["proj_ready"], 1)
                    link(af(log_dt[:], bk(4), ACT.Abs, bias=c["bdt"][:]))
                    af(relu_dt[:], bk(4), ACT.Relu, bias=c["bdt"][:])
                    link(af(log_dt[:], log_dt[:], ACT.Exp, scale=-1.0))
                    af(log_dt[:], log_dt[:], ACT.Ln, bias=1.0).then_inc(s["dt_parts"], 1)
                    act.wait_ge(s["proj_ready"], 2)
                    link(af(bc32[:], bk(5)[0:96, :], ACT.Identity, bias=c["bbc"][:]))
                    af(bc16[:], bc32[:], ACT.Copy).then_inc(s["bc_ready_act"], 1)
                    act.wait_ge(s["proj_ready"], 4)
                    af(z[:], bk(2), ACT.Exp, bias=t["neg_bz"][:], scale=-1.0).then_inc(s["ez_ready"], 1)
                    act.wait_ge(s["shifted"], 1)
                    af(prob[:], prob[:], ACT.Exp).then_inc(s["exp_ready"], 1)
                    act.wait_ge(s["dt_ready"], 1)
                    for n in range(NS):
                        af(a_bar[:, n, :], dt[:], ACT.Exp, scale=t["neg_a"][:, n:n + 1]).then_inc(s["a_ready"], 1)
                    for k in range(E * FT):
                        act.wait_ge(s["gate_psum"], k + 1)
                        if k >= 2:
                            act.wait_ge(s["hid_ready"], k - 1)
                        af(gel[:, k % 2, :], bk(2 + 2 * (k % 2)), ACT.Gelu, bias=c["bg"][:, k:k + 1]).then_inc(s["gel_ready"], 1)
                        if k == FT - 1:
                            act.wait_ge(s["gates_psum"], 1)
                            af(gates_t[:], bk(7)[0:E, :], ACT.Copy).then_inc(s["gates_t_ready"], 1)
                    act.wait_ge(s["acc_done"], E)
                    af(grow[:], macc[:], ACT.Silu).then_inc(s["silu_ready"], 1)

                @block.gpsimd
                def _(pool):
                    for n in range(NS):
                        pool.wait_ge(s["hc_ready"], n + 1)
                        if n == 0:
                            nc.gpsimd.tensor_copy(y[:], hc[:, 0, :]).then_inc(s["y_added"], 1)
                        else:
                            pool.wait_ge(s["y_added"], n)
                            nc.gpsimd.tensor_tensor(y[:], y[:], hc[:, n % 2, :], ALU.add).then_inc(s["y_added"], 1)

                @block.vector
                def _(dve):
                    link = chain_of(dve, s["dve_chain"])
                    v = nc.vector
                    dve.wait_ge(s["x_in"], 16)
                    for j in range(J):
                        last = v.bn_stats(stats[:, j, :], xt[:, j, :])
                    link(last)
                    for j in range(J):
                        last = v.bn_aggr(mv[:, j, :], stats[:, j, :])
                    last.then_inc(s["var_ready"], 1)
                    dve.wait_ge(s["std_ready"], 1)
                    link(v.reciprocal(rstd[:], std[:]))
                    for j in range(J):
                        last = v.tensor_scalar(xn[:, j, :], xt[:, j, :], mv[:, j, 0:1], rstd[:, j:j + 1], ALU.subtract, ALU.mult)
                    last.then_inc(s["xn_ready"], 1)
                    dve.wait_ge(s["dt_parts"], 1)
                    v.tensor_tensor(dt[:], relu_dt[:], log_dt[:], ALU.add).then_inc(s["dt_ready"], 1)
                    dve.wait_ge(s["bc_ready_act"], 1)
                    link(v.tensor_tensor(bc_r1[:], bc32[:], bc16[:], ALU.subtract))
                    v.tensor_copy(bc16[32:64, :], bc_r1[32:64, :])
                    link(v.tensor_copy(bc_mid[:], bc_r1[:]))
                    link(v.tensor_tensor(bc_r2[:], bc_r1[:], bc_mid[:], ALU.subtract))
                    v.tensor_copy(bc16[64:96, :], bc_r2[64:96, :]).then_inc(s["bc16_ready"], 1)
                    dve.wait_ge(s["proj_ready"], 3)
                    dve.wait_ge(s["dt_ready"], 1)
                    v.scalar_tensor_tensor(u[:], bk(3), c["bx"][:], dt[:], ALU.add, ALU.mult).then_inc(s["xs_used"], 1)
                    dve.wait_ge(s["ez_ready"], 1)
                    link(v.tensor_scalar(z[:], z[:], 1.0, None, ALU.add))
                    v.reciprocal(z[:], z[:])
                    dve.wait_ge(s["logits_ready"], 1)
                    link(v.tensor_copy(prob[:], bk(1)[:, 0:J * E].rearrange("p (j e) -> p j e", j=J)))
                    top_two(v, dve, link, t, s, normalise=False)

                    def scan(n):
                        dve.wait_ge(s["bc_psum"], n + 1)
                        link(v.tensor_tensor(ub[:], u[:], bk(0), ALU.mult))
                        dve.wait_ge(s["a_ready"], n + 1)
                        link(v.tensor_tensor_scan(state[:], a_bar[:, n, :], ub[:], 0.0, ALU.mult, ALU.add))
                        if n >= 2:
                            dve.wait_ge(s["y_added"], n - 1)
                        v.tensor_tensor(hc[:, n % 2, :], state[:], bk(1), ALU.mult).then_inc(s["hc_ready"], 1)

                    def hidden(k):
                        e, f = divmod(k, FT)
                        dve.wait_ge(s["up_psum"], k + 1)
                        dve.wait_ge(s["gel_ready"], k + 1)
                        if f == 0 and e >= 2:
                            dve.wait_ge(s["down_psum"], e - 1)
                        v.scalar_tensor_tensor(hid[:, e % 2, f, :], bk(3 + 2 * (k % 2)), c["b1"][:, k:k + 1],
                                               gel[:, k % 2, :], ALU.add, ALU.mult).then_inc(s["hid_ready"], 1)

                    def accumulate(e):
                        dve.wait_ge(s["down_psum"], e + 1)
                        dve.wait_ge(s["acc_done"] if e else s["macc_init"], e if e else 1)
                        for j in range(J):
                            last = v.scalar_tensor_tensor(macc[:, j, :], bk(7 - e % 2)[:, j * P:(j + 1) * P],
                                                          gates[:, j, e:e + 1], macc[:, j, :], ALU.mult, ALU.add)
                        last.then_inc(s["acc_done"], 1)

                    for e in range(E):
                        hidden(FT * e)
                        hidden(FT * e + 1)
                        if e == 1:
                            dve.wait_ge(s["b2_psum"], 1)
                            v.tensor_copy(flat(macc[:]), bk(6)).then_inc(s["macc_init"], 1)
                        scan(2 * e)
                        hidden(FT * e + 2)
                        hidden(FT * e + 3)
                        scan(2 * e + 1)
                        if e >= 1:
                            accumulate(e - 1)
                    accumulate(E - 1)
                    dve.wait_ge(s["y_added"], NS)
                    v.tensor_tensor(yz[:], y[:], z[:], ALU.mult).then_inc(s["yz_ready"], 1)
                    dve.wait_ge(s["s_psum"], 1)
                    for j in range(J):
                        last = v.tensor_tensor(srow[:, j, :], bk(0)[:, j * P:(j + 1) * P], c["bout"][:], ALU.add)
                    link(last)
                    dve.wait_ge(s["silu_ready"], 1)
                    link(v.tensor_tensor(srow[:], srow[:], grow[:], ALU.mult))
                    v.tensor_tensor(x1[:, bass.ds(b, 1)].rearrange("p o j d -> p (o j) d"), srow[:], xt[:],
                                    ALU.add).then_inc(s["x1_ready"], 1)
                    dve.wait_ge(s["x1_ready"], 1)
            nc.all_engine_barrier(sems_to_clear=range(min(nums), max(nums) + 1))


def top_two(v, dve, link, t, s, normalise):
    prob, small, gates, rank, cmp_a, cmp_b, c = (t[k] for k in "prob small gates rank cmp_a cmp_b c".split())

    def over(col):
        return small[:, :, col:col + 1].to_broadcast([P, J, E])
    link(v.tensor_reduce(small[:, :, 0:1], prob[:], AX, ALU.max))
    v.tensor_tensor(prob[:], prob[:], over(0), ALU.subtract).then_inc(s["shifted"], 1)
    dve.wait_ge(s["exp_ready"], 1)
    link(v.tensor_reduce(small[:, :, 1:2], prob[:], AX, ALU.add))
    link(v.reciprocal(small[:, :, 2:3], small[:, :, 1:2]))
    link(v.tensor_tensor(prob[:], prob[:], over(2), ALU.mult))
    other = prob[:].unsqueeze(2).to_broadcast([P, J, E, E])
    mine = prob[:].unsqueeze(3).to_broadcast([P, J, E, E])
    v.tensor_tensor(cmp_a[:], other, mine, ALU.is_gt)
    link(v.tensor_tensor(cmp_b[:], other, mine, ALU.is_equal))
    lower = c["lower"][:].rearrange("p (a b) -> p a b", a=E).unsqueeze(1).to_broadcast([P, J, E, E])
    link(v.tensor_tensor(cmp_b[:], cmp_b[:], lower, ALU.mult))
    link(v.tensor_tensor(cmp_a[:], cmp_a[:], cmp_b[:], ALU.add))
    link(v.tensor_reduce(rank[:].unsqueeze(3), cmp_a[:], AX, ALU.add))
    if not normalise:
        v.scalar_tensor_tensor(gates[:], rank[:], 1.5, prob[:], ALU.is_lt, ALU.mult).then_inc(s["gates_ready"], 1)
        return
    link(v.scalar_tensor_tensor(gates[:], rank[:], 1.5, prob[:], ALU.is_lt, ALU.mult))
    link(v.tensor_reduce(small[:, :, 3:4], gates[:], AX, ALU.add))
    link(v.reciprocal(small[:, :, 2:3], small[:, :, 3:4]))
    v.tensor_tensor(gates[:], gates[:], over(2), ALU.mult).then_inc(s["gates_ready"], 1)


def layer1(nc, ctx, sb, sems, bk, bank, c, out, t):
    xt, stats, mv, std, rstd, xn, xn_t = (t[k] for k in "xt stats mv std rstd xn xn_t".split())
    prob, gates, gates_t, srow, macc, grow, x1, eps = (
        t[k] for k in "prob gates gates_t srow macc grow x1 eps".split())
    vaug, wvo = t["vaug"], t["wvo"]
    with ExitStack() as own:
        def sb(name, shape, dt=F32):
            return own.enter_context(nc.sbuf_tensor(name, shape, dt))
        squares = sb("squares", [P, P])
        ssq = sb("ssq", [P, J])
        xr = sb("xr", [P, J, P])
        xr_t = sb("xr_t", [P, L])
        q1 = sb("q1", [P, L])
        k1 = sb("k1", [P, L])
        v1 = sb("v1", [P, J, P])
        neg_max1 = sb("neg_max1", [P, J])
        den1 = sb("den1", [P, J])
        rden1 = sb("rden1", [P, J])
        p1 = sb("p1", [P, J, L])
        p1_t = sb("p1_t", [P, J, L])
        kc = sb("kc", [P, L])
        ks = sb("ks", [P, L])
        kk = sb("kk", [P, L])
        kk16 = sb("kk16", [P, L], BF16)
        qc = sb("qc", [P, 2, L])
        qs = sb("qs", [P, 2, L])
        q = sb("q", [P, HP, L])
        q16 = sb("q16", [P, HP, L], BF16)
        neg_max = sb("neg_max", [P, J, 2, HP])
        neg_max_t = sb("neg_max_t", [H, L])
        probs = sb("probs", [P, 4, 2, L])
        o = sb("o", [P, 2, L])
        rec = sb("rec", [P, L])
        yn = sb("yn", [P, 4, L])
        x2 = sb("x2", [P, J, P])
        silu_g = sb("silu_g", [P, 2, L])
        hm1 = sb("hm1", [P, L])
        hm = sb("hm", [P, MT + 1, L])

        names = ("x1_copied var_ready std_ready xn_ready xnt_psum xnt_ready squares_ready std2_ready xr_ready xrt_psum xrt_ready "
                 "qkv_psum qk_ready v_ready kproj_psum lat_psum vaug_ready rope_used k_ready s1_psum max1_ready p1_ready pt_psum pt_ready "
                 "av1_psum s1_ready q_psum q_parts q_ready q16_ready max_psum max_used nmt_psum nmt_ready rows_in "
                 "st_psum p_ready av_done o_psum o_ready den_psum yn_ready att_psum x2_ready squares2_ready std3_ready xm_ready "
                 "xmt_psum xmt_ready logits_ready shifted exp_ready gates_ready gates_psum gates_t_ready "
                 "g1_psum u1_psum comb_psum silu1_ready hm_ready moe_psum moe_ready silu_ready out_ready stored act_chain dve_chain")
        s = dict(zip(names.split(), sems(" ".join("l1_" + n for n in names.split()))))
        nums = [v.num for v in s.values()]
        groups = []
        for i in reversed(range(J)):
            width = L // ((i + 1) * P)
            width = {1: 1, 2: 2, 4: 4}[width]
            groups += [(i, range(p0, p0 + width)) for p0 in range(0, HP, width)]
        NG = len(groups)
        ring = [1, 2, 3, 0]

        with nc.Fori(0, B) as b:
            with nc.Block() as block:
                @block.sync
                def _(sp):
                    sp.wait_ge(s["nmt_ready"], 1)
                    sp.wait_ge(s["q_ready"], HP)
                    for parity in range(2):
                        sp.dma_start(q[64 * parity + KD - 1:64 * parity + KD, :, :],
                                     neg_max_t[HP * parity:HP * parity + HP, :]).then_inc(s["rows_in"], 16)
                    sp.wait_ge(s["out_ready"], 1)
                    sp.dma_start(out[bass.ds(b, 1)].rearrange("o (j p) d -> (o p) j d", p=P), macc[:]).then_inc(s["stored"], 16)
                    sp.wait_ge(s["stored"], 16)

                @block.tensor
                def _(pe):
                    mm = nc.tensor.matmul
                    tr = nc.tensor.transpose
                    ident = c["ident"]

                    def rows_to_t(o_, rows, sem):
                        for j in range(J):
                            last = tr(bk(o_)[:, j * P:(j + 1) * P], rows[:, j, :], ident[:])
                        last.then_inc(s[sem], 1)
                    pe.wait_ge(s["xn_ready"], 1)
                    rows_to_t(0, xn, "xnt_psum")
                    pe.wait_ge(s["xr_ready"], 1)
                    rows_to_t(1, xr, "xrt_psum")
                    pe.wait_ge(s["xnt_ready"], 1)
                    mm(bk(2), c["wq1"][:], xn_t[:], start=True, stop=True)
                    mm(bk(3), c["wk1"][:], xn_t[:], start=True, stop=True).then_inc(s["qkv_psum"], 1)
                    for j in range(J):
                        last = mm(bk(4)[:, j * P:(j + 1) * P], xn_t[:, j * P:(j + 1) * P], c["wv1"][:], start=True, stop=True)
                    last.then_inc(s["qkv_psum"], 1)
                    pe.wait_ge(s["xrt_ready"], 1)
                    mm(bk(5), c["wk"][:], xr_t[:], start=True, stop=True)
                    mm(bk(6), c["wk_swap"][:], xr_t[:], start=True, stop=True).then_inc(s["kproj_psum"], 1)
                    for j in range(J):
                        last = mm(bk(7)[:, j * LAT:(j + 1) * LAT], xr_t[:, j * P:(j + 1) * P], c["wlat"][:], start=True, stop=True)
                    last.then_inc(s["lat_psum"], 1)
                    pe.wait_ge(s["qk_ready"], 2)
                    for i in range(J):
                        mm(bk(i)[:, 0:(i + 1) * P], q1[:, i * P:(i + 1) * P], k1[:, 0:(i + 1) * P], start=True, stop=False)
                        mm(bk(i)[:, i * P:(i + 1) * P], t["ident16"][:], t["mask16"][:], start=False, stop=True).then_inc(s["s1_psum"], 1)

                    def query(p):
                        a_, b_ = (5, 6) if p % 2 == 0 else (4, 7)
                        if p == 1:
                            pe.wait_ge(s["v_ready"], 1)
                            pe.wait_ge(s["vaug_ready"], 1)
                        else:
                            pe.wait_ge(s["rope_used"], 1 if p == 0 else p)
                        mm(bk(a_), c["wq"][:, p * P:(p + 1) * P], xr_t[:], start=True, stop=True)
                        mm(bk(b_), c["wq_swap"][:, p * P:(p + 1) * P], xr_t[:], start=True, stop=True).then_inc(s["q_psum"], 1)
                    query(0)
                    query(1)
                    query(2)
                    pe.wait_ge(s["p1_ready"], J)
                    for k in range(J):
                        for i in range(k, J):
                            last = tr(bk(k)[:, i * P:(i + 1) * P], p1[:, i, k * P:(k + 1) * P], ident[:])
                        last.then_inc(s["pt_psum"], 1)
                    for p in range(3, HP):
                        query(p)
                    pe.wait_ge(s["pt_ready"], J)
                    for i in range(J):
                        for k in range(i + 1):
                            last = mm(bk(0)[:, i * P:(i + 1) * P], p1_t[:, k, i * P:(i + 1) * P], v1[:, k, :],
                                      start=(k == 0), stop=(k == i))
                    last.then_inc(s["av1_psum"], 1)

                    pe.wait_ge(s["k_ready"], 1)
                    for g, (i, pairs) in enumerate(groups):
                        if g == 1:
                            pe.wait_ge(s["rope_used"], HP + 1)
                        elif g == 3:
                            pe.wait_ge(s["s1_ready"], 1)
                        elif g >= 4:
                            pe.wait_ge(s["max_used"], g - 3)
                        pe.wait_ge(s["q16_ready"], pairs[-1] + 1)
                        n = (i + 1) * P
                        for m, p in enumerate(pairs):
                            for parity in range(2):
                                rows = slice(64 * parity, 64 * parity + KD - 1)
                                dst = bank[ring[g % 4]][:, parity, m * n:(m + 1) * n]
                                mm(dst, q16[rows, p, i * P:(i + 1) * P], kk16[rows, 0:n], start=True, stop=False)
                                last = mm(dst[:, i * P:n], t["ident16"][:], t["mask16"][:], start=False, stop=True)
                        last.then_inc(s["max_psum"], 1)
                    pe.wait_ge(s["max_used"], NG)
                    for i in range(J):
                        last = tr(bk(0)[0:H, i * P:(i + 1) * P], neg_max[:, i, :, :].rearrange("p a b -> p (a b)"), ident[:])
                    last.then_inc(s["nmt_psum"], 1)

                    def scores(n):
                        p, kt = divmod(n, J)
                        if n == 0:
                            pe.wait_ge(s["rows_in"], 32)
                        elif n >= 3:
                            pe.wait_ge(s["p_ready"], n - 2)
                        for parity in range(2):
                            rows = slice(64 * parity, 64 * parity + KD)
                            dst = bank[n % 3][:, parity, 0:L - kt * P]
                            mm(dst, kk[rows, kt * P:(kt + 1) * P], q[rows, p, kt * P:L], start=True, stop=False)
                            last = mm(dst[:, 0:P], t["ident16"][:], t["mask_t16"][:], start=False, stop=True)
                        last.then_inc(s["st_psum"], 1)

                    def weigh(n):
                        p, kt = divmod(n, J)
                        g = p // 2
                        pe.wait_ge(s["p_ready"], n + 1)
                        if n % 8 == 0 and g >= 2:
                            pe.wait_ge(s["yn_ready"], g - 1)
                        for parity in range(2):
                            slot = 32 * (2 * (p % 2) + parity)
                            last = mm(bk(6 + g % 2)[slot:slot + 32, kt * P:L], vaug[:, kt, :],
                                      probs[:, n % 4, parity, 0:L - kt * P], start=(kt == 0), stop=(kt == J - 1))
                        last.then_inc(s["av_done"], 1)

                    def denominators(g):
                        pe.wait_ge(s["o_ready"], g + 1)
                        mm(bk(6 + g % 2), c["sel_den"][:], o[:, g % 2, :], start=True, stop=True).then_inc(s["den_psum"], 1)

                    steps = HP * J
                    for n in range(steps + 2):
                        if n < steps:
                            scores(n)
                        if n >= 2:
                            weigh(n - 2)
                        if n >= 12 and (n - 12) % 8 == 0:
                            denominators((n - 12) // 8)
                    denominators(3)
                    for g in range(4):
                        pe.wait_ge(s["yn_ready"], g + 1)
                    for j in range(J):
                        for g in range(4):
                            last = mm(bk(0)[:, j * P:(j + 1) * P], yn[:, g, j * P:(j + 1) * P], wvo[:, g, :],
                                      start=(g == 0), stop=(g == 3))
                    last.then_inc(s["att_psum"], 1)

                    pe.wait_ge(s["xm_ready"], 1)
                    rows_to_t(1, xr, "xmt_psum")
                    pe.wait_ge(s["xmt_ready"], 1)
                    for j in range(J):
                        last = mm(bk(2)[:, j * E:(j + 1) * E], xr_t[:, j * P:(j + 1) * P], c["router1"][:], start=True, stop=True)
                    last.then_inc(s["logits_ready"], 1)
                    sets = ((3, 4, 5), (6, 7, 2))

                    def up(n):
                        if n >= 2:
                            pe.wait_ge(s["hm_ready"], n - 1)
                        g_, u_, _ = sets[n % 2]
                        cols = slice(n * P, (n + 1) * P)
                        mm(bk(g_), c["wg1"][:, cols], xr_t[:], start=True, stop=True).then_inc(s["g1_psum"], 1)
                        mm(bk(u_), c["wu1"][:, cols], xr_t[:], start=True, stop=True).then_inc(s["u1_psum"], 1)

                    def spread_gates(n):
                        mm(bk(sets[n % 2][2]), c["sel_comb"][:, n * P:(n + 1) * P], gates_t[:], start=True,
                           stop=True).then_inc(s["comb_psum"], 1)
                    up(0)
                    up(1)
                    pe.wait_ge(s["gates_ready"], 1)
                    for j in range(J):
                        last = tr(bk(0)[0:E, j * P:(j + 1) * P], gates[:, j, :], ident[:])
                    last.then_inc(s["gates_psum"], 1)
                    pe.wait_ge(s["gates_t_ready"], 1)
                    spread_gates(0)
                    spread_gates(1)
                    for n in range(2, MT + 1):
                        up(n)
                        if n < MT:
                            spread_gates(n)
                    for n in range(MT + 1):
                        pe.wait_ge(s["hm_ready"], n + 1)
                    for j in range(J):
                        for n in range(MT + 1):
                            last = mm(bk(1)[:, j * P:(j + 1) * P], hm[:, n, j * P:(j + 1) * P], c["wd1"][:, n * P:(n + 1) * P],
                                      start=(n == 0), stop=(n == MT))
                    last.then_inc(s["moe_psum"], 1)

                @block.scalar
                def _(act):
                    link = chain_of(act, s["act_chain"])
                    af = nc.scalar.activation
                    act.wait_ge(s["var_ready"], 1)
                    af(std[:], mv[:, :, 1], ACT.Sqrt, bias=eps[:]).then_inc(s["std_ready"], 1)

                    def root_mean_square(rows, sem):
                        for j in range(J):
                            link(af(squares[:], rows[:, j, :], ACT.Square, accum_out=ssq[:, j:j + 1]))
                        af(std[:], ssq[:], ACT.Sqrt, bias=eps[:], scale=1.0 / P).then_inc(s[sem], 1)
                    act.wait_ge(s["xn_ready"], 1)
                    root_mean_square(xn, "std2_ready")
                    act.wait_ge(s["xnt_psum"], 1)
                    af(xn_t[:], bk(0), ACT.Copy).then_inc(s["xnt_ready"], 1)
                    act.wait_ge(s["xrt_psum"], 1)
                    af(xr_t[:], bk(1), ACT.Copy, scale=c["ln1"][:]).then_inc(s["xrt_ready"], 1)
                    act.wait_ge(s["qkv_psum"], 1)
                    af(q1[:], bk(2), ACT.Copy).then_inc(s["qk_ready"], 1)
                    af(k1[:], bk(3), ACT.Copy).then_inc(s["qk_ready"], 1)
                    act.wait_ge(s["max1_ready"], 1)
                    for i in range(J):
                        af(p1[:, i, 0:(i + 1) * P], bk(i)[:, 0:(i + 1) * P], ACT.Exp, bias=neg_max1[:, i:i + 1],
                           scale=float(P) ** -0.5, accum_out=den1[:, i:i + 1]).then_inc(s["p1_ready"], 1)
                    for k in range(J):
                        act.wait_ge(s["pt_psum"], k + 1)
                        af(p1_t[:, k, k * P:L], bk(k)[:, k * P:L], ACT.Copy).then_inc(s["pt_ready"], 1)
                    act.wait_ge(s["nmt_psum"], 1)
                    af(neg_max_t[:], bk(0)[0:H, :], ACT.Copy).then_inc(s["nmt_ready"], 1)

                    def take_quad(g):
                        act.wait_ge(s["av_done"], 8 * (g + 1))
                        if g >= 2:
                            act.wait_ge(s["yn_ready"], g - 1)
                        af(o[:, g % 2, :], bk(6 + g % 2), ACT.Copy).then_inc(s["o_ready"], 1)
                    for n in range(HP * J):
                        kt = n % J
                        act.wait_ge(s["st_psum"], n + 1)
                        if n >= 4:
                            act.wait_ge(s["av_done"], n - 3)
                        af(probs[:, n % 4, :, 0:L - kt * P], bank[n % 3][:, :, 0:L - kt * P], ACT.Exp,
                           scale=0.125).then_inc(s["p_ready"], 1)
                        if n >= 10 and (n - 10) % 8 == 0:
                            take_quad((n - 10) // 8)
                    take_quad(3)
                    act.wait_ge(s["x2_ready"], 1)
                    root_mean_square(x2, "std3_ready")
                    act.wait_ge(s["xmt_psum"], 1)
                    af(xr_t[:], bk(1), ACT.Copy, scale=c["ln2"][:]).then_inc(s["xmt_ready"], 1)
                    act.wait_ge(s["shifted"], 1)
                    af(prob[:], prob[:], ACT.Exp).then_inc(s["exp_ready"], 1)
                    for n in range(MT + 1):
                        act.wait_ge(s["g1_psum"], n + 1)
                        if n >= 2:
                            act.wait_ge(s["hm_ready"], n - 1)
                        af(silu_g[:, n % 2, :], bk((3, 6)[n % 2]), ACT.Silu).then_inc(s["silu1_ready"], 1)
                        if n == 1:
                            act.wait_ge(s["gates_psum"], 1)
                            af(gates_t[:], bk(0)[0:E, :], ACT.Copy).then_inc(s["gates_t_ready"], 1)
                    act.wait_ge(s["moe_ready"], 1)
                    af(grow[:], x2[:], ACT.Silu).then_inc(s["silu_ready"], 1)

                @block.gpsimd
                def _(pool):
                    for p in range(HP):
                        pool.wait_ge(s["rope_used"], p + 2)
                        nc.gpsimd.tensor_tensor(q[:, p, :], qc[:, p % 2, :], qs[:, p % 2, :], ALU.add).then_inc(s["q_ready"], 1)
                        pool.wait_ge(s["q_ready"], p + 1)
                        nc.gpsimd.tensor_copy(q16[:, p, :], q[:, p, :]).then_inc(s["q16_ready"], 1)

                @block.vector
                def _(dve):
                    link = chain_of(dve, s["dve_chain"])
                    v = nc.vector
                    link(v.tensor_copy(xt[:], x1[:, bass.ds(b, 1)].rearrange("p o j d -> p (o j) d")))
                    for j in range(J):
                        last = v.bn_stats(stats[:, j, :], xt[:, j, :])
                    link(last)
                    for j in range(J):
                        last = v.bn_aggr(mv[:, j, :], stats[:, j, :])
                    last.then_inc(s["var_ready"], 1)
                    dve.wait_ge(s["std_ready"], 1)
                    link(v.reciprocal(rstd[:], std[:]))
                    for j in range(J):
                        last = v.tensor_scalar(xn[:, j, :], xt[:, j, :], mv[:, j, 0:1], rstd[:, j:j + 1], ALU.subtract, ALU.mult)
                    last.then_inc(s["xn_ready"], 1)

                    def scale_rows(rows, sem_in, sem_out):
                        dve.wait_ge(s[sem_in], 1)
                        link(v.reciprocal(rstd[:], std[:]))
                        v.tensor_tensor(xr[:], rows[:], rstd[:].unsqueeze(2).to_broadcast([P, J, P]), ALU.mult).then_inc(s[sem_out], 1)
                    dve.wait_ge(s["xn_ready"], 1)
                    scale_rows(xn, "std2_ready", "xr_ready")
                    dve.wait_ge(s["qkv_psum"], 2)
                    v.tensor_copy(flat(v1[:]), bk(4)).then_inc(s["v_ready"], 1)
                    dve.wait_ge(s["kproj_psum"], 1)
                    v.tensor_tensor(kc[:], bk(5), c["cos"][:], ALU.mult)
                    v.scalar_tensor_tensor(ks[:], bk(6), c["one_row"][:], c["sin"][:], ALU.add, ALU.mult).then_inc(s["rope_used"], 1)
                    dve.wait_ge(s["lat_psum"], 1)
                    v.tensor_copy(vaug[:, :, 0:LAT], bk(7)[:, 0:J * LAT].rearrange("p (j f) -> p j f", j=J)).then_inc(s["vaug_ready"], 1)
                    dve.wait_ge(s["rope_used"], 1)
                    link(v.tensor_tensor(kk[:], kc[:], ks[:], ALU.add))
                    v.tensor_copy(kk16[:], kk[:]).then_inc(s["k_ready"], 1)
                    for i in range(J):
                        dve.wait_ge(s["s1_psum"], i + 1)
                        last = v.tensor_reduce(neg_max1[:, i:i + 1], bk(i)[:, 0:(i + 1) * P], AX, ALU.max, negate=True)
                    link(last)
                    v.tensor_scalar(neg_max1[:], neg_max1[:], float(P) ** -0.5, None, ALU.mult).then_inc(s["max1_ready"], 1)
                    for p in range(HP):
                        a_, b_ = (5, 6) if p % 2 == 0 else (4, 7)
                        dve.wait_ge(s["q_psum"], p + 1)
                        if p >= 2:
                            dve.wait_ge(s["q_ready"], p - 1)
                        v.tensor_tensor(qc[:, p % 2, :], bk(a_), c["cos"][:], ALU.mult)
                        v.tensor_tensor(qs[:, p % 2, :], bk(b_), c["sin"][:], ALU.mult).then_inc(s["rope_used"], 1)
                    dve.wait_ge(s["p1_ready"], J)
                    link(v.reciprocal(rden1[:], den1[:]))
                    dve.wait_ge(s["av1_psum"], 1)
                    v.tensor_tensor(srow[:], bk(0).rearrange("p (j d) -> p j d", j=J),
                                    rden1[:].unsqueeze(2).to_broadcast([P, J, P]), ALU.mult).then_inc(s["s1_ready"], 1)
                    for g, (i, pairs) in enumerate(groups):
                        n = (i + 1) * P
                        dve.wait_ge(s["max_psum"], g + 1)
                        src = bank[ring[g % 4]][:, :, 0:len(pairs) * n].rearrange("p a (m n) -> p a m n", n=n)
                        v.tensor_reduce(neg_max[:, i, :, pairs[0]:pairs[-1] + 1].unsqueeze(3), src, AX, ALU.max,
                                        negate=True).then_inc(s["max_used"], 1)
                    for g in range(4):
                        dve.wait_ge(s["den_psum"], g + 1)
                        if g >= 1:
                            dve.wait_ge(s["yn_ready"], g)
                        link(v.reciprocal(rec[:], bk(6 + g % 2)))
                        v.tensor_tensor(yn[:, g, :], o[:, g % 2, :], rec[:], ALU.mult).then_inc(s["yn_ready"], 1)
                    dve.wait_ge(s["att_psum"], 1)
                    v.tensor_tensor(flat(x2[:]), flat(xn[:]), bk(0), ALU.add).then_inc(s["x2_ready"], 1)
                    dve.wait_ge(s["x2_ready"], 1)
                    scale_rows(x2, "std3_ready", "xm_ready")
                    dve.wait_ge(s["logits_ready"], 1)
                    link(v.tensor_tensor(prob[:], bk(2)[:, 0:J * E].rearrange("p (j e) -> p j e", j=J),
                                         c["bias1"][:].unsqueeze(1).to_broadcast([P, J, E]), ALU.add))
                    top_two(v, dve, link, t, s, normalise=True)
                    for n in range(MT + 1):
                        _, u_, cb = ((3, 4, 5), (6, 7, 2))[n % 2]
                        dve.wait_ge(s["u1_psum"], n + 1)
                        dve.wait_ge(s["silu1_ready"], n + 1)
                        if n >= 1:
                            dve.wait_ge(s["hm_ready"], n)
                        if n < MT:
                            link(v.tensor_tensor(hm1[:], bk(u_), silu_g[:, n % 2, :], ALU.mult))
                            dve.wait_ge(s["comb_psum"], n + 1)
                            v.tensor_tensor(hm[:, n, :], hm1[:], bk(cb), ALU.mult).then_inc(s["hm_ready"], 1)
                        else:
                            v.tensor_tensor(hm[:, n, :], bk(u_), silu_g[:, n % 2, :], ALU.mult).then_inc(s["hm_ready"], 1)
                    dve.wait_ge(s["moe_psum"], 1)
                    v.tensor_tensor(flat(x2[:]), flat(x2[:]), bk(1), ALU.add).then_inc(s["moe_ready"], 1)
                    dve.wait_ge(s["silu_ready"], 1)
                    link(v.tensor_tensor(macc[:], srow[:], grow[:], ALU.mult))
                    v.tensor_tensor(macc[:], macc[:], xt[:], ALU.add).then_inc(s["out_ready"], 1)
            nc.all_engine_barrier(sems_to_clear=range(min(nums), max(nums) + 1))


def shape_tables():
    rows = np.arange(P)
    lane = rows % 64
    freq = (1.0 / np.float32(100000.0) ** (np.arange(0, ROPE, 2, dtype=np.float32) / np.float32(ROPE))).astype(np.float32)
    angle = np.outer(np.arange(L, dtype=np.float32), freq).astype(np.float32)
    cos, sin = np.zeros((P, L), np.float32), np.zeros((P, L), np.float32)
    for r in rows:
        if lane[r] < ROPE:
            cos[r] = np.cos(angle[:, lane[r] // 2])
            sin[r] = np.sin(angle[:, lane[r] // 2]) * (1 if lane[r] % 2 else -1)
        elif lane[r] < ROPE + LAT:
            cos[r] = 1.0
        elif lane[r] == KD - 1:
            sin[r] = 1.0
    one_row = (lane == KD - 1).astype(np.float32)[:, None]
    part = np.arange(96) % 32
    sel_bc = (part[:, None, None] == np.arange(32)[None, :, None]) * np.ones((1, 1, P))
    lower = np.tile((np.arange(E)[None, :] < np.arange(E)[:, None]).reshape(1, E * E), (P, 1))
    sel_den = (rows[:, None] == 32 * (rows[None, :] // 32) + LAT)
    tile_col = np.arange(MT * P)
    sel_comb = np.arange(E)[:, None] == tile_col[None, :] // I1
    tables = {
        "ident": np.eye(P), "sel_bc": sel_bc.reshape(96, 32 * P), "mask": np.where(rows[None, :] > rows[:, None], MASKED, 0.0),
        "mask_t": np.where(rows[:, None] > rows[None, :], MASKED, 0.0), "cos": cos, "sin": sin, "one_row": one_row,
        "lower": lower, "sel_den": sel_den, "sel_comb": sel_comb}
    return {k: np.ascontiguousarray(v.astype(np.float32)) for k, v in tables.items()}


def lay_out(i):
    def column(a):
        return a.reshape(-1, 1)

    def padded(a, width):
        return np.concatenate([a, np.zeros((*a.shape[:-1], width - a.shape[-1]), a.dtype)], axis=-1)
    swap = np.arange(ROPE) ^ 1
    wq = i["L1_ffn_Wq"].reshape(P, H, 64)
    rope = wq[:, :, 32:]
    wkva = i["L1_ffn_Wkva"]
    k_rope, k_lat = wkva[:, LAT:], wkva[:, :LAT]
    wkvb = i["L1_ffn_Wkvb"].reshape(LAT, H, 32)
    wo = i["L1_ffn_Wo"].reshape(H, 64, P)
    bc = np.concatenate([i["L0_attn_WB"], i["L0_attn_WC"]], axis=1)
    bbc = np.concatenate([i["L0_attn_bB"], i["L0_attn_bC"]])

    def experts_in(routed, shared):
        r = routed.transpose(1, 0, 2).reshape(P, E * I1)
        return np.concatenate([r, padded(shared[0], P)], axis=1)
    down = i["L1_ffn_Wd"].reshape(MT, P, P).transpose(1, 0, 2)
    down_shared = np.concatenate([i["L1_ffn_sWd"][0], np.zeros((P - I1, P), np.float32)])[:, None, :]
    return {
        "wz": i["L0_attn_Wz"], "wx": i["L0_attn_Wx"], "wdt": i["L0_attn_Wdt"], "wbc": np.concatenate([bc] * 3, axis=1),
        "a_log": i["L0_attn_A_log"], "wout": i["L0_attn_Wout"], "bz": column(i["L0_attn_bz"]), "bx": column(i["L0_attn_bx"]),
        "bdt": column(i["L0_attn_bdt"]), "bbc": column(np.concatenate([bbc] * 3)), "bout": i["L0_attn_bout"].reshape(1, P),
        "router0": i["L0_ffn_router_w"].T, "w1": i["L0_ffn_w1_w"].transpose(2, 0, 1).reshape(P, E * FF),
        "wg": i["L0_ffn_wg_w"].transpose(2, 0, 1).reshape(P, E * FF),
        "w2": i["L0_ffn_w2_w"].reshape(E, P, FT, P).transpose(3, 0, 2, 1).reshape(P, E * FT * P),
        "b1": i["L0_ffn_w1_b"].reshape(E * FT, P).T, "bg": i["L0_ffn_wg_b"].reshape(E * FT, P).T, "b2": i["L0_ffn_w2_b"],
        "wq1": i["L1_attn_WQ"], "wk1": i["L1_attn_WK"], "wv1": i["L1_attn_WV"],
        "ln1": column(i["L1_ffn_w_ln1"]), "ln2": column(i["L1_ffn_w_ln2"]),
        "wq": padded(rope, 64).reshape(P, HP * P), "wq_swap": padded(rope[:, :, swap], 64).reshape(P, HP * P),
        "wk": np.concatenate([padded(np.concatenate([k_rope, k_lat], axis=1), 64)] * 2, axis=1),
        "wk_swap": np.concatenate([padded(k_rope[:, swap], 64)] * 2, axis=1),
        "wq_nope_t": wq[:, :, :32].transpose(2, 1, 0).reshape(32, H * P),
        "wkvb_t": wkvb.transpose(2, 1, 0).reshape(32, H * LAT),
        "wo_nope": wo[:, :32].transpose(1, 0, 2).reshape(32, H * P), "wlat": k_lat,
        "router1": i["L1_ffn_Wgate"], "bias1": i["L1_ffn_expert_bias"].reshape(1, E),
        "wg1": experts_in(i["L1_ffn_Wg"], i["L1_ffn_sWg"]), "wu1": experts_in(i["L1_ffn_Wu"], i["L1_ffn_sWu"]),
        "wd1": np.concatenate([down, down_shared], axis=1).reshape(P, (MT + 1) * P),
    }


def kernel(**inputs):
    import concourse.bacc as _bacc
    from concourse.bass_utils import run_bass_kernel_spmd as _run

    host = {k: np.asarray(v) for k, v in inputs.items()}
    x = np.ascontiguousarray(host["L0_attn_x"])
    given = {**shape_tables(), **lay_out(host)}
    nc = _bacc.Bacc("TRN2", target_bir_lowering=False, num_devices=1)
    arrays = {"in_x": x}
    x_ap = nc.dram_tensor("in_x", x.shape, F32, kind="ExternalInput").ap()
    w = {}
    for name, _ in WEIGHTS:
        arrays["in_" + name] = np.ascontiguousarray(given[name])
        w[name] = nc.dram_tensor("in_" + name, given[name].shape, F32, kind="ExternalInput").ap()
    out = nc.dram_tensor("out", x.shape, F32, kind="ExternalOutput").ap()
    two_layers(nc, x_ap, w, out)
    r = _run(nc, [arrays], core_ids=[0])
    return r.results[0]["out"]
```

```python
from contextlib import ExitStack

import numpy as np

import concourse.bass as bass
from concourse import mybir

ALU = mybir.AluOpType
ACT = mybir.ActivationFunctionType
AX = mybir.AxisListType.X
F32 = mybir.dt.float32
BF16 = mybir.dt.bfloat16
F32R = mybir.dt.float32r
U32 = mybir.dt.uint32

P = 128
B, L = 8, 512
J = L // P
NS = 16
E, FF = 8, 512
FT = FF // P
H, HP = 16, 8
ROPE, LAT = 32, 16
KD = ROPE + LAT + 1
I1 = 64
MT = E * I1 // P
EPS = 1e-5
MASKED = -1e30
T = B * J
NT = T * 2 + E
PASSES = 4
TP = NT // PASSES
XW = 3 * FF
XB = 2 * FF + P

WEIGHTS = [
    ("ident", [P, P]), ("sel_bc", [96, 32 * P]), ("mask", [P, P]), ("mask_t", [P, P]), ("cos", [P, L]), ("sin", [P, L]),
    ("one_row", [P, 1]), ("lower", [P, E * E]), ("sel_den", [P, 4]), ("sel_comb", [E, MT * P]),
    ("wz", [P, P]), ("wx", [P, P]), ("wdt", [P, P]), ("wbc", [P, 96]), ("a_log", [P, NS]), ("wout", [P, P]),
    ("bz", [P, 1]), ("bx", [P, 1]), ("bdt", [P, 1]), ("bbc", [96, 1]), ("bout", [P, P]),
    ("router0", [P, E]), ("wexp", [P, E * XW]), ("bexp", [P, E * XB // P]),
    ("before", [P, P]), ("ones", [P, P]), ("steps", [P, T]), ("tiles", [P, NT]),
    ("wq1", [P, P]), ("wk1", [P, P]), ("wv1", [P, P]),
    ("ln1", [P, 1]), ("ln2", [P, 1]), ("wq", [P, HP * P]), ("wq_swap", [P, HP * P]), ("wk", [P, P]), ("wk_swap", [P, P]),
    ("wq_nope_t", [32, H * P]), ("wkvb_t", [32, H * LAT]), ("wo_nope", [32, H * P]), ("wlat", [P, LAT]),
    ("router1", [P, E]), ("bias1", [P, E]), ("wg1", [P, (MT + 1) * P]), ("wu1", [P, (MT + 1) * P]), ("wd1", [P, (MT + 1) * P]),
]
SETUP_ONLY = {"sel_bc", "mask", "mask_t", "wq_nope_t", "wkvb_t", "wo_nope", "a_log", "bexp"}
LAYER0_ONLY = {"wexp", "before", "steps", "tiles", "router0"}
BROADCAST = {"bout", "bias1"}


def two_layers(nc, x, w, out, xs, ys):
    with ExitStack() as ctx:
        def sb(name, shape, dt=F32):
            return ctx.enter_context(nc.sbuf_tensor(name, shape, dt))

        def sems(names, scope=ctx):
            return [scope.enter_context(nc.semaphore(n)) for n in names.split()]

        def sems_of_stage(names, scope, taken):
            first = setup_rows.num + 1 + len(taken)
            found = [scope.enter_context(nc.semaphore(n, num=first + i)) for i, n in enumerate(names.split())]
            taken += found
            return found

        c = {name: sb("c_" + name, shape) for name, shape in WEIGHTS
             if name not in SETUP_ONLY | LAYER0_ONLY}
        bank = [ctx.enter_context(nc.psum_tensor(f"bank{i}", [P, 2, L], F32)) for i in range(4)]

        def bk(i):
            return bank[i // 2][:, i % 2, :]

        ident16 = sb("ident16", [P, P], BF16)
        mask16 = sb("mask16", [P, P], BF16)
        mask_t16 = sb("mask_t16", [P, P], BF16)
        neg_a = sb("neg_a", [P, NS])
        half_bz = sb("half_bz", [P, 1])
        minus_half = sb("minus_half", [P, J])
        eps = sb("eps", [P, 1])
        wvo = sb("wvo", [P, 4, P])
        vaug = sb("vaug", [P, J, 32])
        xn_t_all = sb("xn_t_all", [P, (B + 1) * L])
        scan = scan_tiles(nc, ctx)
        sel_bc = sb("sel_bc16", [96, 32, P], BF16)
        gate2 = sb("gate2", [P, 2, T])
        slot2 = sb("slot2", [P, 2, T], U32)

        only0 = ctx.enter_context(ExitStack())
        expert_of = only0.enter_context(nc.sbuf_tensor("expert_of", [P, NT], U32))
        bias16 = only0.enter_context(nc.sbuf_tensor("bias16", [3, E * XB], BF16))
        ones16 = only0.enter_context(nc.sbuf_tensor("ones16", [3, P], BF16))
        for name, shape in WEIGHTS:
            if name in LAYER0_ONLY:
                c[name] = only0.enter_context(nc.sbuf_tensor("c_" + name, shape, F32))
        rows_scattered, rows_gathered = sems("rows_scattered rows_gathered")
        (setup_in, setup_mm, setup_act, setup_dve, setup_done, setup_bias, setup_rows) = sems(
            "setup_in setup_mm setup_act setup_dve setup_done setup_bias setup_rows")

        with ExitStack() as own:
            for name, shape in WEIGHTS:
                if name in SETUP_ONLY:
                    c[name] = own.enter_context(nc.sbuf_tensor("c_" + name, shape, F32))
            bias_part = own.enter_context(nc.sbuf_tensor("bias_part", [P, 3, E * XB // P], BF16))
            bias_rest = own.enter_context(nc.sbuf_tensor("bias_rest", [P, 2, E * XB // P], F32))
            with nc.Block() as block:
                @block.sync
                def _(sp):
                    for name, shape in WEIGHTS:
                        src = w[name]
                        if name in BROADCAST:
                            src = src.partition_broadcast(P)
                        sp.dma_start(c[name][:, :], src).then_inc(setup_in, 16)
                    sp.wait_ge(setup_bias, 5)
                    for part in range(3):
                        sp.dma_start(bias16[part:part + 1, :], bias_part[:, part, :]).then_inc(setup_rows, 16)
                    sp.wait_ge(setup_rows, 48)
    
                @block.vector
                def _(dve):
                    nc.vector.memset(eps[:], EPS)
                    nc.vector.memset(minus_half[:], -0.5)
                    nc.vector.memset(xn_t_all[:, B * L:], 0.0)
                    nc.vector.memset(wvo[:], 0.0).then_inc(setup_dve, 1)
                    nc.vector.memset(vaug[:], 0.0).then_inc(setup_dve, 1)
                    dve.wait_ge(setup_dve, 2)
                    nc.vector.memset(vaug[:, :, LAT:LAT + 1], 1.0)
                    dve.wait_ge(setup_in, 16 * len(WEIGHTS))
                    nc.vector.tensor_copy(sel_bc[:].rearrange("p a b -> p (a b)"), c["sel_bc"][:, :])
                    nc.vector.memset(ones16[:], 1.0)
                    split = chain_of(dve, setup_bias)
                    split(nc.vector.tensor_copy(bias_part[:, 0, :], c["bexp"][:]))
                    split(nc.vector.tensor_tensor(bias_rest[:, 0, :], c["bexp"][:], bias_part[:, 0, :], ALU.subtract))
                    split(nc.vector.tensor_copy(bias_part[:, 1, :], bias_rest[:, 0, :]))
                    split(nc.vector.tensor_tensor(bias_rest[:, 1, :], bias_rest[:, 0, :], bias_part[:, 1, :], ALU.subtract))
                    split(nc.vector.tensor_copy(bias_part[:, 2, :], bias_rest[:, 1, :]))
                    nc.vector.tensor_copy(ident16[:], c["ident"][:])
                    nc.vector.tensor_copy(mask16[:], c["mask"][:])
                    nc.vector.tensor_copy(mask_t16[:], c["mask_t"][:])
                    nc.vector.tensor_scalar(half_bz[:], c["bz"][:], 0.5, None, ALU.mult)
                    dve.wait_ge(setup_act, 1)
                    nc.vector.tensor_scalar(neg_a[:], neg_a[:], -1.0, None, ALU.mult)
                    dve.wait_ge(setup_mm, 1)
                    nc.vector.tensor_copy(
                        c["wq"][:].rearrange("p (h f) -> p h f", h=H)[:, :, ROPE:ROPE + LAT],
                        bk(0)[:, 0:H * LAT].rearrange("p (h f) -> p h f", h=H))
                    for s in range(4):
                        last = nc.vector.tensor_copy(wvo[32 * s:32 * s + LAT, :, :],
                                                     bk(2)[32 * s:32 * s + LAT, :].rearrange("p (g f) -> p g f", g=4))
                    last.then_inc(setup_done, 1)
                    dve.wait_ge(setup_done, 1)
    
                @block.scalar
                def _(act):
                    act.wait_ge(setup_in, 16 * len(WEIGHTS))
                    nc.scalar.activation(neg_a[:], c["a_log"][:], ACT.Exp).then_inc(setup_act, 1)
    
                @block.tensor
                def _(pe):
                    pe.wait_ge(setup_in, 16 * len(WEIGHTS))
                    for h in range(H):
                        nc.tensor.matmul(bk(0)[:, h * LAT:(h + 1) * LAT], c["wq_nope_t"][:, h * P:(h + 1) * P],
                                         c["wkvb_t"][:, h * LAT:(h + 1) * LAT], start=True, stop=True)
                    for h in range(H):
                        s, g = h % 4, h // 4
                        last = nc.tensor.matmul(bk(2)[32 * s:32 * s + LAT, g * P:(g + 1) * P],
                                                c["wkvb_t"][:, h * LAT:(h + 1) * LAT],
                                                c["wo_nope"][:, h * P:(h + 1) * P], start=True, stop=True)
                    last.then_inc(setup_mm, 1)
    
            nc.all_engine_barrier()

        route(nc, sems_of_stage, bk, c, x, xs, locals())
        experts0(nc, sems_of_stage, bk, c, xs, ys, locals())
        only0.close()
        nc.all_engine_barrier()
        layer1(nc, sems_of_stage, bk, bank, c, x, ys, out, locals())


def chain_of(eng, sem):
    count = [0]

    def link(ins):
        count[0] += 1
        ins.then_inc(sem, 1)
        eng.wait_ge(sem, count[0])
    return link


def span(taken):
    return range(taken[0].num, taken[0].num + len(taken))


def flat(t):
    return t.rearrange("p a b -> p (a b)")


SCAN_SEMS = ("sc_copied sc_proj sc_dt_parts sc_bc32 sc_bc16 sc_dt sc_u sc_tanh sc_a sc_spread sc_hc sc_added sc_yz sc_out_psum sc_done "
             "sc_act_chain sc_dve_chain")


def scan_tiles(nc, ctx):
    def sb(name, shape, dt=F32):
        return ctx.enter_context(nc.sbuf_tensor("sc_" + name, shape, dt))
    return dict(
        xn_t=sb("xn_t", [P, L]), relu_dt=sb("relu_dt", [P, L]), log_dt=sb("log_dt", [P, L]), dt=sb("dt", [P, L]),
        bc32=sb("bc32", [96, L]), r1=sb("r1", [96, L]), r2=sb("r2", [96, L]), mid=sb("mid", [96, L], BF16),
        bc16=sb("bc16", [96, L], BF16), z=sb("z", [P, L]), u=sb("u", [P, L]), a_bar=sb("a_bar", [P, 4, L]),
        ub=sb("ub", [P, L]), state=sb("state", [P, L]), hc=sb("hc", [P, 2, L]), y=sb("y", [P, L]), yz=sb("yz", [P, L]),
        rows=sb("rows", [P, J, P]))


class Scan:

    def __init__(self, nc, t, c, bk, s):
        self.nc, self.t, self.c, self.bk, self.s = nc, t, c, bk, s
        self.v = t["scan"]

    def copy_in(self, pool, batch):
        v, s = self.v, self.s
        self.nc.gpsimd.tensor_copy(v["xn_t"][:], self.t["xn_t_all"][:, bass.ds(batch * L, L)]).then_inc(s["sc_copied"], 1)

    def project(self, pe, what):
        mm, v, s, c, bk = self.nc.tensor.matmul, self.v, self.s, self.c, self.bk
        w, o, rows = {"dt": (c["wdt"], 6, P), "bc": (c["wbc"], 7, 96), "x": (c["wx"], 6, P), "z": (c["wz"], 7, P)}[what]
        if what == "dt":
            pe.wait_ge(s["sc_copied"], 1)
        elif what == "x":
            pe.wait_ge(s["sc_dt_parts"], 1)
        elif what == "z":
            pe.wait_ge(s["sc_bc32"], 1)
        mm(bk(o)[0:rows, :], w[:], v["xn_t"][:], start=True, stop=True).then_inc(s["sc_proj"], 1)

    def spread(self, pe, n):
        mm, v, s, bk = self.nc.tensor.matmul, self.v, self.s, self.bk
        if n == 0:
            pe.wait_ge(s["sc_bc16"], 1)
            pe.wait_ge(s["sc_u"], 1)
            pe.wait_ge(s["sc_tanh"], 1)
        else:
            pe.wait_ge(s["sc_hc"], n)
        mm(bk(6), self.t["sel_bc"][:, n, :], v["bc16"][:], start=True, stop=True)
        mm(bk(7), self.t["sel_bc"][:, NS + n, :], v["bc16"][:], start=True, stop=True).then_inc(s["sc_spread"], 1)

    def project_out(self, pe):
        mm, v, s = self.nc.tensor.matmul, self.v, self.s
        pe.wait_ge(s["sc_yz"], 1)
        for j in range(J):
            last = mm(self.bk(6)[:, j * P:(j + 1) * P], v["yz"][:, j * P:(j + 1) * P], self.c["wout"][:], start=True, stop=True)
        last.then_inc(s["sc_out_psum"], 1)

    def act_front(self, act):
        af, v, s, c, bk = self.nc.scalar.activation, self.v, self.s, self.c, self.bk
        link = chain_of(act, s["sc_act_chain"])
        act.wait_ge(s["sc_proj"], 1)
        link(af(v["log_dt"][:], bk(6), ACT.Abs, bias=c["bdt"][:]))
        af(v["relu_dt"][:], bk(6), ACT.Relu, bias=c["bdt"][:])
        link(af(v["log_dt"][:], v["log_dt"][:], ACT.Exp, scale=-1.0))
        af(v["log_dt"][:], v["log_dt"][:], ACT.Ln, bias=1.0).then_inc(s["sc_dt_parts"], 1)
        act.wait_ge(s["sc_proj"], 2)
        link(af(v["bc32"][:], bk(7)[0:96, :], ACT.Identity, bias=c["bbc"][:]))
        af(v["bc16"][:], v["bc32"][:], ACT.Copy).then_inc(s["sc_bc32"], 1)
        act.wait_ge(s["sc_proj"], 4)
        af(v["z"][:], bk(7), ACT.Tanh, bias=self.t["half_bz"][:], scale=0.5).then_inc(s["sc_tanh"], 1)

    def decay(self, act, n):
        s, v = self.s, self.v
        if n == 0:
            act.wait_ge(s["sc_dt"], 1)
        if n >= 4:
            act.wait_ge(s["sc_hc"], n - 3)
        self.nc.scalar.activation(v["a_bar"][:, n % 4, :], v["dt"][:], ACT.Exp,
                                  scale=self.t["neg_a"][:, n:n + 1]).then_inc(s["sc_a"], 1)

    def add(self, pool, n):
        s, v = self.s, self.v
        pool.wait_ge(s["sc_hc"], n + 1)
        if n == 0:
            self.nc.gpsimd.tensor_copy(v["y"][:], v["hc"][:, 0, :]).then_inc(s["sc_added"], 1)
        else:
            pool.wait_ge(s["sc_added"], n)
            self.nc.gpsimd.tensor_tensor(v["y"][:], v["y"][:], v["hc"][:, n % 2, :], ALU.add).then_inc(s["sc_added"], 1)

    def vector_front(self, dve):
        ve, v, s = self.nc.vector, self.v, self.s
        self.link = link = chain_of(dve, s["sc_dve_chain"])
        dve.wait_ge(s["sc_dt_parts"], 1)
        ve.tensor_tensor(v["dt"][:], v["relu_dt"][:], v["log_dt"][:], ALU.add).then_inc(s["sc_dt"], 1)
        dve.wait_ge(s["sc_bc32"], 1)
        link(ve.tensor_tensor(v["r1"][:], v["bc32"][:], v["bc16"][:], ALU.subtract))
        ve.tensor_copy(v["bc16"][32:64, :], v["r1"][32:64, :])
        link(ve.tensor_copy(v["mid"][:], v["r1"][:]))
        link(ve.tensor_tensor(v["r2"][:], v["r1"][:], v["mid"][:], ALU.subtract))
        ve.tensor_copy(v["bc16"][64:96, :], v["r2"][64:96, :]).then_inc(s["sc_bc16"], 1)
        dve.wait_ge(s["sc_proj"], 3)
        dve.wait_ge(s["sc_dt"], 1)
        ve.scalar_tensor_tensor(v["u"][:], self.bk(6), self.c["bx"][:], v["dt"][:], ALU.add, ALU.mult).then_inc(s["sc_u"], 1)

    def step(self, dve, n):
        ve, v, s, link = self.nc.vector, self.v, self.s, self.link
        dve.wait_ge(s["sc_spread"], n + 1)
        if n == 0:
            dve.wait_ge(s["sc_u"], 1)
        link(ve.tensor_tensor(v["ub"][:], v["u"][:], self.bk(6), ALU.mult))
        dve.wait_ge(s["sc_a"], n + 1)
        if n >= 1:
            dve.wait_ge(s["sc_hc"], n)
        link(ve.tensor_tensor_scan(v["state"][:], v["a_bar"][:, n % 4, :], v["ub"][:], 0.0, ALU.mult, ALU.add))
        if n >= 2:
            dve.wait_ge(s["sc_added"], n - 1)
        ve.tensor_tensor(v["hc"][:, n % 2, :], v["state"][:], self.bk(7), ALU.mult).then_inc(s["sc_hc"], 1)

    def gate(self, dve):
        dve.wait_ge(self.s["sc_added"], NS)
        v = self.v
        self.nc.vector.scalar_tensor_tensor(v["yz"][:], v["z"][:], 1.0, v["y"][:], ALU.add, ALU.mult).then_inc(self.s["sc_yz"], 1)

    def finish(self, dve):
        dve.wait_ge(self.s["sc_out_psum"], 1)
        self.nc.vector.scalar_tensor_tensor(self.v["rows"][:], self.bk(6).rearrange("p (j d) -> p j d", j=J), 0.5,
                                            self.c["bout"][:].unsqueeze(1).to_broadcast([P, J, P]),
                                            ALU.mult, ALU.add).then_inc(self.s["sc_done"], 1)
        dve.wait_ge(self.s["sc_done"], 1)


def route(nc, sems_of_stage, bk, c, x, xs, t):
    xn_t_all, eps = t["xn_t_all"], t["eps"]
    taken = []
    with ExitStack() as own:
        def sb(name, shape, dt=F32):
            return own.enter_context(nc.sbuf_tensor(name, shape, dt))
        rows_all = sb("rows_all", [P, T, P])
        stats = sb("r_stats", [P, T, 6])
        mv = sb("r_mv", [P, T, 2])
        std = sb("r_std", [P, T])
        rstd = sb("r_rstd", [P, T])
        zeros = sb("zeros", [P, NT * P // 8])
        prob = sb("r_prob", [P, T, E])
        small = sb("r_small", [P, T, 4])
        rank = sb("r_rank", [P, T, E])
        cmp_a = t["scan"]["a_bar"][:].rearrange("p a b -> p (a b)").rearrange("p (a b c) -> p a b c", a=T, b=E)
        cmp_b = sb("r_cmp_b", [P, T, E, E])
        picked = sb("picked", [P, T, E])
        upto = sb("upto", [P, E, T])
        slot = sb("slot", [P, T, E])
        n_tiles = sb("n_tiles", [P, E])
        first = sb("first", [P, E])
        chosen = sb("chosen", [P, T, E])
        slot_f = sb("slot_f", [P, 2, T])
        expert_f = sb("expert_f", [P, NT])
        scattered = t["rows_scattered"]
        x_landed = sems_of_stage(" ".join(f"x_landed{b}" for b in range(B)), own, taken)
        names = ("zeroed filled var_ready std_ready xn_ready xnt_psum xnt_ready logits_ready shifted exp_ready gates_ready "
                 "picked_ready counts_psum slots_ready chain")
        s = dict(zip(names.split(), sems_of_stage(" ".join("r_" + n for n in names.split()), own, taken)))
        s.update(zip(SCAN_SEMS.split(), sems_of_stage(" ".join("r_" + n for n in SCAN_SEMS.split()), own, taken)))
        scan = Scan(nc, t, c, bk, s)
        x_v = x.rearrange("b (j p) d -> b p j d", p=P)
        with nc.Block() as block:
            @block.sync
            def _(sp):
                for b in range(B):
                    sp.dma_start(rows_all[:, b * J:(b + 1) * J, :], x_v[b]).then_inc(x_landed[b], 16)
                sp.wait_ge(s["zeroed"], 1)
                fill = xs.rearrange("(q p r) d -> q p (r d)", q=8, p=P)
                for q in range(8):
                    sp.dma_start(fill[q], zeros[:]).then_inc(s["filled"], 16)

            @block.tensor
            def _(pe):
                mm = nc.tensor.matmul
                for b in range(B + 1):
                    if b < B:
                        pe.wait_ge(s["xn_ready"], b + 1)
                        if b >= 4:
                            pe.wait_ge(s["xnt_ready"], b - 3)
                        for j in range(J):
                            last = nc.tensor.transpose(bk(b % 4)[:, j * P:(j + 1) * P], rows_all[:, b * J + j, :], c["ident"][:])
                        last.then_inc(s["xnt_psum"], 1)
                    if b >= 1:
                        pe.wait_ge(s["xnt_ready"], b)
                        for i in range(J * (b - 1), J * b):
                            last = mm(bk(4)[:, i * E:(i + 1) * E], xn_t_all[:, i * P:(i + 1) * P], c["router0"][:],
                                      start=True, stop=True)
                last.then_inc(s["logits_ready"], 1)
                pe.wait_ge(s["picked_ready"], 1)
                mm(bk(5)[:, 0:T * E], c["before"][:], picked[:].rearrange("p a b -> p (a b)"), start=True, stop=True)
                mm(bk(0)[:, 0:T * E], c["ones"][:], picked[:].rearrange("p a b -> p (a b)"), start=True,
                   stop=True).then_inc(s["counts_psum"], 1)
                for what in ("dt", "bc", "x", "z"):
                    scan.project(pe, what)
                for n in range(NS):
                    scan.spread(pe, n)
                scan.project_out(pe)

            @block.scalar
            def _(act):
                af = nc.scalar.activation
                for b in range(B + 1):
                    if b < B:
                        act.wait_ge(s["var_ready"], b + 1)
                        af(std[:, b * J:(b + 1) * J], mv[:, b * J:(b + 1) * J, 1], ACT.Sqrt, bias=eps[:]).then_inc(s["std_ready"], 1)
                    if b >= 1:
                        act.wait_ge(s["xnt_psum"], b)
                        af(xn_t_all[:, (b - 1) * L:b * L], bk((b - 1) % 4), ACT.Copy).then_inc(s["xnt_ready"], 1)
                act.wait_ge(s["shifted"], 1)
                af(prob[:], prob[:], ACT.Exp).then_inc(s["exp_ready"], 1)
                scan.act_front(act)
                for n in range(NS):
                    scan.decay(act, n)

            @block.gpsimd
            def _(pool):
                nc.gpsimd.memset(zeros[:], 0.0).then_inc(s["zeroed"], 1)
                pool.wait_ge(s["xnt_ready"], 1)
                scan.copy_in(pool, 0)
                pool.wait_ge(s["filled"], 16 * 8)
                pool.wait_ge(s["slots_ready"], 1)
                for i in range(T):
                    if i % 2 == 0:
                        scan.add(pool, i // 2)
                    for k in range(2):
                        nc.gpsimd.indirect_dma_start(
                            out=xs, out_offset=bass.IndirectOffsetOnAxis(ap=t["slot2"][:, k, i:i + 1], axis=0),
                            in_=rows_all[:, i, :], in_offset=None).then_inc(scattered, 16)
                pool.wait_ge(scattered, 16 * 2 * T)

            @block.vector
            def _(dve):
                link = chain_of(dve, s["chain"])
                v = nc.vector
                for b in range(B + 1):
                    if b < B:
                        dve.wait_ge(x_landed[b], 16)
                        for i in range(b * J, (b + 1) * J):
                            last = v.bn_stats(stats[:, i, :], rows_all[:, i, :])
                        link(last)
                        for i in range(b * J, (b + 1) * J):
                            last = v.bn_aggr(mv[:, i, :], stats[:, i, :])
                        last.then_inc(s["var_ready"], 1)
                    if b >= 1:
                        dve.wait_ge(s["std_ready"], b)
                        link(v.reciprocal(rstd[:, (b - 1) * J:b * J], std[:, (b - 1) * J:b * J]))
                        for i in range((b - 1) * J, b * J):
                            last = v.tensor_scalar(rows_all[:, i, :], rows_all[:, i, :], mv[:, i, 0:1], rstd[:, i:i + 1],
                                                   ALU.subtract, ALU.mult)
                        last.then_inc(s["xn_ready"], 1)
                dve.wait_ge(s["logits_ready"], 1)
                link(v.tensor_copy(prob[:], bk(4)[:, 0:T * E].rearrange("p (j e) -> p j e", j=T)))
                top_two(v, dve, link, dict(prob=prob, small=small, rank=rank, gates=picked, cmp_a=cmp_a, cmp_b=cmp_b, c=c),
                        s, normalise=False)
                dve.wait_ge(s["gates_ready"], 1)
                for k in range(2):
                    link(v.scalar_tensor_tensor(chosen[:], rank[:], float(k), prob[:], ALU.is_equal, ALU.mult))
                    link(v.tensor_reduce(t["gate2"][:, k, :].unsqueeze(2), chosen[:], AX, ALU.add))
                v.tensor_scalar(picked[:], rank[:], 1.5, None, ALU.is_lt).then_inc(s["picked_ready"], 1)
                dve.wait_ge(s["counts_psum"], 1)
                counts = bk(0)[:, 0:T * E].rearrange("p (i e) -> p e i", e=E)
                link(v.tensor_copy(upto[:], counts))
                for e in range(E):
                    last = v.tensor_tensor_scan(slot[:].rearrange("p i e -> p (i e)")[:, e * T:(e + 1) * T], c["ones"][:, 0:T],
                                                upto[:, e, :], 0.0, ALU.mult, ALU.add)
                link(last)
                total = slot[:].rearrange("p i e -> p (i e)").rearrange("p (e i) -> p e i", e=E)
                link(v.tensor_tensor(upto[:], total, upto[:], ALU.subtract))
                over = chosen[:].rearrange("p i e -> p (i e)").rearrange("p (e i) -> p e i", e=E)
                link(v.tensor_tensor(over, total[:, :, T - 1:T].to_broadcast([P, E, T]),
                                     c["steps"][:].unsqueeze(1).to_broadcast([P, E, T]), ALU.is_gt))
                link(v.tensor_reduce(n_tiles[:].unsqueeze(2), over, AX, ALU.add))
                link(v.tensor_tensor_scan(first[:], c["ones"][:, 0:E], n_tiles[:], 0.0, ALU.mult, ALU.add))
                link(v.tensor_tensor(first[:], first[:], n_tiles[:], ALU.subtract))
                link(v.scalar_tensor_tensor(upto[:], first[:].unsqueeze(2).to_broadcast([P, E, T]), float(P), upto[:],
                                            ALU.mult, ALU.add))
                link(v.tensor_tensor(slot[:], bk(5)[:, 0:T * E].rearrange("p (i e) -> p i e", e=E),
                                     upto[:].rearrange("p e i -> p i e"), ALU.add))
                for k in range(2):
                    link(v.scalar_tensor_tensor(chosen[:], rank[:], float(k), slot[:], ALU.is_equal, ALU.mult))
                    link(v.tensor_reduce(slot_f[:, k, :].unsqueeze(2), chosen[:], AX, ALU.add))
                v.tensor_copy(t["slot2"][:], slot_f[:]).then_inc(s["slots_ready"], 1)
                dve.wait_ge(s["slots_ready"], 1)
                for h in range(0, NT, 32):
                    n = min(32, NT - h)
                    reached = cmp_a[:].rearrange("p a b c -> p (a b) c")[:, 0:n, :]
                    link(v.tensor_tensor(reached, c["tiles"][:, h:h + n].unsqueeze(2).to_broadcast([P, n, E]),
                                         first[:].unsqueeze(1).to_broadcast([P, n, E]), ALU.is_ge))
                    link(v.tensor_reduce(expert_f[:, h:h + n].unsqueeze(2), reached, AX, ALU.add))
                link(v.tensor_scalar(expert_f[:], expert_f[:], -1.0, None, ALU.add))
                link(v.tensor_copy(t["expert_of"][:], expert_f[:]))
                scan.vector_front(dve)
                for n in range(NS):
                    scan.step(dve, n)
                scan.gate(dve)
                scan.finish(dve)
        nc.all_engine_barrier(sems_to_clear=span(taken))


def experts0(nc, sems_of_stage, bk, c, xs, ys, t):
    wexp, bias16, ones16, expert_of = c["wexp"], t["bias16"], t["ones16"], t["expert_of"]
    taken = []
    with ExitStack() as own:
        def sb(name, shape, dt=F32):
            return own.enter_context(nc.sbuf_tensor(name, shape, dt))
        xrow = sb("xrow", [P, TP, P])
        xcol = sb("xcol", [P, 3, P])
        gel = sb("gel", [P, 2, L])
        hid = sb("hid", [P, 2, L])
        hid_t = sb("hid_t", [P, 2, L])
        yrow = sb("yrow", [P, TP, P])
        names = ("rows_in rows2_in xcol_psum xcol_ready gate_psum up_psum gel_ready hid_ready hid_t_psum hid_t_ready down_psum yrow_ready y_out")
        s = dict(zip(names.split(), sems_of_stage(names, own, taken)))

        with nc.Fori(0, PASSES) as b:
            with nc.Block() as block:
                @block.sync
                def _(sp):
                    half = TP // 2
                    for h, sem in enumerate(("rows_in", "rows2_in")):
                        rows = xs[bass.ds(b * (TP * P) + h * (half * P), half * P)]
                        sp.dma_start(xrow[:, h * half:(h + 1) * half, :], rows.rearrange("(m p) d -> p m d", p=P)).then_inc(s[sem], 16)
                    for h in range(2):
                        sp.wait_ge(s["yrow_ready"], (h + 1) * half)
                        rows = ys[bass.ds(b * (TP * P) + h * (half * P), half * P)]
                        sp.dma_start(rows.rearrange("(m p) d -> p m d", p=P), yrow[:, h * half:(h + 1) * half, :]).then_inc(s["y_out"], 16)
                    sp.wait_ge(s["y_out"], 32)

                @block.tensor
                def _(pe):
                    mm = nc.tensor.matmul
                    experts = {}

                    def turn_rows(m):
                        if m == 0:
                            pe.wait_ge(s["rows_in"], 16)
                        if m == TP // 2:
                            pe.wait_ge(s["rows2_in"], 16)
                        if m >= 1:
                            pe.wait_ge(s["xcol_ready"], m)
                        nc.tensor.transpose(bk(6)[:, 0:P], xrow[:, m, :], c["ident"][:]).then_inc(s["xcol_psum"], 1)

                    def up(m):
                        pair = 2 * (m % 2)
                        experts[m] = pe.value_load(expert_of[0:1, bass.ds(b * TP + m, 1)], min_val=0, max_val=E - 1)
                        if m >= 2:
                            pe.wait_ge(s["hid_ready"], m - 1)
                        pe.wait_ge(s["xcol_ready"], m + 1)
                        for half, sem in ((0, "gate_psum"), (1, "up_psum")):
                            mm(bk(pair + half), ones16[:], bias16[:, bass.ds(experts[m] * XB + half * FF, FF)], start=True, stop=False)
                            mm(bk(pair + half), xcol[:, m % 3, :], wexp[:, bass.ds(experts[m] * XW + half * FF, FF)],
                               start=False, stop=True).then_inc(s[sem], 1)

                    def turn_hidden(m):
                        pe.wait_ge(s["hid_ready"], m + 1)
                        if m >= 2:
                            pe.wait_ge(s["hid_t_ready"], m - 1)
                        for f in range(FT):
                            last = nc.tensor.transpose(bk(4 + m % 2)[:, f * P:(f + 1) * P], hid[:, m % 2, f * P:(f + 1) * P], c["ident"][:])
                        last.then_inc(s["hid_t_psum"], 1)

                    def down(m):
                        pe.wait_ge(s["hid_t_ready"], m + 1)
                        if m >= 1:
                            pe.wait_ge(s["yrow_ready"], m)
                        mm(bk(7)[:, 0:P], ones16[:], bias16[:, bass.ds(experts[m] * XB + 2 * FF, P)], start=True, stop=False)
                        for f in range(FT):
                            last = mm(bk(7)[:, 0:P], hid_t[:, m % 2, f * P:(f + 1) * P],
                                      wexp[:, bass.ds(experts[m] * XW + (2 * FF + f * P), P)], start=False, stop=(f == FT - 1))
                        last.then_inc(s["down_psum"], 1)

                    turn_rows(0)
                    turn_rows(1)
                    for m in range(TP + 2):
                        if m < TP:
                            up(m)
                        if m + 2 < TP:
                            turn_rows(m + 2)
                        if 1 <= m <= TP:
                            turn_hidden(m - 1)
                        if m >= 2:
                            down(m - 2)

                @block.scalar
                def _(act):
                    af = nc.scalar.activation

                    def take_rows(m):
                        act.wait_ge(s["xcol_psum"], m + 1)
                        if m >= 3:
                            act.wait_ge(s["up_psum"], m - 2)
                        af(xcol[:, m % 3, :], bk(6)[:, 0:P], ACT.Copy).then_inc(s["xcol_ready"], 1)
                    take_rows(0)
                    take_rows(1)
                    for m in range(TP + 1):
                        if m < TP:
                            act.wait_ge(s["gate_psum"], m + 1)
                            if m >= 2:
                                act.wait_ge(s["hid_ready"], m - 1)
                            af(gel[:, m % 2, :], bk(2 * (m % 2)), ACT.Gelu).then_inc(s["gel_ready"], 1)
                        if m + 2 < TP:
                            take_rows(m + 2)
                        if m >= 1:
                            act.wait_ge(s["hid_t_psum"], m)
                            if m >= 3:
                                act.wait_ge(s["down_psum"], m - 2)
                            af(hid_t[:, (m - 1) % 2, :], bk(4 + (m - 1) % 2), ACT.Copy).then_inc(s["hid_t_ready"], 1)

                @block.vector
                def _(dve):
                    v = nc.vector
                    for m in range(TP + 2):
                        if m < TP:
                            dve.wait_ge(s["up_psum"], m + 1)
                            dve.wait_ge(s["gel_ready"], m + 1)
                            if m >= 2:
                                dve.wait_ge(s["hid_t_psum"], m - 1)
                            v.tensor_tensor(hid[:, m % 2, :], bk(1 + 2 * (m % 2)), gel[:, m % 2, :], ALU.mult).then_inc(s["hid_ready"], 1)
                        if m >= 2:
                            dve.wait_ge(s["down_psum"], m - 1)
                            v.tensor_copy(yrow[:, m - 2, :], bk(7)[:, 0:P]).then_inc(s["yrow_ready"], 1)
            nc.all_engine_barrier(sems_to_clear=span(taken))


def top_two(v, dve, link, t, s, normalise):
    prob, small, gates, rank, cmp_a, cmp_b, c = (t[k] for k in "prob small gates rank cmp_a cmp_b c".split())

    n = prob.shape[1]

    def over(col):
        return small[:, :, col:col + 1].to_broadcast([P, n, E])
    link(v.tensor_reduce(small[:, :, 0:1], prob[:], AX, ALU.max))
    v.tensor_tensor(prob[:], prob[:], over(0), ALU.subtract).then_inc(s["shifted"], 1)
    dve.wait_ge(s["exp_ready"], 1)
    link(v.tensor_reduce(small[:, :, 1:2], prob[:], AX, ALU.add))
    link(v.reciprocal(small[:, :, 2:3], small[:, :, 1:2]))
    link(v.tensor_tensor(prob[:], prob[:], over(2), ALU.mult))
    other = prob[:].unsqueeze(2).to_broadcast([P, n, E, E])
    mine = prob[:].unsqueeze(3).to_broadcast([P, n, E, E])
    v.tensor_tensor(cmp_a[:], other, mine, ALU.is_gt)
    link(v.tensor_tensor(cmp_b[:], other, mine, ALU.is_equal))
    lower = c["lower"][:].rearrange("p (a b) -> p a b", a=E).unsqueeze(1).to_broadcast([P, n, E, E])
    link(v.tensor_tensor(cmp_b[:], cmp_b[:], lower, ALU.mult))
    link(v.tensor_tensor(cmp_a[:], cmp_a[:], cmp_b[:], ALU.add))
    link(v.tensor_reduce(rank[:].unsqueeze(3), cmp_a[:], AX, ALU.add))
    if not normalise:
        v.scalar_tensor_tensor(gates[:], rank[:], 1.5, prob[:], ALU.is_lt, ALU.mult).then_inc(s["gates_ready"], 1)
        return
    link(v.scalar_tensor_tensor(gates[:], rank[:], 1.5, prob[:], ALU.is_lt, ALU.mult))
    link(v.tensor_reduce(small[:, :, 3:4], gates[:], AX, ALU.add))
    link(v.reciprocal(small[:, :, 2:3], small[:, :, 3:4]))
    v.tensor_tensor(gates[:], gates[:], over(2), ALU.mult).then_inc(s["gates_ready"], 1)


def layer1(nc, sems_of_stage, bk, bank, c, x, ys, out, t):
    vaug, wvo = t["vaug"], t["wvo"]
    taken = []
    with ExitStack() as own:
        def sb(name, shape, dt=F32):
            return own.enter_context(nc.sbuf_tensor(name, shape, dt))
        xt = sb("xt", [P, J, P])
        stats = sb("stats", [P, J, 6])
        mv = sb("mv", [P, J, 2])
        spread2 = sb("spread2", [P, J])
        rstd = sb("rstd", [P, J])
        mean_sq = sb("mean_sq", [P, J])
        rrms = sb("rrms", [P, J])
        xn = sb("xn", [P, J, P])
        xn_t = sb("xn_t", [P, L])
        prob = sb("prob", [P, J, E])
        small = sb("small", [P, J, 4])
        cmp_a = sb("cmp_a", [P, J, E, E])
        cmp_b = sb("cmp_b", [P, J, E, E])
        rank = sb("rank", [P, J, E])
        gates = sb("gates", [P, J, E])
        gates_t = sb("gates_t", [E, L])
        srow = sb("srow", [P, J, P])
        macc = sb("macc", [P, J, P])
        grow = sb("grow", [P, J, P])
        gate_now = sb("gate_now", [P, 2, J])
        slot_now = sb("slot_now", [P, 2, J], U32)
        expert_out = sb("expert_out", [P, 2, J, P])
        ssq = sb("ssq", [P, J])
        xr = sb("xr", [P, J, P])
        xr_t = sb("xr_t", [P, L])
        q1 = sb("q1", [P, L])
        k1 = sb("k1", [P, L])
        v1 = sb("v1", [P, J, P])
        neg_max1 = sb("neg_max1", [P, J])
        den1 = sb("den1", [P, J])
        rden1 = sb("rden1", [P, J])
        p1 = sb("p1", [P, J, L])
        p1_t = sb("p1_t", [P, J, L])
        kk = sb("kk", [P, L])
        k_high = sb("k_high", [P, L], F32R)
        k_low = sb("k_low", [P, L], F32R)
        qc = sb("qc", [P, 2, L])
        qs = sb("qs", [P, 2, L])
        q = sb("q", [P, 2, L])
        q_stack = sb("q_stack", [P, 4, 2, L], F32R)
        neg_max = sb("neg_max", [P, 2, J, 2])
        neg_max_t = sb("neg_max_t", [2, 2, L], F32R)
        probs = sb("probs", [P, 3, 2, L])
        o = sb("o", [P, 4, L])
        rec = sb("rec", [P, J, 4])
        rec_wide = macc
        x2 = expert_out[:, 0, :, :]
        hm = [p1[:, n, :] for n in range(MT)] + [p1_t[:, 0, :]]
        hm1 = p1_t[:, 1, :]
        silu_g = [p1_t[:, 2, :], p1_t[:, 3, :]]

        rows_gathered = t["rows_gathered"]
        names = ("x_in slot_copied moe0_ready silu0_ready var_ready rstd_ready xn_ready xnt_psum xnt_ready rrms_ready xr_ready xrt_psum xrt_ready "
                 "qkv_psum qk_ready v_ready kproj_psum lat_psum vaug_ready rope_used kk_ready kh_ready k_ready s1_psum max1_ready p1_ready pt_psum "
                 "pt_ready av1_psum s1_ready q_psum q_ready high_ready low_ready max_psum max_used nmt_psum nmt_ready "
                 "st_psum p_ready av_done o_ready den_psum recip_ready wide_ready rec_psum yn_ready att_psum x2_ready ssq_ready rrms2_ready xm_ready "
                 "xmt_psum xmt_ready logits_ready shifted exp_ready gates_ready gates_psum gates_t_ready "
                 "g1_psum u1_psum comb_psum silu1_ready hm_ready moe_psum moe_ready silu_ready out_ready stored dve_chain pool_chain")
        s = dict(zip(names.split(), sems_of_stage(" ".join("l1_" + n for n in names.split()), own, taken)))
        s.update(zip(SCAN_SEMS.split(), sems_of_stage(" ".join("l1_" + n for n in SCAN_SEMS.split()), own, taken)))
        row_in = sems_of_stage(" ".join(f"l1_row_in{p}" for p in range(HP)), own, taken)
        scan = Scan(nc, t, c, bk, s)
        groups = (((3, 0),), ((2, 0), (0, 3 * P)), ((1, 0),))
        scan_at = scan_steps_of_pairs()

        def quad_bank(g):
            return bk(4 + (g + 1) % 2)

        with nc.Fori(0, B) as b:
            with nc.Block() as block:
                @block.sync
                def _(sp):
                    sp.dma_start(xt[:], x[bass.ds(b, 1)].rearrange("o (j p) d -> (o p) j d", p=P)).then_inc(s["x_in"], 16)

                    def maximum_rows(p):
                        sp.wait_ge(s["nmt_ready"], p + 1)
                        sp.wait_ge(s["low_ready"], p + 1)
                        for parity in range(2):
                            row = 64 * parity + KD - 1
                            sp.dma_start(q_stack[row:row + 1, p % 4, parity, :].bitcast(F32),
                                         neg_max_t[parity:parity + 1, p % 2, :].bitcast(F32)).then_inc(row_in[p], 16)

                    maximum_rows(0)
                    for p in range(HP):
                        if p + 1 < HP:
                            maximum_rows(p + 1)
                    sp.wait_ge(s["out_ready"], 1)
                    sp.dma_start(out[bass.ds(b, 1)].rearrange("o (j p) d -> (o p) j d", p=P), macc[:]).then_inc(s["stored"], 16)
                    sp.wait_ge(s["stored"], 16)

                @block.tensor
                def _(pe):
                    mm = nc.tensor.matmul
                    tr = nc.tensor.transpose
                    ident = c["ident"]

                    def rows_to_t(o_, rows, sem):
                        for j in range(J):
                            last = tr(bk(o_)[:, j * P:(j + 1) * P], rows[:, j, :], ident[:])
                        last.then_inc(s[sem], 1)
                    for what in ("dt", "bc", "x", "z"):
                        scan.project(pe, what)
                    scan.spread(pe, 0)
                    scan.spread(pe, 1)
                    pe.wait_ge(s["xn_ready"], 1)
                    rows_to_t(0, xn, "xnt_psum")
                    pe.wait_ge(s["xr_ready"], 1)
                    rows_to_t(1, xr, "xrt_psum")
                    scan.spread(pe, 2)
                    pe.wait_ge(s["xnt_ready"], 1)
                    mm(bk(2), c["wq1"][:], xn_t[:], start=True, stop=True)
                    mm(bk(3), c["wk1"][:], xn_t[:], start=True, stop=True).then_inc(s["qkv_psum"], 1)
                    for j in range(J):
                        last = mm(bk(4)[:, j * P:(j + 1) * P], xn_t[:, j * P:(j + 1) * P], c["wv1"][:], start=True, stop=True)
                    last.then_inc(s["qkv_psum"], 1)
                    pe.wait_ge(s["xrt_ready"], 1)
                    mm(bk(0), c["wk"][:], xr_t[:], start=True, stop=True)
                    mm(bk(1), c["wk_swap"][:], xr_t[:], start=True, stop=True).then_inc(s["kproj_psum"], 1)
                    for j in range(J):
                        last = mm(bk(5)[:, j * LAT:(j + 1) * LAT], xr_t[:, j * P:(j + 1) * P], c["wlat"][:], start=True, stop=True)
                    last.then_inc(s["lat_psum"], 1)

                    def query(p):
                        if p <= 1:
                            pe.wait_ge(s["rope_used"], p + 1)
                        elif p == 2:
                            pe.wait_ge(s["max_used"], 3)
                        else:
                            pe.wait_ge(s["nmt_ready"], p - 1)
                        cols = slice(p * P, (p + 1) * P)
                        mm(bk(0), c["wq"][:, cols], xr_t[:], start=True, stop=True)
                        mm(bk(1), c["wq_swap"][:, cols], xr_t[:], start=True, stop=True).then_inc(s["q_psum"], 1)

                    def maxima(p, g):
                        if g > 0:
                            pe.wait_ge(s["max_used"], 3 * p + g)
                        elif p == 0:
                            pe.wait_ge(s["rope_used"], 3)
                            pe.wait_ge(s["kh_ready"], 1)
                        elif p == 1 or p == HP - 1:
                            pe.wait_ge(s["nmt_ready"], p)
                        else:
                            pe.wait_ge(s["rope_used"], p + 3)
                        pe.wait_ge(s["high_ready"], p + 1)
                        for i, at in groups[g]:
                            n = (i + 1) * P
                            for parity in range(2):
                                rows = slice(64 * parity, 64 * parity + KD - 1)
                                dst = bank[0][:, parity, at:at + n]
                                mm(dst, q_stack[rows, p % 4, parity, i * P:(i + 1) * P], k_high[rows, 0:n], start=True, stop=False)
                                last = mm(dst[:, i * P:n], t["ident16"][:], t["mask16"][:], start=False, stop=True)
                        last.then_inc(s["max_psum"], 1)

                    def turn_maxima(p):
                        pe.wait_ge(s["max_used"], 3 * (p + 1))
                        if p == 0:
                            pe.wait_ge(s["rope_used"], 4)
                        for i in range(J):
                            last = tr(bk(0)[0:2, i * P:(i + 1) * P], neg_max[:, p % 2, i, :], ident[:])
                        last.then_inc(s["nmt_psum"], 1)

                    def scores(n):
                        p, kt = divmod(n, J)
                        if kt == 0:
                            pe.wait_ge(row_in[p], 32)
                        if n == 0:
                            pe.wait_ge(s["k_ready"], 1)
                        else:
                            pe.wait_ge(s["p_ready"], n)
                        for parity in range(2):
                            dst = bank[1][:, parity, 0:L - kt * P]
                            query_t = q_stack[:, p % 4, parity, kt * P:L]
                            mm(dst, k_high[:, kt * P:(kt + 1) * P], query_t, start=True, stop=False)
                            mm(dst, k_low[:, kt * P:(kt + 1) * P], query_t, start=False, stop=False)
                            last = mm(dst[:, 0:P], t["ident16"][:], t["mask_t16"][:], start=False, stop=True)
                        last.then_inc(s["st_psum"], 1)

                    def weigh(n):
                        p, kt = divmod(n, J)
                        g = p // 2
                        pe.wait_ge(s["p_ready"], n + 1)
                        if n == 8:
                            pe.wait_ge(s["s1_ready"], 1)
                        elif n % 8 == 0 and g >= 2:
                            pe.wait_ge(s["yn_ready"], g - 1)
                        for parity in range(2):
                            slot = 32 * (2 * (p % 2) + parity)
                            last = mm(quad_bank(g)[slot:slot + 32, kt * P:L], vaug[:, kt, :],
                                      probs[:, n % 3, parity, 0:L - kt * P], start=(kt == 0), stop=(kt == J - 1))
                        last.then_inc(s["av_done"], 1)

                    def denominators(g):
                        pe.wait_ge(s["o_ready"], g + 1)
                        for j in range(J):
                            last = mm(quad_bank(g)[:, 4 * j:4 * j + 4], o[:, g, j * P:(j + 1) * P], c["sel_den"][:],
                                      start=True, stop=True)
                        last.then_inc(s["den_psum"], 1)

                    def spread_reciprocals(g):
                        pe.wait_ge(s["wide_ready"], g + 1)
                        for j in range(J):
                            last = tr(quad_bank(g)[:, j * P:(j + 1) * P], rec_wide[:, j, :], ident[:])
                        last.then_inc(s["rec_psum"], 1)

                    query(0)
                    pe.wait_ge(s["qk_ready"], 2)
                    for i in range(J):
                        if i == 2:
                            pe.wait_ge(s["v_ready"], 1)
                        if i == 3:
                            pe.wait_ge(s["vaug_ready"], 1)
                        mm(bk(2 + i)[:, 0:(i + 1) * P], q1[:, i * P:(i + 1) * P], k1[:, 0:(i + 1) * P], start=True, stop=False)
                        mm(bk(2 + i)[:, i * P:(i + 1) * P], t["ident16"][:], t["mask16"][:], start=False,
                           stop=True).then_inc(s["s1_psum"], 1)
                    query(1)
                    scan.spread(pe, 3)
                    pe.wait_ge(s["p1_ready"], J)
                    for k in range(J):
                        for i in range(k, J):
                            last = tr(bk(2 + k)[:, i * P:(i + 1) * P], p1[:, i, k * P:(k + 1) * P], ident[:])
                        last.then_inc(s["pt_psum"], 1)
                    for g in range(3):
                        maxima(0, g)
                    query(2)
                    turn_maxima(0)
                    maxima(1, 0)
                    pe.wait_ge(s["pt_ready"], J)
                    for i in range(J):
                        for k in range(i + 1):
                            last = mm(bk(4)[:, i * P:(i + 1) * P], p1_t[:, k, i * P:(i + 1) * P], v1[:, k, :],
                                      start=(k == 0), stop=(k == i))
                    last.then_inc(s["av1_psum"], 1)
                    maxima(1, 1)
                    maxima(1, 2)

                    for p in range(HP):
                        if p + 1 < HP:
                            turn_maxima(p + 1)
                        scores(4 * p)
                        if p >= 1:
                            weigh(4 * p - 1)
                        if p + 3 < HP:
                            query(p + 3)
                        for n in scan_at[p][:1]:
                            scan.spread(pe, n)
                        scores(4 * p + 1)
                        weigh(4 * p)
                        if p + 2 < HP:
                            maxima(p + 2, 0)
                        if p % 2 == 1 and p >= 3:
                            spread_reciprocals((p - 3) // 2)
                        scores(4 * p + 2)
                        weigh(4 * p + 1)
                        if p % 2 == 0 and p >= 2:
                            denominators(p // 2 - 1)
                        if p + 2 < HP:
                            maxima(p + 2, 1)
                        for n in scan_at[p][1:]:
                            scan.spread(pe, n)
                        scores(4 * p + 3)
                        weigh(4 * p + 2)
                        if p + 2 < HP:
                            maxima(p + 2, 2)
                    weigh(4 * HP - 1)
                    scan.spread(pe, NS - 2)
                    denominators(3)
                    scan.spread(pe, NS - 1)

                    for g in range(4):
                        if g == 3:
                            spread_reciprocals(3)
                        pe.wait_ge(s["yn_ready"], g + 1)
                        if g == 0:
                            pe.wait_ge(s["p_ready"], HP * J)
                        for j in range(J):
                            last = mm(bk(j)[:, 0:P], o[:, g, j * P:(j + 1) * P], wvo[:, g, :], start=(g == 0), stop=(g == 3))
                    last.then_inc(s["att_psum"], 1)
                    scan.project_out(pe)

                    pe.wait_ge(s["xm_ready"], 1)
                    rows_to_t(4, xr, "xmt_psum")
                    pe.wait_ge(s["xmt_ready"], 1)
                    for j in range(J):
                        last = mm(bk(5)[:, j * E:(j + 1) * E], xr_t[:, j * P:(j + 1) * P], c["router1"][:], start=True, stop=True)
                    last.then_inc(s["logits_ready"], 1)
                    sets = ((0, 1, 2), (3, 4, 5))

                    def up(n):
                        if n >= 2:
                            pe.wait_ge(s["hm_ready"], n - 1)
                        g_, u_, _ = sets[n % 2]
                        cols = slice(n * P, (n + 1) * P)
                        mm(bk(g_), c["wg1"][:, cols], xr_t[:], start=True, stop=True).then_inc(s["g1_psum"], 1)
                        mm(bk(u_), c["wu1"][:, cols], xr_t[:], start=True, stop=True).then_inc(s["u1_psum"], 1)

                    def spread_gates(n):
                        mm(bk(sets[n % 2][2]), c["sel_comb"][:, n * P:(n + 1) * P], gates_t[:], start=True,
                           stop=True).then_inc(s["comb_psum"], 1)
                    up(0)
                    up(1)
                    pe.wait_ge(s["gates_ready"], 1)
                    for j in range(J):
                        last = tr(bk(2)[0:E, j * P:(j + 1) * P], gates[:, j, :], ident[:])
                    last.then_inc(s["gates_psum"], 1)
                    pe.wait_ge(s["gates_t_ready"], 1)
                    spread_gates(0)
                    spread_gates(1)
                    for n in range(2, MT + 1):
                        up(n)
                        if n < MT:
                            spread_gates(n)
                    for n in range(MT + 1):
                        pe.wait_ge(s["hm_ready"], n + 1)
                    for j in range(J):
                        for n in range(MT + 1):
                            last = mm(bk(3)[:, j * P:(j + 1) * P], hm[n][:, j * P:(j + 1) * P], c["wd1"][:, n * P:(n + 1) * P],
                                      start=(n == 0), stop=(n == MT))
                    last.then_inc(s["moe_psum"], 1)

                @block.scalar
                def _(act):
                    af = nc.scalar.activation
                    scan.act_front(act)
                    for n in range(4):
                        scan.decay(act, n)
                    act.wait_ge(s["moe0_ready"], 1)
                    af(grow[:], macc[:], ACT.Silu).then_inc(s["silu0_ready"], 1)
                    scan.decay(act, 4)
                    scan.decay(act, 5)
                    act.wait_ge(s["xnt_psum"], 1)
                    af(xn_t[:], bk(0), ACT.Copy).then_inc(s["xnt_ready"], 1)
                    act.wait_ge(s["xrt_psum"], 1)
                    af(xr_t[:], bk(1), ACT.Copy, scale=c["ln1"][:]).then_inc(s["xrt_ready"], 1)
                    act.wait_ge(s["qkv_psum"], 1)
                    af(q1[:], bk(2), ACT.Copy).then_inc(s["qk_ready"], 1)
                    af(k1[:], bk(3), ACT.Copy).then_inc(s["qk_ready"], 1)
                    act.wait_ge(s["kk_ready"], 1)
                    af(k_high[:], kk[:], ACT.Copy).then_inc(s["kh_ready"], 1)
                    scan.decay(act, 6)

                    def high_parts(p):
                        act.wait_ge(s["q_ready"], p + 1)
                        if p >= 4:
                            act.wait_ge(s["st_psum"], 4 * (p - 3))
                        for parity in range(2):
                            rows = slice(64 * parity, 64 * parity + 64)
                            last = af(q_stack[rows, p % 4, parity, :], q[rows, p % 2, :], ACT.Copy)
                        last.then_inc(s["high_ready"], 1)

                    def take_maxima(p):
                        act.wait_ge(s["nmt_psum"], p + 1)
                        if p >= 2:
                            act.wait_ge(row_in[p - 2], 32)
                        af(neg_max_t[:, p % 2, :], bk(0)[0:2, :], ACT.Copy).then_inc(s["nmt_ready"], 1)

                    def take_quad(g):
                        act.wait_ge(s["av_done"], 8 * (g + 1))
                        af(o[:, g, :], quad_bank(g), ACT.Copy).then_inc(s["o_ready"], 1)

                    def exponentials(n):
                        kt = n % J
                        act.wait_ge(s["st_psum"], n + 1)
                        if n >= 3:
                            act.wait_ge(s["av_done"], n - 2)
                        af(probs[:, n % 3, :, 0:L - kt * P], bank[1][:, :, 0:L - kt * P], ACT.Exp,
                           scale=0.125).then_inc(s["p_ready"], 1)
                    high_parts(0)
                    act.wait_ge(s["max1_ready"], 1)
                    for i in range(J):
                        af(p1[:, i, 0:(i + 1) * P], bk(2 + i)[:, 0:(i + 1) * P], ACT.Exp, bias=neg_max1[:, i:i + 1],
                           scale=float(P) ** -0.5, accum_out=den1[:, i:i + 1]).then_inc(s["p1_ready"], 1)
                    high_parts(1)
                    for k in range(J):
                        act.wait_ge(s["pt_psum"], k + 1)
                        af(p1_t[:, k, k * P:L], bk(2 + k)[:, k * P:L], ACT.Copy).then_inc(s["pt_ready"], 1)
                    scan.decay(act, 7)
                    take_maxima(0)
                    high_parts(2)
                    for p in range(HP):
                        if p + 1 < HP:
                            take_maxima(p + 1)
                        exponentials(4 * p)
                        if p % 2 == 0 and p >= 2:
                            take_quad(p // 2 - 1)
                        exponentials(4 * p + 1)
                        if p + 3 < HP:
                            high_parts(p + 3)
                        exponentials(4 * p + 2)
                        for n in scan_at[p]:
                            if n + 4 < NS:
                                scan.decay(act, n + 4)
                        exponentials(4 * p + 3)
                    take_quad(3)
                    act.wait_ge(s["x2_ready"], 1)
                    for j in range(J):
                        last = af(grow[:, j, :], x2[:, j, :], ACT.Square, accum_out=ssq[:, j:j + 1])
                    last.then_inc(s["ssq_ready"], 1)
                    act.wait_ge(s["xmt_psum"], 1)
                    af(xr_t[:], bk(4), ACT.Copy, scale=c["ln2"][:]).then_inc(s["xmt_ready"], 1)
                    act.wait_ge(s["shifted"], 1)
                    af(prob[:], prob[:], ACT.Exp).then_inc(s["exp_ready"], 1)
                    for n in range(MT + 1):
                        act.wait_ge(s["g1_psum"], n + 1)
                        if n >= 2:
                            act.wait_ge(s["hm_ready"], n - 1)
                        af(silu_g[n % 2], bk((0, 3)[n % 2]), ACT.Silu).then_inc(s["silu1_ready"], 1)
                        if n == 1:
                            act.wait_ge(s["gates_psum"], 1)
                            af(gates_t[:], bk(2)[0:E, :], ACT.Copy).then_inc(s["gates_t_ready"], 1)
                    act.wait_ge(s["ssq_ready"], 1)
                    act.wait_ge(s["moe_ready"], 1)
                    af(grow[:], x2[:], ACT.Silu).then_inc(s["silu_ready"], 1)

                @block.gpsimd
                def _(pool):
                    link = chain_of(pool, s["pool_chain"])
                    g_ = nc.gpsimd
                    scan.copy_in(pool, b + 1)
                    g_.tensor_copy(slot_now[:], t["slot2"][:, :, bass.ds(b * J, J)]).then_inc(s["slot_copied"], 1)
                    pool.wait_ge(s["slot_copied"], 1)
                    for j in range(J):
                        for k in range(2):
                            g_.indirect_dma_start(
                                out=expert_out[:, k, j, :], out_offset=None, in_=ys,
                                in_offset=bass.IndirectOffsetOnAxis(ap=slot_now[:, k, j:j + 1], axis=0)).then_inc(rows_gathered, 16)
                    scan.add(pool, 0)
                    scan.add(pool, 1)
                    pool.wait_ge(s["var_ready"], 1)
                    link(g_.tensor_scalar(spread2[:], mv[:, :, 1], EPS, None, ALU.add))
                    g_.tensor_tensor(rstd[:], spread2[:], t["minus_half"][:], ALU.pow).then_inc(s["rstd_ready"], 1)
                    pool.wait_ge(s["rstd_ready"], 1)
                    link(g_.tensor_tensor(mean_sq[:], rstd[:], rstd[:], ALU.mult))
                    link(g_.tensor_tensor(mean_sq[:], mean_sq[:], mv[:, :, 1], ALU.mult))
                    link(g_.tensor_scalar(mean_sq[:], mean_sq[:], EPS, None, ALU.add))
                    g_.tensor_tensor(rrms[:], mean_sq[:], t["minus_half"][:], ALU.pow).then_inc(s["rrms_ready"], 1)
                    scan.add(pool, 2)

                    def queries(p):
                        pool.wait_ge(s["rope_used"], p + 2)
                        if p >= 2:
                            pool.wait_ge(s["low_ready"], p - 1)
                        g_.tensor_tensor(q[:, p % 2, :], qc[:, p % 2, :], qs[:, p % 2, :], ALU.add).then_inc(s["q_ready"], 1)

                    def widen(g):
                        pool.wait_ge(s["recip_ready"], g + 1)
                        if g >= 1:
                            pool.wait_ge(s["rec_psum"], g)
                        else:
                            pool.wait_ge(s["silu0_ready"], 1)
                        g_.tensor_copy(rec_wide[:].rearrange("p j (k r) -> p j k r", k=4),
                                       rec[:].unsqueeze(3).to_broadcast([P, J, 4, 32])).then_inc(s["wide_ready"], 1)
                    queries(0)
                    queries(1)
                    scan.add(pool, 3)
                    queries(2)
                    for p in range(HP):
                        if p + 3 < HP:
                            queries(p + 3)
                        for n in scan_at[p][:1]:
                            scan.add(pool, n)
                        if p % 2 == 0 and p >= 2:
                            widen(p // 2 - 1)
                        for n in scan_at[p][1:]:
                            scan.add(pool, n)
                    scan.add(pool, NS - 2)
                    widen(3)
                    scan.add(pool, NS - 1)
                    pool.wait_ge(s["ssq_ready"], 1)
                    link(g_.tensor_scalar(mean_sq[:], ssq[:], 1.0 / P, EPS, ALU.mult, ALU.add))
                    pool.wait_ge(s["xr_ready"], 1)
                    g_.tensor_tensor(rrms[:], mean_sq[:], t["minus_half"][:], ALU.pow).then_inc(s["rrms2_ready"], 1)

                @block.vector
                def _(dve):
                    link = chain_of(dve, s["dve_chain"])
                    v = nc.vector
                    scan.vector_front(dve)
                    scan.step(dve, 0)
                    scan.step(dve, 1)
                    link(v.tensor_copy(gate_now[:], t["gate2"][:, :, bass.ds(b * J, J)]))
                    dve.wait_ge(rows_gathered, b * (16 * 2 * J) + 16 * 2 * J)
                    for j in range(J):
                        last = v.tensor_scalar(macc[:, j, :], expert_out[:, 0, j, :], gate_now[:, 0, j:j + 1], None, ALU.mult)
                    link(last)
                    for j in range(J):
                        last = v.scalar_tensor_tensor(macc[:, j, :], expert_out[:, 1, j, :], gate_now[:, 1, j:j + 1], macc[:, j, :],
                                                      ALU.mult, ALU.add)
                    last.then_inc(s["moe0_ready"], 1)
                    dve.wait_ge(s["silu0_ready"], 1)
                    link(v.tensor_tensor(srow[:], t["scan"]["rows"][:], grow[:], ALU.mult))
                    dve.wait_ge(s["x_in"], 16)
                    link(v.tensor_tensor(xt[:], xt[:], srow[:], ALU.add))
                    for j in range(J):
                        last = v.bn_stats(stats[:, j, :], xt[:, j, :])
                    link(last)
                    for j in range(J):
                        last = v.bn_aggr(mv[:, j, :], stats[:, j, :])
                    last.then_inc(s["var_ready"], 1)
                    dve.wait_ge(s["rstd_ready"], 1)
                    for j in range(J):
                        last = v.tensor_scalar(xn[:, j, :], xt[:, j, :], mv[:, j, 0:1], rstd[:, j:j + 1], ALU.subtract, ALU.mult)
                    last.then_inc(s["xn_ready"], 1)
                    dve.wait_ge(s["xn_ready"], 1)
                    dve.wait_ge(s["rrms_ready"], 1)
                    v.tensor_tensor(xr[:], xn[:], rrms[:].unsqueeze(2).to_broadcast([P, J, P]), ALU.mult).then_inc(s["xr_ready"], 1)
                    scan.step(dve, 2)
                    dve.wait_ge(s["qkv_psum"], 2)
                    v.tensor_copy(flat(v1[:]), bk(4)).then_inc(s["v_ready"], 1)
                    dve.wait_ge(s["kproj_psum"], 1)
                    v.tensor_tensor(qc[:, 0, :], bk(0), c["cos"][:], ALU.mult)
                    v.scalar_tensor_tensor(qs[:, 0, :], bk(1), c["one_row"][:], c["sin"][:], ALU.add, ALU.mult).then_inc(s["rope_used"], 1)
                    dve.wait_ge(s["rope_used"], 1)
                    v.tensor_tensor(kk[:], qc[:, 0, :], qs[:, 0, :], ALU.add).then_inc(s["kk_ready"], 1)
                    dve.wait_ge(s["lat_psum"], 1)
                    v.tensor_copy(vaug[:, :, 0:LAT], bk(5)[:, 0:J * LAT].rearrange("p (j f) -> p j f", j=J)).then_inc(s["vaug_ready"], 1)

                    def rope(p):
                        dve.wait_ge(s["q_psum"], p + 1)
                        if p >= 2:
                            dve.wait_ge(s["q_ready"], p - 1)
                        v.tensor_tensor(qc[:, p % 2, :], bk(0), c["cos"][:], ALU.mult)
                        v.tensor_tensor(qs[:, p % 2, :], bk(1), c["sin"][:], ALU.mult).then_inc(s["rope_used"], 1)

                    def low_parts(p):
                        dve.wait_ge(s["high_ready"], p + 1)
                        for parity in range(2):
                            rows = slice(64 * parity, 64 * parity + 64)
                            other = slice(64 - 64 * parity, 128 - 64 * parity)
                            last = v.tensor_tensor(q_stack[other, p % 4, parity, :], q[rows, p % 2, :],
                                                   q_stack[rows, p % 4, parity, :].bitcast(F32), ALU.subtract)
                        last.then_inc(s["low_ready"], 1)

                    def reduce_maxima(p, g):
                        dve.wait_ge(s["max_psum"], 3 * p + g + 1)
                        if p >= 2 and g == 0:
                            dve.wait_ge(s["nmt_psum"], p - 1)
                        for i, at in groups[g]:
                            last = v.tensor_reduce(neg_max[:, p % 2, i, :].unsqueeze(2), bank[0][:, :, at:at + (i + 1) * P], AX,
                                                   ALU.max, negate=True)
                        last.then_inc(s["max_used"], 1)

                    def reciprocals(g):
                        dve.wait_ge(s["den_psum"], g + 1)
                        if g >= 1:
                            dve.wait_ge(s["wide_ready"], g)
                        v.reciprocal(rec[:], quad_bank(g)[:, 0:4 * J].rearrange("p (j k) -> p j k", j=J)).then_inc(s["recip_ready"], 1)

                    def normalise(g):
                        dve.wait_ge(s["rec_psum"], g + 1)
                        v.tensor_tensor(o[:, g, :], o[:, g, :], quad_bank(g), ALU.mult).then_inc(s["yn_ready"], 1)

                    dve.wait_ge(s["kk_ready"], 1)
                    rope(0)
                    for i in range(J):
                        dve.wait_ge(s["s1_psum"], i + 1)
                        last = v.tensor_reduce(neg_max1[:, i:i + 1], bk(2 + i)[:, 0:(i + 1) * P], AX, ALU.max, negate=True)
                    link(last)
                    v.tensor_scalar(neg_max1[:], neg_max1[:], float(P) ** -0.5, None, ALU.mult).then_inc(s["max1_ready"], 1)
                    rope(1)
                    dve.wait_ge(s["kh_ready"], 1)
                    v.tensor_tensor(k_low[:], kk[:], k_high[:].bitcast(F32), ALU.subtract).then_inc(s["k_ready"], 1)
                    scan.step(dve, 3)
                    low_parts(0)
                    dve.wait_ge(s["p1_ready"], J)
                    link(v.reciprocal(rden1[:], den1[:]))
                    for g in range(3):
                        reduce_maxima(0, g)
                    low_parts(1)
                    rope(2)
                    reduce_maxima(1, 0)
                    dve.wait_ge(s["av1_psum"], 1)
                    v.tensor_tensor(srow[:], bk(4).rearrange("p (j d) -> p j d", j=J),
                                    rden1[:].unsqueeze(2).to_broadcast([P, J, P]), ALU.mult).then_inc(s["s1_ready"], 1)
                    reduce_maxima(1, 1)
                    reduce_maxima(1, 2)
                    low_parts(2)
                    for p in range(HP):
                        if p + 3 < HP:
                            rope(p + 3)
                        for n in scan_at[p][:1]:
                            scan.step(dve, n)
                        if p + 2 < HP:
                            reduce_maxima(p + 2, 0)
                        if p % 2 == 1 and p >= 3:
                            normalise((p - 3) // 2)
                        if p + 2 < HP:
                            reduce_maxima(p + 2, 1)
                        if p % 2 == 0 and p >= 2:
                            reciprocals(p // 2 - 1)
                        for n in scan_at[p][1:]:
                            scan.step(dve, n)
                        if p + 2 < HP:
                            reduce_maxima(p + 2, 2)
                        if p + 3 < HP:
                            low_parts(p + 3)
                    scan.step(dve, NS - 2)
                    reciprocals(3)
                    scan.step(dve, NS - 1)
                    scan.gate(dve)
                    normalise(3)
                    dve.wait_ge(s["att_psum"], 1)
                    for h in range(2):
                        last = v.tensor_tensor(x2[:, 2 * h:2 * h + 2, :], xn[:, 2 * h:2 * h + 2, :], bank[h][:, :, 0:P], ALU.add)
                    last.then_inc(s["x2_ready"], 1)
                    scan.finish(dve)
                    dve.wait_ge(s["x2_ready"], 1)
                    dve.wait_ge(s["rrms2_ready"], 1)
                    v.tensor_tensor(xr[:], x2[:], rrms[:].unsqueeze(2).to_broadcast([P, J, P]), ALU.mult).then_inc(s["xm_ready"], 1)
                    dve.wait_ge(s["logits_ready"], 1)
                    link(v.tensor_tensor(prob[:], bk(5)[:, 0:J * E].rearrange("p (j e) -> p j e", j=J),
                                         c["bias1"][:].unsqueeze(1).to_broadcast([P, J, E]), ALU.add))
                    top_two(v, dve, link, dict(prob=prob, small=small, rank=rank, gates=gates, cmp_a=cmp_a, cmp_b=cmp_b, c=c),
                            s, normalise=True)
                    for n in range(MT + 1):
                        u_, cb = ((1, 2), (4, 5))[n % 2]
                        dve.wait_ge(s["u1_psum"], n + 1)
                        dve.wait_ge(s["silu1_ready"], n + 1)
                        if n >= 1:
                            dve.wait_ge(s["hm_ready"], n)
                        if n < MT:
                            link(v.tensor_tensor(hm1, bk(u_), silu_g[n % 2], ALU.mult))
                            dve.wait_ge(s["comb_psum"], n + 1)
                            v.tensor_tensor(hm[n], hm1, bk(cb), ALU.mult).then_inc(s["hm_ready"], 1)
                        else:
                            v.tensor_tensor(hm[n], bk(u_), silu_g[n % 2], ALU.mult).then_inc(s["hm_ready"], 1)
                    dve.wait_ge(s["moe_psum"], 1)
                    v.tensor_tensor(flat(x2[:]), flat(x2[:]), bk(3), ALU.add).then_inc(s["moe_ready"], 1)
                    dve.wait_ge(s["silu_ready"], 1)
                    link(v.tensor_tensor(macc[:], srow[:], grow[:], ALU.mult))
                    v.tensor_tensor(macc[:], macc[:], xt[:], ALU.add).then_inc(s["out_ready"], 1)
            nc.all_engine_barrier(sems_to_clear=span(taken))


def scan_steps_of_pairs():
    counts = [1, 1, 1, 1, 1, 1, 2, 2]
    steps, n = [], 4
    for count in counts:
        steps.append(list(range(n, n + count)))
        n += count
    return steps


def shape_tables():
    rows = np.arange(P)
    lane = rows % 64
    freq = (1.0 / np.float32(100000.0) ** (np.arange(0, ROPE, 2, dtype=np.float32) / np.float32(ROPE))).astype(np.float32)
    angle = np.outer(np.arange(L, dtype=np.float32), freq).astype(np.float32)
    cos, sin = np.zeros((P, L), np.float32), np.zeros((P, L), np.float32)
    for r in rows:
        if lane[r] < ROPE:
            cos[r] = np.cos(angle[:, lane[r] // 2])
            sin[r] = np.sin(angle[:, lane[r] // 2]) * (1 if lane[r] % 2 else -1)
        elif lane[r] < ROPE + LAT:
            cos[r] = 1.0
        elif lane[r] == KD - 1:
            sin[r] = 1.0
    one_row = (lane == KD - 1).astype(np.float32)[:, None]
    part = np.arange(96) % 32
    sel_bc = (part[:, None, None] == np.arange(32)[None, :, None]) * np.ones((1, 1, P))
    lower = np.tile((np.arange(E)[None, :] < np.arange(E)[:, None]).reshape(1, E * E), (P, 1))
    sel_den = rows[:, None] == 32 * np.arange(4)[None, :] + LAT
    tile_col = np.arange(MT * P)
    sel_comb = np.arange(E)[:, None] == tile_col[None, :] // I1
    tables = {
        "ident": np.eye(P), "sel_bc": sel_bc.reshape(96, 32 * P), "mask": np.where(rows[None, :] > rows[:, None], MASKED, 0.0),
        "mask_t": np.where(rows[:, None] > rows[None, :], MASKED, 0.0), "cos": cos, "sin": sin, "one_row": one_row,
        "before": rows[:, None] < rows[None, :], "ones": np.ones((P, P)),
        "steps": np.tile(np.arange(T) * P, (P, 1)), "tiles": np.tile(np.arange(NT), (P, 1)),
        "lower": lower, "sel_den": sel_den, "sel_comb": sel_comb}
    return {k: np.ascontiguousarray(v.astype(np.float32)) for k, v in tables.items()}


def lay_out(i):
    def column(a):
        return a.reshape(-1, 1)

    def padded(a, width):
        return np.concatenate([a, np.zeros((*a.shape[:-1], width - a.shape[-1]), a.dtype)], axis=-1)
    swap = np.arange(ROPE) ^ 1
    wq = i["L1_ffn_Wq"].reshape(P, H, 64)
    rope = wq[:, :, 32:]
    wkva = i["L1_ffn_Wkva"]
    k_rope, k_lat = wkva[:, LAT:], wkva[:, :LAT]
    wkvb = i["L1_ffn_Wkvb"].reshape(LAT, H, 32)
    wo = i["L1_ffn_Wo"].reshape(H, 64, P)
    bc = np.concatenate([i["L0_attn_WB"], i["L0_attn_WC"]], axis=1)
    bbc = np.concatenate([i["L0_attn_bB"], i["L0_attn_bC"]])

    def experts_in(routed, shared):
        r = routed.transpose(1, 0, 2).reshape(P, E * I1)
        return np.concatenate([r, padded(shared[0], P)], axis=1)
    wexp = np.concatenate([i["L0_ffn_wg_w"].transpose(2, 0, 1), i["L0_ffn_w1_w"].transpose(2, 0, 1),
                           i["L0_ffn_w2_w"].reshape(E, P, FT, P).transpose(3, 0, 2, 1).reshape(P, E, FF)], axis=2)
    bexp = np.concatenate([i["L0_ffn_wg_b"], i["L0_ffn_w1_b"], i["L0_ffn_w2_b"]], axis=1)
    down = i["L1_ffn_Wd"].reshape(MT, P, P).transpose(1, 0, 2)
    down_shared = np.concatenate([i["L1_ffn_sWd"][0], np.zeros((P - I1, P), np.float32)])[:, None, :]
    return {
        "wz": i["L0_attn_Wz"], "wx": i["L0_attn_Wx"], "wdt": i["L0_attn_Wdt"], "wbc": np.concatenate([bc] * 3, axis=1),
        "a_log": i["L0_attn_A_log"], "wout": i["L0_attn_Wout"], "bz": column(i["L0_attn_bz"]), "bx": column(i["L0_attn_bx"]),
        "bdt": column(i["L0_attn_bdt"]), "bbc": column(np.concatenate([bbc] * 3)), "bout": i["L0_attn_bout"].reshape(1, P),
        "router0": i["L0_ffn_router_w"].T, "wexp": wexp.reshape(P, E * XW), "bexp": bexp.reshape(P, E * XB // P),
        "wq1": i["L1_attn_WQ"], "wk1": i["L1_attn_WK"], "wv1": i["L1_attn_WV"],
        "ln1": column(i["L1_ffn_w_ln1"]), "ln2": column(i["L1_ffn_w_ln2"]),
        "wq": padded(rope, 64).reshape(P, HP * P), "wq_swap": padded(rope[:, :, swap], 64).reshape(P, HP * P),
        "wk": np.concatenate([padded(np.concatenate([k_rope, k_lat], axis=1), 64)] * 2, axis=1),
        "wk_swap": np.concatenate([padded(k_rope[:, swap], 64)] * 2, axis=1),
        "wq_nope_t": wq[:, :, :32].transpose(2, 1, 0).reshape(32, H * P),
        "wkvb_t": wkvb.transpose(2, 1, 0).reshape(32, H * LAT),
        "wo_nope": wo[:, :32].transpose(1, 0, 2).reshape(32, H * P), "wlat": k_lat,
        "router1": i["L1_ffn_Wgate"], "bias1": i["L1_ffn_expert_bias"].reshape(1, E),
        "wg1": experts_in(i["L1_ffn_Wg"], i["L1_ffn_sWg"]), "wu1": experts_in(i["L1_ffn_Wu"], i["L1_ffn_sWu"]),
        "wd1": np.concatenate([down, down_shared], axis=1).reshape(P, (MT + 1) * P),
    }


def kernel(**inputs):
    import concourse.bacc as _bacc
    from concourse.bass_utils import run_bass_kernel_spmd as _run

    host = {k: np.asarray(v) for k, v in inputs.items()}
    x = np.ascontiguousarray(host["L0_attn_x"])
    given = {**shape_tables(), **lay_out(host)}
    nc = _bacc.Bacc("TRN2", target_bir_lowering=False, num_devices=1)
    arrays = {"in_x": x}
    x_ap = nc.dram_tensor("in_x", x.shape, F32, kind="ExternalInput").ap()
    w = {}
    for name, _ in WEIGHTS:
        arrays["in_" + name] = np.ascontiguousarray(given[name])
        w[name] = nc.dram_tensor("in_" + name, given[name].shape, F32, kind="ExternalInput").ap()
    out = nc.dram_tensor("out", x.shape, F32, kind="ExternalOutput").ap()
    xs = nc.dram_tensor("sorted_in", (NT * P, P), F32, kind="Internal").ap()
    ys = nc.dram_tensor("sorted_out", (NT * P, P), F32, kind="Internal").ap()
    two_layers(nc, x_ap, w, out, xs, ys)
    r = _run(nc, [arrays], core_ids=[0])
    return r.results[0]["out"]
```

```python
from contextlib import ExitStack

import numpy as np

import concourse.bass as bass
from concourse import mybir

ALU = mybir.AluOpType
ACT = mybir.ActivationFunctionType
AX = mybir.AxisListType.X
F32 = mybir.dt.float32
BF16 = mybir.dt.bfloat16
F32R = mybir.dt.float32r
U32 = mybir.dt.uint32

P = 128
B, L = 8, 512
J = L // P
NS = 16
E, FF = 8, 512
FT = FF // P
H, HP = 16, 8
ROPE, LAT = 32, 16
KD = ROPE + LAT + 1
I1 = 64
MT = E * I1 // P
EPS = 1e-5
MASKED = -1e30
T = B * J
NT = T * 2 + E
PASSES = 2
TP = NT // PASSES
XW = 3 * FF
XB = 2 * FF + P

WEIGHTS = [
    ("ident", [P, P]), ("sel_bc", [96, 32]), ("mask", [P, P]), ("mask_t", [P, P]), ("cos", [P, L]), ("sin", [P, L]),
    ("one_row", [P, 1]), ("lower", [P, E * E]), ("sel_den", [P, 4]), ("sel_comb", [3 * E, MT * P]),
    ("wz", [P, P]), ("wx", [P, P]), ("wdt", [P, P]), ("wbc", [P, 96]), ("a_log", [P, NS]), ("wout", [P, P]),
    ("bz", [P, 1]), ("bx", [P, 1]), ("bdt", [P, 1]), ("bbc", [96, 1]), ("bout", [P, P]),
    ("router0", [P, E]), ("wexp", [P, E * XW]), ("bexp", [P, E * XB // P]),
    ("before", [P, P]), ("ones", [P, P]), ("steps", [P, T]), ("tiles", [P, NT]),
    ("wq1", [P, P]), ("wk1", [P, P]), ("wv1", [P, P]),
    ("ln1", [P, 1]), ("ln2", [P, 1]), ("wq", [P, HP * P]), ("wq_swap", [P, HP * P]), ("wk", [P, P]), ("wk_swap", [P, P]),
    ("wq_nope_t", [32, H * P]), ("wkvb_t", [32, H * LAT]), ("wo_nope", [32, H * P]), ("wlat", [P, LAT]),
    ("router1", [P, E]), ("bias1", [P, E]), ("wg1", [P, (MT + 1) * P]), ("wu1", [P, (MT + 1) * P]), ("wd1", [P, (MT + 1) * P]),
]
SETUP_ONLY = {"sel_bc", "sel_comb", "mask", "mask_t", "wq_nope_t", "wkvb_t", "wo_nope", "a_log", "bexp"}
LAYER0_ONLY = {"wexp", "before", "steps", "tiles", "router0"}
LATE = {"wexp", "cos", "sin", "wk", "wk_swap", "wq_swap", "wq1", "wk1", "wv1", "wg1", "wu1", "wd1", "ln1", "ln2", "one_row",
        "sel_den", "wlat", "router1", "bias1"}
BROADCAST = {"bout", "bias1"}


def two_layers(nc, x, w, out, xs, ys):
    with ExitStack() as ctx:
        def sb(name, shape, dt=F32):
            return ctx.enter_context(nc.sbuf_tensor(name, shape, dt))

        def sems(names, scope=ctx):
            return [scope.enter_context(nc.semaphore(n)) for n in names.split()]

        def sems_of_stage(names, scope, taken):
            first = setup_rows.num + 1 + len(taken)
            found = [scope.enter_context(nc.semaphore(n, num=first + i)) for i, n in enumerate(names.split())]
            taken += found
            return found

        c = {name: sb("c_" + name, shape) for name, shape in WEIGHTS
             if name not in SETUP_ONLY | LAYER0_ONLY}
        bank = [ctx.enter_context(nc.psum_tensor(f"bank{i}", [P, 2, L], F32)) for i in range(4)]

        def bk(i):
            return bank[i // 2][:, i % 2, :]

        ident16 = sb("ident16", [P, P], BF16)
        mask16 = sb("mask16", [P, P], BF16)
        mask_t16 = sb("mask_t16", [P, P], BF16)
        neg_a = sb("neg_a", [P, NS])
        half_bz = sb("half_bz", [P, 1])
        minus_half = sb("minus_half", [P, J])
        eps = sb("eps", [P, 1])
        wvo = sb("wvo", [P, 4, P])
        vaug = sb("vaug", [P, J, 32])
        sel_comb16 = sb("sel_comb16", [3 * E, MT * P], BF16)
        xn_t_all = sb("xn_t_all", [P, (B + 1) * L])
        scan = scan_tiles(nc, ctx)
        sel_bc = sb("sel_bc16", [96, 32, P], BF16)
        gate2 = sb("gate2", [P, 2, T + J])
        slot2 = sb("slot2", [P, 2, T + J], U32)

        only0 = ctx.enter_context(ExitStack())
        expert_of = only0.enter_context(nc.sbuf_tensor("expert_of", [P, NT], U32))
        bias16 = only0.enter_context(nc.sbuf_tensor("bias16", [3, E * XB], BF16))
        ones16 = only0.enter_context(nc.sbuf_tensor("ones16", [3, P], BF16))
        for name, shape in WEIGHTS:
            if name in LAYER0_ONLY:
                c[name] = only0.enter_context(nc.sbuf_tensor("c_" + name, shape, F32))
        rows_scattered, rows_gathered, late_in = sems("rows_scattered rows_gathered late_in")
        (setup_in, setup_mm, setup_act, setup_dve, setup_done, setup_bias, setup_rows) = sems(
            "setup_in setup_mm setup_act setup_dve setup_done setup_bias setup_rows")

        with ExitStack() as own:
            for name, shape in WEIGHTS:
                if name in SETUP_ONLY:
                    c[name] = own.enter_context(nc.sbuf_tensor("c_" + name, shape, F32))
            bias_part = own.enter_context(nc.sbuf_tensor("bias_part", [P, 3, E * XB // P], BF16))
            bias_rest = own.enter_context(nc.sbuf_tensor("bias_rest", [P, 2, E * XB // P], F32))
            with nc.Block() as block:
                @block.sync
                def _(sp):
                    for name, shape in WEIGHTS:
                        if name not in LATE:
                            src = w[name].partition_broadcast(P) if name in BROADCAST else w[name]
                            sp.dma_start(c[name][:, :], src).then_inc(setup_in, 16)
                    sp.wait_ge(setup_bias, 5)
                    for part in range(3):
                        sp.dma_start(bias16[part:part + 1, :], bias_part[:, part, :]).then_inc(setup_rows, 16)
                    sp.wait_ge(setup_rows, 48)
    
                @block.vector
                def _(dve):
                    nc.vector.memset(eps[:], EPS)
                    nc.vector.memset(minus_half[:], -0.5)
                    nc.vector.memset(gate2[:, :, T:], 0.0)
                    nc.vector.memset(slot2[:, :, T:], 0)
                    nc.vector.memset(xn_t_all[:, B * L:], 0.0)
                    nc.vector.memset(wvo[:], 0.0).then_inc(setup_dve, 1)
                    nc.vector.memset(vaug[:], 0.0).then_inc(setup_dve, 1)
                    dve.wait_ge(setup_dve, 2)
                    nc.vector.memset(vaug[:, :, LAT:LAT + 1], 1.0)
                    dve.wait_ge(setup_in, 16 * (len(WEIGHTS) - len(LATE)))
                    nc.vector.tensor_copy(sel_bc[:], c["sel_bc"][:].unsqueeze(2).to_broadcast([96, 32, P]))
                    nc.vector.memset(ones16[:], 1.0)
                    split = chain_of(dve, setup_bias)
                    split(nc.vector.tensor_copy(bias_part[:, 0, :], c["bexp"][:]))
                    split(nc.vector.tensor_tensor(bias_rest[:, 0, :], c["bexp"][:], bias_part[:, 0, :], ALU.subtract))
                    split(nc.vector.tensor_copy(bias_part[:, 1, :], bias_rest[:, 0, :]))
                    split(nc.vector.tensor_tensor(bias_rest[:, 1, :], bias_rest[:, 0, :], bias_part[:, 1, :], ALU.subtract))
                    split(nc.vector.tensor_copy(bias_part[:, 2, :], bias_rest[:, 1, :]))
                    nc.vector.tensor_copy(ident16[:], c["ident"][:])
                    nc.vector.tensor_copy(mask16[:], c["mask"][:])
                    nc.vector.tensor_copy(sel_comb16[:], c["sel_comb"][:])
                    nc.vector.tensor_copy(mask_t16[:], c["mask_t"][:])
                    nc.vector.tensor_scalar(half_bz[:], c["bz"][:], 0.5, None, ALU.mult)
                    dve.wait_ge(setup_act, 1)
                    nc.vector.tensor_scalar(neg_a[:], neg_a[:], -1.0, None, ALU.mult)
                    dve.wait_ge(setup_mm, 1)
                    nc.vector.tensor_copy(
                        c["wq"][:].rearrange("p (h f) -> p h f", h=H)[:, :, ROPE:ROPE + LAT],
                        bk(0)[:, 0:H * LAT].rearrange("p (h f) -> p h f", h=H))
                    for s in range(4):
                        last = nc.vector.tensor_copy(wvo[32 * s:32 * s + LAT, :, :],
                                                     bk(2)[32 * s:32 * s + LAT, :].rearrange("p (g f) -> p g f", g=4))
                    last.then_inc(setup_done, 1)
                    dve.wait_ge(setup_done, 1)
    
                @block.scalar
                def _(act):
                    act.wait_ge(setup_in, 16 * (len(WEIGHTS) - len(LATE)))
                    nc.scalar.activation(neg_a[:], c["a_log"][:], ACT.Exp).then_inc(setup_act, 1)
    
                @block.tensor
                def _(pe):
                    pe.wait_ge(setup_in, 16 * (len(WEIGHTS) - len(LATE)))
                    for h in range(H):
                        nc.tensor.matmul(bk(0)[:, h * LAT:(h + 1) * LAT], c["wq_nope_t"][:, h * P:(h + 1) * P],
                                         c["wkvb_t"][:, h * LAT:(h + 1) * LAT], start=True, stop=True)
                    for h in range(H):
                        s, g = h % 4, h // 4
                        last = nc.tensor.matmul(bk(2)[32 * s:32 * s + LAT, g * P:(g + 1) * P],
                                                c["wkvb_t"][:, h * LAT:(h + 1) * LAT],
                                                c["wo_nope"][:, h * P:(h + 1) * P], start=True, stop=True)
                    last.then_inc(setup_mm, 1)
    
            nc.all_engine_barrier()

        route(nc, sems_of_stage, bk, c, x, xs, locals())
        experts0(nc, sems_of_stage, bk, c, xs, ys, locals())
        only0.close()
        nc.all_engine_barrier()
        layer1(nc, sems_of_stage, bk, bank, c, x, ys, out, locals())


def chain_of(eng, sem):
    count = [0]

    def link(ins):
        count[0] += 1
        ins.then_inc(sem, 1)
        eng.wait_ge(sem, count[0])
    return link


def span(taken):
    return range(taken[0].num, taken[0].num + len(taken))


def flat(t):
    return t.rearrange("p a b -> p (a b)")


SCAN_SEMS = ("sc_copied sc_proj sc_dt_parts sc_dt_read sc_bc32 sc_bc16 sc_dt sc_u sc_tanh sc_a sc_spread sc_hc sc_added sc_yz sc_out_psum sc_done "
             "sc_act_chain sc_dve_chain")


def scan_tiles(nc, ctx):
    def sb(name, shape, dt=F32):
        return ctx.enter_context(nc.sbuf_tensor("sc_" + name, shape, dt))
    return dict(
        xn_t=sb("xn_t", [P, L]), relu_dt=sb("relu_dt", [P, L]), log_dt=sb("log_dt", [P, L]), dt=sb("dt", [P, L]),
        bc32=sb("bc32", [96, L]), r1=sb("r1", [96, L]), r2=sb("r2", [96, L]), mid=sb("mid", [96, L], BF16),
        bc16=sb("bc16", [96, L], BF16), z=sb("z", [P, L]), u=sb("u", [P, L]), a_bar=sb("a_bar", [P, 4, L]),
        ub=sb("ub", [P, L]), state=sb("state", [P, L]), hc=sb("hc", [P, 2, L]), y=sb("y", [P, L]), yz=sb("yz", [P, L]),
        rows=sb("rows", [P, J, P]))


class Scan:

    def __init__(self, nc, t, c, bk, s):
        self.nc, self.t, self.c, self.bk, self.s = nc, t, c, bk, s
        self.v = t["scan"]

    def copy_in(self, pool, batch):
        v, s = self.v, self.s
        self.nc.gpsimd.tensor_copy(v["xn_t"][:], self.t["xn_t_all"][:, bass.ds(batch * L, L)]).then_inc(s["sc_copied"], 1)

    def project(self, pe, what):
        mm, v, s, c, bk = self.nc.tensor.matmul, self.v, self.s, self.c, self.bk
        w, o, rows = {"dt": (c["wdt"], 6, P), "bc": (c["wbc"], 7, 96), "x": (c["wx"], 6, P), "z": (c["wz"], 7, P)}[what]
        if what == "dt":
            pe.wait_ge(s["sc_copied"], 1)
        elif what == "x":
            pe.wait_ge(s["sc_dt_read"], 1)
        elif what == "z":
            pe.wait_ge(s["sc_bc32"], 1)
        mm(bk(o)[0:rows, :], w[:], v["xn_t"][:], start=True, stop=True).then_inc(s["sc_proj"], 1)

    def spread(self, pe, n):
        mm, v, s, bk = self.nc.tensor.matmul, self.v, self.s, self.bk
        if n == 0:
            pe.wait_ge(s["sc_bc16"], 1)
            pe.wait_ge(s["sc_u"], 1)
            pe.wait_ge(s["sc_tanh"], 1)
        else:
            pe.wait_ge(s["sc_hc"], n)
        mm(bk(6), self.t["sel_bc"][:, n, :], v["bc16"][:], start=True, stop=True)
        mm(bk(7), self.t["sel_bc"][:, NS + n, :], v["bc16"][:], start=True, stop=True).then_inc(s["sc_spread"], 1)

    def project_out(self, pe):
        mm, v, s = self.nc.tensor.matmul, self.v, self.s
        pe.wait_ge(s["sc_yz"], 1)
        for j in range(J):
            last = mm(self.bk(6)[:, j * P:(j + 1) * P], v["yz"][:, j * P:(j + 1) * P], self.c["wout"][:], start=True, stop=True)
        last.then_inc(s["sc_out_psum"], 1)

    def take_bc(self, act):
        af, v, s = self.nc.scalar.activation, self.v, self.s
        act.wait_ge(s["sc_proj"], 2)
        af(v["bc32"][:], self.bk(7)[0:96, :], ACT.Identity, bias=self.c["bbc"][:]).then_inc(s["sc_act_chain"], 1)
        act.wait_ge(s["sc_act_chain"], 1)
        af(v["bc16"][:], v["bc32"][:], ACT.Copy).then_inc(s["sc_bc32"], 1)

    def take_dt(self, act):
        af, v, s, c = self.nc.scalar.activation, self.v, self.s, self.c
        act.wait_ge(s["sc_proj"], 2)
        af(v["log_dt"][:], self.bk(6), ACT.Abs, bias=c["bdt"][:]).then_inc(s["sc_act_chain"], 1)
        af(v["relu_dt"][:], self.bk(6), ACT.Relu, bias=c["bdt"][:]).then_inc(s["sc_dt_read"], 1)
        act.wait_ge(s["sc_act_chain"], 2)
        af(v["log_dt"][:], v["log_dt"][:], ACT.Exp, scale=-1.0).then_inc(s["sc_act_chain"], 1)
        act.wait_ge(s["sc_proj"], 3)
        af(v["z"][:], self.bk(7), ACT.Tanh, bias=self.t["half_bz"][:], scale=0.5).then_inc(s["sc_tanh"], 1)

    def logarithm(self, act):
        s, v = self.s, self.v
        act.wait_ge(s["sc_act_chain"], 3)
        self.nc.scalar.activation(v["log_dt"][:], v["log_dt"][:], ACT.Ln, bias=1.0).then_inc(s["sc_dt_parts"], 1)

    def decay(self, act, n):
        s, v = self.s, self.v
        if n == 0:
            act.wait_ge(s["sc_dt"], 1)
        if n >= 4:
            act.wait_ge(s["sc_hc"], n - 3)
        self.nc.scalar.activation(v["a_bar"][:, n % 4, :], v["dt"][:], ACT.Exp,
                                  scale=self.t["neg_a"][:, n:n + 1]).then_inc(s["sc_a"], 1)

    def add(self, eng, n):
        s, v = self.s, self.v
        eng.wait_ge(s["sc_hc"], n + 1)
        if n == 0:
            eng.tensor_copy(v["y"][:], v["hc"][:, 0, :]).then_inc(s["sc_added"], 1)
        else:
            eng.wait_ge(s["sc_added"], n)
            eng.tensor_tensor(v["y"][:], v["y"][:], v["hc"][:, n % 2, :], ALU.add).then_inc(s["sc_added"], 1)

    def split_bc(self, dve):
        ve, v, s = self.nc.vector, self.v, self.s
        self.link = link = chain_of(dve, s["sc_dve_chain"])
        dve.wait_ge(s["sc_bc32"], 1)
        link(ve.tensor_tensor(v["r1"][:], v["bc32"][:], v["bc16"][:], ALU.subtract))
        ve.tensor_copy(v["bc16"][32:64, :], v["r1"][32:64, :])
        link(ve.tensor_copy(v["mid"][:], v["r1"][:]))
        link(ve.tensor_tensor(v["r2"][:], v["r1"][:], v["mid"][:], ALU.subtract))
        ve.tensor_copy(v["bc16"][64:96, :], v["r2"][64:96, :]).then_inc(s["sc_bc16"], 1)

    def make_u(self, dve):
        ve, v, s = self.nc.vector, self.v, self.s
        dve.wait_ge(s["sc_dt_parts"], 1)
        ve.tensor_tensor(v["dt"][:], v["relu_dt"][:], v["log_dt"][:], ALU.add).then_inc(s["sc_dt"], 1)
        dve.wait_ge(s["sc_proj"], 4)
        dve.wait_ge(s["sc_dt"], 1)
        ve.scalar_tensor_tensor(v["u"][:], self.bk(6), self.c["bx"][:], v["dt"][:], ALU.add, ALU.mult).then_inc(s["sc_u"], 1)

    def step(self, dve, n):
        ve, v, s, link = self.nc.vector, self.v, self.s, self.link
        dve.wait_ge(s["sc_spread"], n + 1)
        if n == 0:
            dve.wait_ge(s["sc_u"], 1)
        link(ve.tensor_tensor(v["ub"][:], v["u"][:], self.bk(6), ALU.mult))
        dve.wait_ge(s["sc_a"], n + 1)
        if n >= 1:
            dve.wait_ge(s["sc_hc"], n)
        link(ve.tensor_tensor_scan(v["state"][:], v["a_bar"][:, n % 4, :], v["ub"][:], 0.0, ALU.mult, ALU.add))
        if n >= 2:
            dve.wait_ge(s["sc_added"], n - 1)
        ve.tensor_tensor(v["hc"][:, n % 2, :], v["state"][:], self.bk(7), ALU.mult).then_inc(s["sc_hc"], 1)

    def gate(self, dve):
        dve.wait_ge(self.s["sc_added"], NS)
        v = self.v
        self.nc.vector.scalar_tensor_tensor(v["yz"][:], v["z"][:], 1.0, v["y"][:], ALU.add, ALU.mult).then_inc(self.s["sc_yz"], 1)

    def finish(self, dve):
        dve.wait_ge(self.s["sc_out_psum"], 1)
        self.nc.vector.scalar_tensor_tensor(self.v["rows"][:], self.bk(6).rearrange("p (j d) -> p j d", j=J), 0.5,
                                            self.c["bout"][:].unsqueeze(1).to_broadcast([P, J, P]),
                                            ALU.mult, ALU.add).then_inc(self.s["sc_done"], 1)
        dve.wait_ge(self.s["sc_done"], 1)


def route(nc, sems_of_stage, bk, c, x, xs, t):
    xn_t_all, eps = t["xn_t_all"], t["eps"]
    taken = []
    with ExitStack() as own:
        def sb(name, shape, dt=F32):
            return own.enter_context(nc.sbuf_tensor(name, shape, dt))
        rows_all = sb("rows_all", [P, T, P])
        stats = sb("r_stats", [P, T, 6])
        mv = sb("r_mv", [P, T, 2])
        std = sb("r_std", [P, T])
        rstd = sb("r_rstd", [P, T])
        zeros = sb("zeros", [P, NT * P // 8])
        prob = sb("r_prob", [P, T, E])
        small = sb("r_small", [P, T, 4])
        rank = sb("r_rank", [P, T, E])
        cmp_a = t["scan"]["a_bar"][:].rearrange("p a b -> p (a b)").rearrange("p (a b c) -> p a b c", a=T, b=E)
        cmp_b = sb("r_cmp_b", [P, T, E, E])
        picked = sb("picked", [P, T, E])
        upto = sb("upto", [P, E, T])
        slot = sb("slot", [P, T, E])
        n_tiles = sb("n_tiles", [P, E])
        first = sb("first", [P, E])
        chosen = sb("chosen", [P, T, E])
        slot_f = sb("slot_f", [P, 2, T])
        expert_f = sb("expert_f", [P, NT])
        scattered = t["rows_scattered"]
        x_landed = sems_of_stage(" ".join(f"x_landed{b}" for b in range(B)), own, taken)
        names = ("zeroed filled var_ready std_ready xn_ready xnt_psum xnt_ready logits_ready shifted exp_ready gates_ready "
                 "picked_ready counts_psum slots_ready chain")
        s = dict(zip(names.split(), sems_of_stage(" ".join("r_" + n for n in names.split()), own, taken)))
        s.update(zip(SCAN_SEMS.split(), sems_of_stage(" ".join("r_" + n for n in SCAN_SEMS.split()), own, taken)))
        scan = Scan(nc, t, c, bk, s)
        x_v = x.rearrange("b (j p) d -> b p j d", p=P)
        with nc.Block() as block:
            @block.sync
            def _(sp):
                for b in range(B):
                    sp.dma_start(rows_all[:, b * J:(b + 1) * J, :], x_v[b]).then_inc(x_landed[b], 16)
                sp.wait_ge(s["zeroed"], 1)
                fill = xs.rearrange("(q p r) d -> q p (r d)", q=8, p=P)
                for q in range(8):
                    sp.dma_start(fill[q], zeros[:]).then_inc(s["filled"], 16)
                for name, _ in WEIGHTS:
                    if name in LATE:
                        src = t["w"][name].partition_broadcast(P) if name in BROADCAST else t["w"][name]
                        sp.dma_start(c[name][:, :], src).then_inc(t["late_in"], 16)
                sp.wait_ge(t["late_in"], 16 * len(LATE))

            @block.tensor
            def _(pe):
                mm = nc.tensor.matmul
                for b in range(B + 1):
                    if b < B:
                        pe.wait_ge(s["xn_ready"], b + 1)
                        if b >= 4:
                            pe.wait_ge(s["xnt_ready"], b - 3)
                        for j in range(J):
                            last = nc.tensor.transpose(bk(b % 4)[:, j * P:(j + 1) * P], rows_all[:, b * J + j, :], c["ident"][:])
                        last.then_inc(s["xnt_psum"], 1)
                    if b >= 1:
                        pe.wait_ge(s["xnt_ready"], b)
                        for i in range(J * (b - 1), J * b):
                            last = mm(bk(4)[:, i * E:(i + 1) * E], xn_t_all[:, i * P:(i + 1) * P], c["router0"][:],
                                      start=True, stop=True)
                last.then_inc(s["logits_ready"], 1)
                pe.wait_ge(s["picked_ready"], 1)
                mm(bk(5)[:, 0:T * E], c["before"][:], picked[:].rearrange("p a b -> p (a b)"), start=True, stop=True)
                mm(bk(0)[:, 0:T * E], c["ones"][:], picked[:].rearrange("p a b -> p (a b)"), start=True,
                   stop=True).then_inc(s["counts_psum"], 1)
                for what in ("dt", "bc", "z", "x"):
                    scan.project(pe, what)
                for n in range(NS):
                    scan.spread(pe, n)
                scan.project_out(pe)

            @block.scalar
            def _(act):
                af = nc.scalar.activation
                for b in range(B + 1):
                    if b < B:
                        act.wait_ge(s["var_ready"], b + 1)
                        af(std[:, b * J:(b + 1) * J], mv[:, b * J:(b + 1) * J, 1], ACT.Sqrt, bias=eps[:]).then_inc(s["std_ready"], 1)
                    if b >= 1:
                        act.wait_ge(s["xnt_psum"], b)
                        af(xn_t_all[:, (b - 1) * L:b * L], bk((b - 1) % 4), ACT.Copy).then_inc(s["xnt_ready"], 1)
                act.wait_ge(s["shifted"], 1)
                af(prob[:], prob[:], ACT.Exp).then_inc(s["exp_ready"], 1)
                scan.take_bc(act)
                scan.take_dt(act)
                scan.logarithm(act)
                for n in range(NS):
                    scan.decay(act, n)

            @block.gpsimd
            def _(pool):
                nc.gpsimd.memset(zeros[:], 0.0).then_inc(s["zeroed"], 1)
                pool.wait_ge(s["xnt_ready"], 1)
                scan.copy_in(pool, 0)
                pool.wait_ge(s["filled"], 16 * 8)
                pool.wait_ge(s["slots_ready"], 1)
                for i in range(T):
                    for k in range(2):
                        nc.gpsimd.indirect_dma_start(
                            out=xs, out_offset=bass.IndirectOffsetOnAxis(ap=t["slot2"][:, k, i:i + 1], axis=0),
                            in_=rows_all[:, i, :], in_offset=None).then_inc(scattered, 16)
                pool.wait_ge(scattered, 16 * 2 * T)

            @block.vector
            def _(dve):
                link = chain_of(dve, s["chain"])
                v = nc.vector
                for b in range(B + 1):
                    if b < B:
                        dve.wait_ge(x_landed[b], 16)
                        for i in range(b * J, (b + 1) * J):
                            last = v.bn_stats(stats[:, i, :], rows_all[:, i, :])
                        link(last)
                        for i in range(b * J, (b + 1) * J):
                            last = v.bn_aggr(mv[:, i, :], stats[:, i, :])
                        last.then_inc(s["var_ready"], 1)
                    if b >= 1:
                        dve.wait_ge(s["std_ready"], b)
                        link(v.reciprocal(rstd[:, (b - 1) * J:b * J], std[:, (b - 1) * J:b * J]))
                        for i in range((b - 1) * J, b * J):
                            last = v.tensor_scalar(rows_all[:, i, :], rows_all[:, i, :], mv[:, i, 0:1], rstd[:, i:i + 1],
                                                   ALU.subtract, ALU.mult)
                        last.then_inc(s["xn_ready"], 1)
                dve.wait_ge(s["logits_ready"], 1)
                link(v.tensor_copy(prob[:], bk(4)[:, 0:T * E].rearrange("p (j e) -> p j e", j=T)))
                top_two(v, dve, link, dict(prob=prob, small=small, rank=rank, gates=picked, cmp_a=cmp_a, cmp_b=cmp_b, c=c),
                        s, normalise=False)
                dve.wait_ge(s["gates_ready"], 1)
                for k in range(2):
                    link(v.scalar_tensor_tensor(chosen[:], rank[:], float(k), prob[:], ALU.is_equal, ALU.mult))
                    link(v.tensor_reduce(t["gate2"][:, k, 0:T].unsqueeze(2), chosen[:], AX, ALU.add))
                v.tensor_scalar(picked[:], rank[:], 1.5, None, ALU.is_lt).then_inc(s["picked_ready"], 1)
                dve.wait_ge(s["counts_psum"], 1)
                counts = bk(0)[:, 0:T * E].rearrange("p (i e) -> p e i", e=E)
                link(v.tensor_copy(upto[:], counts))
                for e in range(E):
                    last = v.tensor_tensor_scan(slot[:].rearrange("p i e -> p (i e)")[:, e * T:(e + 1) * T], c["ones"][:, 0:T],
                                                upto[:, e, :], 0.0, ALU.mult, ALU.add)
                link(last)
                total = slot[:].rearrange("p i e -> p (i e)").rearrange("p (e i) -> p e i", e=E)
                link(v.tensor_tensor(upto[:], total, upto[:], ALU.subtract))
                over = chosen[:].rearrange("p i e -> p (i e)").rearrange("p (e i) -> p e i", e=E)
                link(v.tensor_tensor(over, total[:, :, T - 1:T].to_broadcast([P, E, T]),
                                     c["steps"][:].unsqueeze(1).to_broadcast([P, E, T]), ALU.is_gt))
                link(v.tensor_reduce(n_tiles[:].unsqueeze(2), over, AX, ALU.add))
                link(v.tensor_tensor_scan(first[:], c["ones"][:, 0:E], n_tiles[:], 0.0, ALU.mult, ALU.add))
                link(v.tensor_tensor(first[:], first[:], n_tiles[:], ALU.subtract))
                link(v.scalar_tensor_tensor(upto[:], first[:].unsqueeze(2).to_broadcast([P, E, T]), float(P), upto[:],
                                            ALU.mult, ALU.add))
                link(v.tensor_tensor(slot[:], bk(5)[:, 0:T * E].rearrange("p (i e) -> p i e", e=E),
                                     upto[:].rearrange("p e i -> p i e"), ALU.add))
                for k in range(2):
                    link(v.scalar_tensor_tensor(chosen[:], rank[:], float(k), slot[:], ALU.is_equal, ALU.mult))
                    link(v.tensor_reduce(slot_f[:, k, :].unsqueeze(2), chosen[:], AX, ALU.add))
                v.tensor_copy(t["slot2"][:, :, 0:T], slot_f[:]).then_inc(s["slots_ready"], 1)
                dve.wait_ge(s["slots_ready"], 1)
                for h in range(0, NT, 32):
                    n = min(32, NT - h)
                    reached = cmp_a[:].rearrange("p a b c -> p (a b) c")[:, 0:n, :]
                    link(v.tensor_tensor(reached, c["tiles"][:, h:h + n].unsqueeze(2).to_broadcast([P, n, E]),
                                         first[:].unsqueeze(1).to_broadcast([P, n, E]), ALU.is_ge))
                    link(v.tensor_reduce(expert_f[:, h:h + n].unsqueeze(2), reached, AX, ALU.add))
                link(v.tensor_scalar(expert_f[:], expert_f[:], -1.0, None, ALU.add))
                link(v.tensor_copy(t["expert_of"][:], expert_f[:]))
                scan.split_bc(dve)
                scan.make_u(dve)
                for n in range(NS):
                    scan.step(dve, n)
                    scan.add(dve, n)
                scan.gate(dve)
                scan.finish(dve)
        nc.all_engine_barrier(sems_to_clear=span(taken))


def experts0(nc, sems_of_stage, bk, c, xs, ys, t):
    wexp, bias16, ones16, expert_of = c["wexp"], t["bias16"], t["ones16"], t["expert_of"]
    taken = []
    with ExitStack() as own:
        def sb(name, shape, dt=F32):
            return own.enter_context(nc.sbuf_tensor(name, shape, dt))
        xrow = sb("xrow", [P, TP, P])
        xcol = sb("xcol", [P, 3, P])
        gel = sb("gel", [P, 2, L])
        hid = sb("hid", [P, 2, L])
        hid_t = sb("hid_t", [P, 2, L])
        yrow = xrow
        names = ("xcol_psum xcol_ready gate_psum up_psum gel_ready hid_ready hid_t_psum hid_t_ready down_psum yrow_ready y_out")
        s = dict(zip(names.split(), sems_of_stage(names, own, taken)))
        PARTS = 4
        part = TP // PARTS
        rows_in = sems_of_stage(" ".join(f"rows_in{k}" for k in range(PARTS)), own, taken)

        with nc.Fori(0, PASSES) as b:
            with nc.Block() as block:
                @block.sync
                def _(sp):
                    for k in range(PARTS):
                        rows = xs[bass.ds(b * (TP * P) + k * (part * P), part * P)]
                        sp.dma_start(xrow[:, k * part:(k + 1) * part, :], rows.rearrange("(m p) d -> p m d", p=P)).then_inc(rows_in[k], 16)
                    for k in range(PARTS):
                        sp.wait_ge(s["yrow_ready"], (k + 1) * part)
                        rows = ys[bass.ds(b * (TP * P) + k * (part * P), part * P)]
                        sp.dma_start(rows.rearrange("(m p) d -> p m d", p=P), yrow[:, k * part:(k + 1) * part, :]).then_inc(s["y_out"], 16)
                    sp.wait_ge(s["y_out"], 16 * PARTS)

                @block.tensor
                def _(pe):
                    mm = nc.tensor.matmul
                    experts = {}

                    def turn_rows(m):
                        if m % part == 0:
                            pe.wait_ge(rows_in[m // part], 16)
                        if m >= 1:
                            pe.wait_ge(s["xcol_ready"], m)
                        nc.tensor.transpose(bk(6)[:, 0:P], xrow[:, m, :], c["ident"][:]).then_inc(s["xcol_psum"], 1)

                    def up(m):
                        pair = 2 * (m % 2)
                        experts[m] = pe.value_load(expert_of[0:1, bass.ds(b * TP + m, 1)], min_val=0, max_val=E - 1)
                        if m >= 2:
                            pe.wait_ge(s["hid_ready"], m - 1)
                        pe.wait_ge(s["xcol_ready"], m + 1)
                        for half, sem in ((0, "gate_psum"), (1, "up_psum")):
                            mm(bk(pair + half), ones16[:], bias16[:, bass.ds(experts[m] * XB + half * FF, FF)], start=True, stop=False)
                            mm(bk(pair + half), xcol[:, m % 3, :], wexp[:, bass.ds(experts[m] * XW + half * FF, FF)],
                               start=False, stop=True).then_inc(s[sem], 1)

                    def turn_hidden(m):
                        pe.wait_ge(s["hid_ready"], m + 1)
                        if m >= 2:
                            pe.wait_ge(s["hid_t_ready"], m - 1)
                        for f in range(FT):
                            last = nc.tensor.transpose(bk(4 + m % 2)[:, f * P:(f + 1) * P], hid[:, m % 2, f * P:(f + 1) * P], c["ident"][:])
                        last.then_inc(s["hid_t_psum"], 1)

                    def down(m):
                        pe.wait_ge(s["hid_t_ready"], m + 1)
                        if m >= 1:
                            pe.wait_ge(s["yrow_ready"], m)
                        mm(bk(7)[:, 0:P], ones16[:], bias16[:, bass.ds(experts[m] * XB + 2 * FF, P)], start=True, stop=False)
                        for f in range(FT):
                            last = mm(bk(7)[:, 0:P], hid_t[:, m % 2, f * P:(f + 1) * P],
                                      wexp[:, bass.ds(experts[m] * XW + (2 * FF + f * P), P)], start=False, stop=(f == FT - 1))
                        last.then_inc(s["down_psum"], 1)

                    turn_rows(0)
                    turn_rows(1)
                    for m in range(TP + 2):
                        if m < TP:
                            up(m)
                        if m + 2 < TP:
                            turn_rows(m + 2)
                        if 1 <= m <= TP:
                            turn_hidden(m - 1)
                        if m >= 2:
                            down(m - 2)

                @block.scalar
                def _(act):
                    af = nc.scalar.activation

                    def take_rows(m):
                        act.wait_ge(s["xcol_psum"], m + 1)
                        if m >= 3:
                            act.wait_ge(s["up_psum"], m - 2)
                        af(xcol[:, m % 3, :], bk(6)[:, 0:P], ACT.Copy).then_inc(s["xcol_ready"], 1)
                    take_rows(0)
                    take_rows(1)
                    for m in range(TP + 1):
                        if m < TP:
                            act.wait_ge(s["gate_psum"], m + 1)
                            if m >= 2:
                                act.wait_ge(s["hid_ready"], m - 1)
                            af(gel[:, m % 2, :], bk(2 * (m % 2)), ACT.Gelu).then_inc(s["gel_ready"], 1)
                        if m + 2 < TP:
                            take_rows(m + 2)
                        if m >= 1:
                            act.wait_ge(s["hid_t_psum"], m)
                            if m >= 3:
                                act.wait_ge(s["down_psum"], m - 2)
                            af(hid_t[:, (m - 1) % 2, :], bk(4 + (m - 1) % 2), ACT.Copy).then_inc(s["hid_t_ready"], 1)

                @block.vector
                def _(dve):
                    v = nc.vector
                    for m in range(TP + 2):
                        if m < TP:
                            dve.wait_ge(s["up_psum"], m + 1)
                            dve.wait_ge(s["gel_ready"], m + 1)
                            if m >= 2:
                                dve.wait_ge(s["hid_t_psum"], m - 1)
                            v.tensor_tensor(hid[:, m % 2, :], bk(1 + 2 * (m % 2)), gel[:, m % 2, :], ALU.mult).then_inc(s["hid_ready"], 1)
                        if m >= 2:
                            dve.wait_ge(s["down_psum"], m - 1)
                            v.tensor_copy(yrow[:, m - 2, :], bk(7)[:, 0:P]).then_inc(s["yrow_ready"], 1)
            nc.all_engine_barrier(sems_to_clear=span(taken))


def top_two(v, dve, link, t, s, normalise):
    prob, small, gates, rank, cmp_a, cmp_b, c = (t[k] for k in "prob small gates rank cmp_a cmp_b c".split())

    n = prob.shape[1]

    def over(col):
        return small[:, :, col:col + 1].to_broadcast([P, n, E])
    link(v.tensor_reduce(small[:, :, 0:1], prob[:], AX, ALU.max))
    v.tensor_tensor(prob[:], prob[:], over(0), ALU.subtract).then_inc(s["shifted"], 1)
    dve.wait_ge(s["exp_ready"], 1)
    link(v.tensor_reduce(small[:, :, 1:2], prob[:], AX, ALU.add))
    link(v.reciprocal(small[:, :, 2:3], small[:, :, 1:2]))
    link(v.tensor_tensor(prob[:], prob[:], over(2), ALU.mult))
    other = prob[:].unsqueeze(2).to_broadcast([P, n, E, E])
    mine = prob[:].unsqueeze(3).to_broadcast([P, n, E, E])
    v.tensor_tensor(cmp_a[:], other, mine, ALU.is_gt)
    link(v.tensor_tensor(cmp_b[:], other, mine, ALU.is_equal))
    lower = c["lower"][:].rearrange("p (a b) -> p a b", a=E).unsqueeze(1).to_broadcast([P, n, E, E])
    link(v.tensor_tensor(cmp_b[:], cmp_b[:], lower, ALU.mult))
    link(v.tensor_tensor(cmp_a[:], cmp_a[:], cmp_b[:], ALU.add))
    link(v.tensor_reduce(rank[:].unsqueeze(3), cmp_a[:], AX, ALU.add))
    if not normalise:
        v.scalar_tensor_tensor(gates[:], rank[:], 1.5, prob[:], ALU.is_lt, ALU.mult).then_inc(s["gates_ready"], 1)
        return
    link(v.scalar_tensor_tensor(gates[:], rank[:], 1.5, prob[:], ALU.is_lt, ALU.mult))
    link(v.tensor_reduce(small[:, :, 3:4], gates[:], AX, ALU.add))
    link(v.reciprocal(small[:, :, 2:3], small[:, :, 3:4]))
    v.tensor_tensor(gates[:], gates[:], over(2), ALU.mult).then_inc(s["gates_ready"], 1)


def layer1(nc, sems_of_stage, bk, bank, c, x, ys, out, t):
    vaug, wvo = t["vaug"], t["wvo"]
    taken = []
    with ExitStack() as own:
        def sb(name, shape, dt=F32):
            return own.enter_context(nc.sbuf_tensor(name, shape, dt))
        xt = sb("xt", [P, J, P])
        stats = sb("stats", [P, J, 6])
        mv = sb("mv", [P, J, 2])
        var_eps = sb("var_eps", [P, J])
        rstd = sb("rstd", [P, J])
        rrms = sb("rrms", [P, J])
        mean_sq = sb("mean_sq", [P, J])
        rrms2 = sb("rrms2", [P, J])
        xn = sb("xn", [P, J, P])
        xn_t = sb("xn_t", [P, L])
        prob = sb("prob", [P, J, E])
        small = sb("small", [P, J, 4])
        cmp_a = sb("cmp_a", [P, J, E, E])
        cmp_b = sb("cmp_b", [P, J, E, E])
        rank = sb("rank", [P, J, E])
        gates = sb("gates", [P, J, E])
        gates_t = sb("gates_t", [3 * E, L], BF16)
        gate_parts = sb("gate_parts", [P, J, 3 * E])
        gate16 = sb("gate16", [P, J, 2 * E], BF16)
        gate_rest = sb("gate_rest", [P, J, E])
        srow = sb("srow", [P, J, P])
        macc = sb("macc", [P, J, P])
        grow = sb("grow", [P, J, P])
        gate_now = sb("gate_now", [P, 2, J])
        slot_now = sb("slot_now", [P, 2, J], U32)
        expert_out = sb("expert_out", [P, 2, J, P])
        ssq = sb("ssq", [P, J])
        xr = sb("xr", [P, J, P])
        xr_t = sb("xr_t", [P, L])
        q1 = sb("q1", [P, L])
        k1 = sb("k1", [P, L])
        v1 = sb("v1", [P, J, P])
        xt_next = sb("xt_next", [P, J, P])
        xm = q1[:].rearrange("p (j d) -> p j d", j=J)
        xm_t = k1
        neg_max1 = sb("neg_max1", [P, J])
        den1 = sb("den1", [P, J])
        rden1 = sb("rden1", [P, J])
        p1 = sb("p1", [P, J, L])
        p1_t = sb("p1_t", [P, J, L])
        kk = grow[:].rearrange("p j d -> p (j d)")
        k_high = sb("k_high", [P, L], F32R)
        k_low = sb("k_low", [P, L], F32R)
        qc = sb("qc", [P, 2, L])
        qs = sb("qs", [P, 2, L])
        q = sb("q", [P, 2, L])
        q_stack = sb("q_stack", [P, 4, 2, L], F32R)
        neg_max = sb("neg_max", [P, 2, J, 2])
        neg_max_t = sb("neg_max_t", [2, 2, L], F32R)
        probs = sb("probs", [P, 3, 2, L])
        o = sb("o", [P, 4, L])
        rec = sb("rec", [P, J, 4])
        rec_wide = macc
        x2 = q[:, 0, :].rearrange("p (j d) -> p j d", j=J)
        grow0 = q[:, 1, :].rearrange("p (j d) -> p j d", j=J)
        hm = [p1[:, n, :] for n in range(MT)] + [p1_t[:, 0, :]]
        silu_g = [p1_t[:, 2, :], p1_t[:, 3, :]]

        rows_gathered = t["rows_gathered"]
        names = ("x_in xt_ready slot_copied moe0_ready silu0_ready var_ready rstd_ready xn_ready xnt_psum rrms_ready xr_ready xrt_psum "
                 "qkv_psum qk_ready v_ready kproj_psum lat_psum vaug_ready rope_used kk_ready kh_ready k_ready s1_psum max1_ready p1_ready pt_psum "
                 "pt_ready av1_psum s1_ready q_psum q_ready high_ready low_ready max_psum max_used nmt_psum nmt_ready "
                 "st_psum p_ready av_done o_ready den_psum recip_ready wide_ready rec_psum yn_ready att_psum x2_ready ssq_ready rrms2_ready "
                 "xm_ready xmt_psum xmt_ready logits_ready shifted exp_ready gates_ready parts_ready gates_psum gates_t_ready "
                 "g1_psum u1_psum comb_psum silu1_ready hm1_ready hm_ready logits_used moe_psum moe_ready silu_ready out_ready stored dve_chain pool_chain")
        s = dict(zip(names.split(), sems_of_stage(" ".join("l1_" + n for n in names.split()), own, taken)))
        s.update(zip(SCAN_SEMS.split(), sems_of_stage(" ".join("l1_" + n for n in SCAN_SEMS.split()), own, taken)))
        row_in = sems_of_stage(" ".join(f"l1_row_in{p}" for p in range(HP)), own, taken)
        scan = Scan(nc, t, c, bk, s)
        key_groups = (((0, 0),), ((1, 0), (3, 3 * P)), ((2, 0),))
        KG = len(key_groups)
        groups = (((3, 0),), ((2, 0), (0, 3 * P)), ((1, 0),))

        def quad_bank(g):
            return bk(4 + (g + 1) % 2)

        def fetch_x(batch):
            nc.sync.dma_start(xt_next[:], x[bass.ds(batch, 1)].rearrange("o (j p) d -> (o p) j d", p=P)).then_inc(s["x_in"], 16)

        def gather(pool, batch):
            nc.gpsimd.tensor_copy(slot_now[:], t["slot2"][:, :, bass.ds(batch * J, J)])
            nc.gpsimd.tensor_copy(gate_now[:], t["gate2"][:, :, bass.ds(batch * J, J)]).then_inc(s["slot_copied"], 1)
            pool.wait_ge(s["slot_copied"], 1)
            for j in range(J):
                for k in range(2):
                    nc.gpsimd.indirect_dma_start(
                        out=expert_out[:, k, j, :], out_offset=None, in_=ys,
                        in_offset=bass.IndirectOffsetOnAxis(ap=slot_now[:, k, j:j + 1], axis=0)).then_inc(rows_gathered, 16)

        def combine(dve, link, gathered):
            v = nc.vector
            dve.wait_ge(rows_gathered, gathered)
            for j in range(J):
                last = v.tensor_scalar(expert_out[:, 0, j, :], expert_out[:, 0, j, :], gate_now[:, 0, j:j + 1], None, ALU.mult)
            link(last)
            for j in range(J):
                last = v.scalar_tensor_tensor(expert_out[:, 0, j, :], expert_out[:, 1, j, :], gate_now[:, 1, j:j + 1],
                                              expert_out[:, 0, j, :], ALU.mult, ALU.add)
            last.then_inc(s["moe0_ready"], 1)

        def silu0(act):
            act.wait_ge(s["moe0_ready"], 1)
            nc.scalar.activation(grow0, expert_out[:, 0, :, :], ACT.Silu).then_inc(s["silu0_ready"], 1)

        def end_layer0(dve, link):
            v = nc.vector
            dve.wait_ge(s["silu0_ready"], 1)
            link(v.tensor_tensor(grow0, t["scan"]["rows"][:], grow0, ALU.mult))
            dve.wait_ge(s["x_in"], 16)
            link(v.tensor_tensor(xt_next[:], xt_next[:], grow0, ALU.add))
            for j in range(J):
                last = v.bn_stats(stats[:, j, :], xt_next[:, j, :])
            link(last)
            for j in range(J):
                last = v.bn_aggr(mv[:, j, :], stats[:, j, :])
            last.then_inc(s["var_ready"], 1)

        def inverse_roots(pool, link):
            g_ = nc.gpsimd
            pool.wait_ge(s["var_ready"], 1)
            link(g_.tensor_scalar(var_eps[:], mv[:, :, 1], EPS, None, ALU.add))
            g_.tensor_tensor(rstd[:], var_eps[:], t["minus_half"][:], ALU.pow).then_inc(s["rstd_ready"], 1)
            pool.wait_ge(s["rstd_ready"], 1)
            link(g_.tensor_tensor(var_eps[:], rstd[:], rstd[:], ALU.mult))
            link(g_.tensor_tensor(var_eps[:], var_eps[:], mv[:, :, 1], ALU.mult))
            link(g_.tensor_scalar(var_eps[:], var_eps[:], EPS, None, ALU.add))
            g_.tensor_tensor(rrms[:], var_eps[:], t["minus_half"][:], ALU.pow).then_inc(s["rrms_ready"], 1)

        def norm_rows(dve):
            v = nc.vector
            dve.wait_ge(s["rstd_ready"], 1)
            for j in range(J):
                last = v.tensor_scalar(xn[:, j, :], xt_next[:, j, :], mv[:, j, 0:1], rstd[:, j:j + 1], ALU.subtract, ALU.mult)
            last.then_inc(s["xn_ready"], 1)

        def scale_rows(dve):
            v = nc.vector
            dve.wait_ge(s["xn_ready"], 1)
            dve.wait_ge(s["rrms_ready"], 1)
            v.tensor_tensor(xr[:], xn[:], rrms[:].unsqueeze(2).to_broadcast([P, J, P]), ALU.mult).then_inc(s["xr_ready"], 1)

        def rows_to_t(o_, rows, sem):
            for j in range(J):
                last = nc.tensor.transpose(bk(o_)[:, j * P:(j + 1) * P], rows[:, j, :], c["ident"][:])
            last.then_inc(s[sem], 1)

        def turn_norms(pe):
            pe.wait_ge(s["xn_ready"], 1)
            rows_to_t(0, xn, "xnt_psum")
            pe.wait_ge(s["xr_ready"], 1)
            rows_to_t(1, xr, "xrt_psum")

        def take_norms(act):
            act.wait_ge(s["xnt_psum"], 1)
            nc.scalar.activation(xn_t[:], bk(0), ACT.Copy)
            act.wait_ge(s["xrt_psum"], 1)
            nc.scalar.activation(xr_t[:], bk(1), ACT.Copy, scale=c["ln1"][:])

        with nc.Block() as block:
            @block.sync
            def _(sp):
                fetch_x(0)

            @block.gpsimd
            def _(pool):
                gather(pool, 0)
                inverse_roots(pool, chain_of(pool, s["pool_chain"]))

            @block.vector
            def _(dve):
                link = chain_of(dve, s["dve_chain"])
                combine(dve, link, 16 * 2 * J)
                end_layer0(dve, link)
                norm_rows(dve)
                scale_rows(dve)

            @block.tensor
            def _(pe):
                turn_norms(pe)

            @block.scalar
            def _(act):
                silu0(act)
                take_norms(act)
        nc.all_engine_barrier(sems_to_clear=span(taken))

        with nc.Fori(0, B) as b:
            with nc.Block() as block:
                @block.sync
                def _(sp):
                    sp.wait_ge(s["xt_ready"], 1)
                    fetch_x(b + 1)

                    def maximum_rows(p):
                        sp.wait_ge(s["nmt_ready"], p + 1)
                        sp.wait_ge(s["low_ready"], p + 1)
                        for parity in range(2):
                            row = 64 * parity + KD - 1
                            sp.dma_start(q_stack[row:row + 1, p % 4, parity, :].bitcast(F32),
                                         neg_max_t[parity:parity + 1, p % 2, :].bitcast(F32)).then_inc(row_in[p], 16)

                    maximum_rows(0)
                    for p in range(HP):
                        if p + 1 < HP:
                            maximum_rows(p + 1)
                    sp.wait_ge(s["out_ready"], 1)
                    sp.dma_start(out[bass.ds(b, 1)].rearrange("o (j p) d -> (o p) j d", p=P), macc[:]).then_inc(s["stored"], 16)
                    sp.wait_ge(s["stored"], 16)

                @block.tensor
                def _(pe):
                    mm = nc.tensor.matmul
                    tr = nc.tensor.transpose
                    ident = c["ident"]


                    def keep_warm(bank_no, n):
                        for _ in range(n):
                            mm(bk(bank_no), t["sel_bc"][:, 0, :], t["sel_bc"][:, 0:J, :].rearrange("p a b -> p (a b)"), start=True, stop=True)
                    mm(bk(0), c["wk"][:], xr_t[:], start=True, stop=True)
                    mm(bk(1), c["wk_swap"][:], xr_t[:], start=True, stop=True).then_inc(s["kproj_psum"], 1)
                    mm(bk(2), c["wq1"][:], xn_t[:], start=True, stop=True)
                    mm(bk(3), c["wk1"][:], xn_t[:], start=True, stop=True).then_inc(s["qkv_psum"], 1)
                    for j in range(J):
                        last = mm(bk(5)[:, j * LAT:(j + 1) * LAT], xr_t[:, j * P:(j + 1) * P], c["wlat"][:], start=True, stop=True)
                    last.then_inc(s["lat_psum"], 1)

                    def query(p):
                        if p <= 1:
                            pe.wait_ge(s["rope_used"], p + 1)
                        else:
                            pe.wait_ge(s["nmt_ready"], p - 1)
                        cols = slice(p * P, (p + 1) * P)
                        mm(bk(0), c["wq"][:, cols], xr_t[:], start=True, stop=True)
                        mm(bk(1), c["wq_swap"][:, cols], xr_t[:], start=True, stop=True).then_inc(s["q_psum"], 1)

                    def maxima(p, g):
                        if g == 0:
                            if p + 1 < HP:
                                pe.wait_ge(s["rope_used"], p + 3)
                            else:
                                pe.wait_ge(s["nmt_ready"], p)
                            if p == 0:
                                pe.wait_ge(s["kh_ready"], 1)
                            pe.wait_ge(s["high_ready"], p + 1)
                        for parity in range(2):
                            if g > 0:
                                pe.wait_ge(s["max_used"], 6 * p + 2 * g + parity - 1)
                            for i, at in groups[g]:
                                n = (i + 1) * P
                                rows = slice(64 * parity, 64 * parity + KD - 1)
                                dst = bank[0][:, parity, at:at + n]
                                mm(dst, q_stack[rows, p % 4, parity, i * P:(i + 1) * P], k_high[rows, 0:n], start=True, stop=False)
                                last = mm(dst[:, i * P:n], t["ident16"][:], t["mask16"][:], start=False, stop=True)
                            last.then_inc(s["max_psum"], 1)

                    def turn_maxima(p):
                        pe.wait_ge(s["max_used"], 6 * (p + 1))
                        for i in range(J):
                            last = tr(bk(0)[0:2, i * P:(i + 1) * P], neg_max[:, p % 2, i, :], ident[:])
                        last.then_inc(s["nmt_psum"], 1)

                    def scores(n):
                        p, kg = divmod(n, KG)
                        if kg == 0:
                            pe.wait_ge(row_in[p], 32)
                        if n == 0:
                            pe.wait_ge(s["k_ready"], 1)
                            pe.wait_ge(s["pt_ready"], J)
                        else:
                            pe.wait_ge(s["p_ready"], n)
                        for kt, at in key_groups[kg]:
                            for parity in range(2):
                                dst = bank[1][:, parity, at:at + L - kt * P]
                                query_t = q_stack[:, p % 4, parity, kt * P:L]
                                mm(dst, k_high[:, kt * P:(kt + 1) * P], query_t, start=True, stop=False)
                                mm(dst, k_low[:, kt * P:(kt + 1) * P], query_t, start=False, stop=False)
                                last = mm(dst[:, 0:P], t["ident16"][:], t["mask_t16"][:], start=False, stop=True)
                        last.then_inc(s["st_psum"], 1)

                    def weigh(n, parity):
                        p, kg = divmod(n, KG)
                        g = p // 2
                        if parity == 0:
                            pe.wait_ge(s["p_ready"], n + 1)
                            if n == 2 * KG:
                                pe.wait_ge(s["s1_ready"], 1)
                            elif n % (2 * KG) == 0 and g >= 2:
                                pe.wait_ge(s["yn_ready"], g - 1)
                        slot = 32 * (2 * (p % 2) + parity)
                        for kt, at in key_groups[kg]:
                            last = mm(quad_bank(g)[slot:slot + 32, kt * P:L], vaug[:, kt, :],
                                      probs[:, n % 3, parity, at:at + L - kt * P], start=(kt == 0), stop=(kg == KG - 1))
                        if parity == 1:
                            last.then_inc(s["av_done"], 1)

                    def denominators(g):
                        pe.wait_ge(s["o_ready"], g + 1)
                        for j in range(J):
                            last = mm(quad_bank(g)[:, 4 * j:4 * j + 4], o[:, g, j * P:(j + 1) * P], c["sel_den"][:],
                                      start=True, stop=True)
                        last.then_inc(s["den_psum"], 1)

                    def spread_reciprocals(g):
                        pe.wait_ge(s["wide_ready"], g + 1)
                        for j in range(J):
                            last = tr(quad_bank(g)[:, j * P:(j + 1) * P], rec_wide[:, j, :], ident[:])
                        last.then_inc(s["rec_psum"], 1)

                    query(0)
                    for j in range(J):
                        last = mm(bk(7)[:, j * P:(j + 1) * P], xn_t[:, j * P:(j + 1) * P], c["wv1"][:], start=True, stop=True)
                    last.then_inc(s["qkv_psum"], 1)
                    pe.wait_ge(s["qk_ready"], 2)
                    for i in range(J):
                        if i == 3:
                            pe.wait_ge(s["vaug_ready"], 1)
                        mm(bk(2 + i)[:, 0:(i + 1) * P], q1[:, i * P:(i + 1) * P], k1[:, 0:(i + 1) * P], start=True, stop=False)
                        mm(bk(2 + i)[:, i * P:(i + 1) * P], t["ident16"][:], t["mask16"][:], start=False,
                           stop=True).then_inc(s["s1_psum"], 1)
                    query(1)
                    scan.project(pe, "dt")
                    maxima(0, 0)
                    pe.wait_ge(s["v_ready"], 1)
                    scan.project(pe, "bc")
                    maxima(0, 1)
                    pe.wait_ge(s["p1_ready"], J)

                    def turn_probabilities(k):
                        for i in range(k, J):
                            last = tr(bk(2 + k)[:, i * P:(i + 1) * P], p1[:, i, k * P:(k + 1) * P], ident[:])
                        last.then_inc(s["pt_psum"], 1)
                    turn_probabilities(0)
                    maxima(0, 2)
                    for k in range(1, J):
                        turn_probabilities(k)
                    turn_maxima(0)
                    query(2)
                    scan.project(pe, "z")
                    maxima(1, 0)
                    scan.project(pe, "x")
                    pe.wait_ge(s["pt_ready"], J)
                    for i in range(J):
                        for k in range(i + 1):
                            last = mm(bk(4)[:, i * P:(i + 1) * P], p1_t[:, k, i * P:(i + 1) * P], v1[:, k, :],
                                      start=(k == 0), stop=(k == i))
                    last.then_inc(s["av1_psum"], 1)

                    for p in range(HP):
                        first = KG * p
                        scores(first)
                        scan.spread(pe, 2 * p)
                        if p + 1 < HP:
                            maxima(p + 1, 1)
                        if p >= 1:
                            weigh(first - 1, 0)
                            weigh(first - 1, 1)
                        scores(first + 1)
                        if p + 1 < HP:
                            maxima(p + 1, 2)
                        weigh(first, 0)
                        if p + 1 < HP:
                            turn_maxima(p + 1)
                        weigh(first, 1)
                        scores(first + 2)
                        if p + 3 < HP:
                            query(p + 3)
                        if p % 2 == 0 and p >= 2:
                            denominators(p // 2 - 1)
                        scan.spread(pe, 2 * p + 1)
                        weigh(first + 1, 0)
                        weigh(first + 1, 1)
                        if p + 2 < HP:
                            maxima(p + 2, 0)
                        if p % 2 == 1 and p >= 3:
                            spread_reciprocals((p - 3) // 2)
                    weigh(KG * HP - 1, 0)
                    weigh(KG * HP - 1, 1)
                    denominators(3)

                    for g in range(4):
                        if g == 3:
                            spread_reciprocals(3)
                        pe.wait_ge(s["yn_ready"], g + 1)
                        if g == 0:
                            pe.wait_ge(s["p_ready"], KG * HP)
                        for j in range(J):
                            last = mm(bk(j)[:, 0:P], o[:, g, j * P:(j + 1) * P], wvo[:, g, :], start=(g == 0), stop=(g == 3))
                    last.then_inc(s["att_psum"], 1)
                    scan.project_out(pe)
                    keep_warm(7, 14)

                    pe.wait_ge(s["xm_ready"], 1)
                    rows_to_t(4, xm, "xmt_psum")
                    pe.wait_ge(s["xmt_ready"], 1)
                    for j in range(J):
                        last = mm(bk(5)[:, j * E:(j + 1) * E], xm_t[:, j * P:(j + 1) * P], c["router1"][:], start=True, stop=True)
                    last.then_inc(s["logits_ready"], 1)
                    def up(n):
                        if n >= 3:
                            pe.wait_ge(s["hm1_ready"], n - 2)
                        a_ = 2 * (n % 3)
                        cols = slice(n * P, (n + 1) * P)
                        mm(bk(a_), c["wg1"][:, cols], xm_t[:], start=True, stop=True).then_inc(s["g1_psum"], 1)
                        if n == 2:
                            pe.wait_ge(s["logits_used"], 1)
                        mm(bk(a_ + 1), c["wu1"][:, cols], xm_t[:], start=True, stop=True).then_inc(s["u1_psum"], 1)
                    for n in range(MT + 1):
                        up(n)
                    pe.wait_ge(s["hm1_ready"], 3)
                    pe.wait_ge(s["parts_ready"], 1)
                    for j in range(J):
                        last = tr(bk(4)[0:3 * E, j * P:(j + 1) * P], gate_parts[:, j, :], ident[:])
                    last.then_inc(s["gates_psum"], 1)
                    pe.wait_ge(s["hm1_ready"], MT + 1)
                    pe.wait_ge(s["gates_t_ready"], 1)
                    for n in range(MT):
                        mm(bk(n), t["sel_comb16"][:, n * P:(n + 1) * P], gates_t[:], start=True, stop=True).then_inc(s["comb_psum"], 1)
                    pe.wait_ge(s["sc_done"], 1)
                    for k, n in enumerate([MT, *range(MT)]):
                        if n < MT:
                            pe.wait_ge(s["hm_ready"], n + 1)
                        for j in range(J):
                            last = mm(bk(4 + j)[:, 0:P], hm[n][:, j * P:(j + 1) * P], c["wd1"][:, n * P:(n + 1) * P],
                                      start=(k == 0), stop=(k == MT))
                    last.then_inc(s["moe_psum"], 1)
                    keep_warm(2, 9)
                    turn_norms(pe)
                    keep_warm(2, 10)

                @block.scalar
                def _(act):
                    af = nc.scalar.activation
                    act.wait_ge(s["qkv_psum"], 1)
                    af(q1[:], bk(2), ACT.Copy).then_inc(s["qk_ready"], 1)
                    af(k1[:], bk(3), ACT.Copy).then_inc(s["qk_ready"], 1)
                    act.wait_ge(s["kk_ready"], 1)
                    af(k_high[:], kk, ACT.Copy).then_inc(s["kh_ready"], 1)
                    def high_parts(p):
                        act.wait_ge(s["q_ready"], p + 1)
                        if p >= 4:
                            act.wait_ge(s["st_psum"], KG * (p - 3))
                        for parity in range(2):
                            rows = slice(64 * parity, 64 * parity + 64)
                            last = af(q_stack[rows, p % 4, parity, :], q[rows, p % 2, :], ACT.Copy)
                        last.then_inc(s["high_ready"], 1)

                    def take_maxima(p):
                        act.wait_ge(s["nmt_psum"], p + 1)
                        if p >= 2:
                            act.wait_ge(row_in[p - 2], 32)
                        af(neg_max_t[:, p % 2, :], bk(0)[0:2, :], ACT.Copy).then_inc(s["nmt_ready"], 1)

                    def take_quad(g):
                        act.wait_ge(s["av_done"], 2 * KG * (g + 1))
                        af(o[:, g, :], quad_bank(g), ACT.Copy).then_inc(s["o_ready"], 1)

                    def exponentials(n):
                        act.wait_ge(s["st_psum"], n + 1)
                        if n >= 3:
                            act.wait_ge(s["av_done"], n - 2)
                        width = sum(L - kt * P for kt, _ in key_groups[n % KG])
                        af(probs[:, n % 3, :, 0:width], bank[1][:, :, 0:width], ACT.Exp, scale=0.125).then_inc(s["p_ready"], 1)
                    high_parts(0)
                    act.wait_ge(s["max1_ready"], 1)
                    for i in range(J):
                        af(p1[:, i, 0:(i + 1) * P], bk(2 + i)[:, 0:(i + 1) * P], ACT.Exp, bias=neg_max1[:, i:i + 1],
                           scale=float(P) ** -0.5, accum_out=den1[:, i:i + 1]).then_inc(s["p1_ready"], 1)
                    high_parts(1)
                    scan.take_bc(act)
                    take_maxima(0)
                    scan.take_dt(act)
                    for k in range(J):
                        act.wait_ge(s["pt_psum"], k + 1)
                        af(p1_t[:, k, k * P:L], bk(2 + k)[:, k * P:L], ACT.Copy).then_inc(s["pt_ready"], 1)
                    scan.logarithm(act)
                    for n in range(3):
                        scan.decay(act, n)
                    for p in range(HP):
                        exponentials(KG * p)
                        if p + 2 < HP:
                            high_parts(p + 2)
                        exponentials(KG * p + 1)
                        if p + 1 < HP:
                            take_maxima(p + 1)
                        if p % 2 == 0 and p >= 2:
                            take_quad(p // 2 - 1)
                        if 2 * p + 3 < NS:
                            scan.decay(act, 2 * p + 3)
                        exponentials(KG * p + 2)
                        if 2 * p + 4 < NS:
                            scan.decay(act, 2 * p + 4)
                    take_quad(3)
                    act.wait_ge(s["x2_ready"], 1)
                    for j in range(J):
                        last = af(grow[:, j, :], x2[:, j, :], ACT.Square, accum_out=ssq[:, j:j + 1])
                    last.then_inc(s["ssq_ready"], 1)
                    act.wait_ge(s["xmt_psum"], 1)
                    af(xm_t[:], bk(4), ACT.Copy, scale=c["ln2"][:]).then_inc(s["xmt_ready"], 1)
                    act.wait_ge(s["shifted"], 1)
                    af(prob[:], prob[:], ACT.Exp).then_inc(s["exp_ready"], 1)
                    for n in range(MT + 1):
                        act.wait_ge(s["g1_psum"], n + 1)
                        if n >= 2:
                            act.wait_ge(s["hm1_ready"], n - 1)
                        af(silu_g[n % 2], bk(2 * (n % 3)), ACT.Silu).then_inc(s["silu1_ready"], 1)
                        if n == 1:
                            silu0(act)
                    act.wait_ge(s["gates_psum"], 1)
                    af(gates_t[:], bk(4)[0:3 * E, :], ACT.Copy).then_inc(s["gates_t_ready"], 1)
                    act.wait_ge(s["ssq_ready"], 1)
                    act.wait_ge(s["moe_ready"], 1)
                    af(grow[:], x2, ACT.Silu).then_inc(s["silu_ready"], 1)
                    take_norms(act)

                @block.gpsimd
                def _(pool):
                    link = chain_of(pool, s["pool_chain"])
                    g_ = nc.gpsimd
                    scan.copy_in(pool, b + 1)
                    g_.tensor_copy(xt[:], xt_next[:]).then_inc(s["xt_ready"], 1)

                    def queries(p):
                        pool.wait_ge(s["rope_used"], p + 2)
                        if p >= 2:
                            pool.wait_ge(s["low_ready"], p - 1)
                        g_.tensor_tensor(q[:, p % 2, :], qc[:, p % 2, :], qs[:, p % 2, :], ALU.add).then_inc(s["q_ready"], 1)

                    def widen(g):
                        pool.wait_ge(s["recip_ready"], g + 1)
                        if g >= 1:
                            pool.wait_ge(s["rec_psum"], g)
                        g_.tensor_copy(rec_wide[:].rearrange("p j (k r) -> p j k r", k=4),
                                       rec[:].unsqueeze(3).to_broadcast([P, J, 4, 32])).then_inc(s["wide_ready"], 1)
                    queries(0)
                    queries(1)
                    gather(pool, b + 1)
                    queries(2)
                    for p in range(HP):
                        scan.add(pool, 2 * p)
                        if p + 3 < HP:
                            queries(p + 3)
                        if p % 2 == 0 and p >= 2:
                            widen(p // 2 - 1)
                        scan.add(pool, 2 * p + 1)
                    widen(3)
                    pool.wait_ge(s["ssq_ready"], 1)
                    link(g_.tensor_scalar(mean_sq[:], ssq[:], 1.0 / P, EPS, ALU.mult, ALU.add))
                    g_.tensor_tensor(rrms2[:], mean_sq[:], t["minus_half"][:], ALU.pow).then_inc(s["rrms2_ready"], 1)
                    inverse_roots(pool, link)

                @block.vector
                def _(dve):
                    link = chain_of(dve, s["dve_chain"])
                    v = nc.vector
                    dve.wait_ge(s["kproj_psum"], 1)
                    v.tensor_tensor(qc[:, 0, :], bk(0), c["cos"][:], ALU.mult)
                    v.scalar_tensor_tensor(qs[:, 0, :], bk(1), c["one_row"][:], c["sin"][:], ALU.add, ALU.mult).then_inc(s["rope_used"], 1)
                    dve.wait_ge(s["rope_used"], 1)
                    v.tensor_tensor(kk, qc[:, 0, :], qs[:, 0, :], ALU.add).then_inc(s["kk_ready"], 1)
                    dve.wait_ge(s["lat_psum"], 1)
                    v.tensor_copy(vaug[:, :, 0:LAT], bk(5)[:, 0:J * LAT].rearrange("p (j f) -> p j f", j=J)).then_inc(s["vaug_ready"], 1)

                    def rope(p):
                        dve.wait_ge(s["q_psum"], p + 1)
                        if p >= 2:
                            dve.wait_ge(s["q_ready"], p - 1)
                        v.tensor_tensor(qc[:, p % 2, :], bk(0), c["cos"][:], ALU.mult)
                        v.tensor_tensor(qs[:, p % 2, :], bk(1), c["sin"][:], ALU.mult).then_inc(s["rope_used"], 1)

                    def low_parts(p):
                        dve.wait_ge(s["high_ready"], p + 1)
                        for parity in range(2):
                            rows = slice(64 * parity, 64 * parity + 64)
                            other = slice(64 - 64 * parity, 128 - 64 * parity)
                            last = v.tensor_tensor(q_stack[other, p % 4, parity, :], q[rows, p % 2, :],
                                                   q_stack[rows, p % 4, parity, :].bitcast(F32), ALU.subtract)
                        last.then_inc(s["low_ready"], 1)

                    def reduce_maxima(p, g):
                        if p >= 2 and g == 0:
                            dve.wait_ge(s["nmt_psum"], p - 1)
                        for parity in range(2):
                            dve.wait_ge(s["max_psum"], 6 * p + 2 * g + parity + 1)
                            for i, at in groups[g]:
                                last = v.tensor_reduce(neg_max[:, p % 2, i, parity:parity + 1], bank[0][:, parity, at:at + (i + 1) * P],
                                                       AX, ALU.max, negate=True)
                            last.then_inc(s["max_used"], 1)

                    def reciprocals(g):
                        dve.wait_ge(s["den_psum"], g + 1)
                        if g >= 1:
                            dve.wait_ge(s["wide_ready"], g)
                        v.reciprocal(rec[:], quad_bank(g)[:, 0:4 * J].rearrange("p (j k) -> p j k", j=J)).then_inc(s["recip_ready"], 1)

                    def normalise(g):
                        dve.wait_ge(s["rec_psum"], g + 1)
                        v.tensor_tensor(o[:, g, :], o[:, g, :], quad_bank(g), ALU.mult).then_inc(s["yn_ready"], 1)

                    dve.wait_ge(s["kk_ready"], 1)
                    rope(0)
                    dve.wait_ge(s["qkv_psum"], 2)
                    v.tensor_copy(flat(v1[:]), bk(7)).then_inc(s["v_ready"], 1)
                    for i in range(J):
                        dve.wait_ge(s["s1_psum"], i + 1)
                        last = v.tensor_reduce(neg_max1[:, i:i + 1], bk(2 + i)[:, 0:(i + 1) * P], AX, ALU.max, negate=True)
                    link(last)
                    v.tensor_scalar(neg_max1[:], neg_max1[:], float(P) ** -0.5, None, ALU.mult).then_inc(s["max1_ready"], 1)
                    rope(1)
                    dve.wait_ge(s["kh_ready"], 1)
                    v.tensor_tensor(k_low[:], kk, k_high[:].bitcast(F32), ALU.subtract).then_inc(s["k_ready"], 1)
                    for g in range(3):
                        reduce_maxima(0, g)
                    low_parts(0)
                    scan.split_bc(dve)
                    rope(2)
                    low_parts(1)
                    reduce_maxima(1, 0)
                    dve.wait_ge(s["p1_ready"], J)
                    link(v.reciprocal(rden1[:], den1[:]))
                    dve.wait_ge(s["av1_psum"], 1)
                    v.tensor_tensor(srow[:], bk(4).rearrange("p (j d) -> p j d", j=J),
                                    rden1[:].unsqueeze(2).to_broadcast([P, J, P]), ALU.mult).then_inc(s["s1_ready"], 1)
                    scan.make_u(dve)
                    for p in range(HP):
                        if p % 2 == 0 and p >= 4:
                            normalise(p // 2 - 2)
                        if p + 1 < HP:
                            reduce_maxima(p + 1, 1)
                            reduce_maxima(p + 1, 2)
                        scan.step(dve, 2 * p)
                        if p + 2 < HP:
                            low_parts(p + 2)
                        if p + 3 < HP:
                            rope(p + 3)
                        scan.step(dve, 2 * p + 1)
                        if p % 2 == 0 and p >= 2:
                            reciprocals(p // 2 - 1)
                        if p + 2 < HP:
                            reduce_maxima(p + 2, 0)
                    normalise(2)
                    reciprocals(3)
                    scan.gate(dve)
                    combine(dve, link, (b + 1) * (16 * 2 * J) + 16 * 2 * J)
                    normalise(3)
                    dve.wait_ge(s["att_psum"], 1)
                    for h in range(2):
                        last = v.tensor_tensor(x2[:, 2 * h:2 * h + 2, :], xn[:, 2 * h:2 * h + 2, :], bank[h][:, :, 0:P], ALU.add)
                    last.then_inc(s["x2_ready"], 1)
                    scan.finish(dve)
                    dve.wait_ge(s["x2_ready"], 1)
                    dve.wait_ge(s["rrms2_ready"], 1)
                    v.tensor_tensor(xm, x2, rrms2[:].unsqueeze(2).to_broadcast([P, J, P]), ALU.mult).then_inc(s["xm_ready"], 1)
                    dve.wait_ge(s["logits_ready"], 1)
                    v.tensor_tensor(prob[:], bk(5)[:, 0:J * E].rearrange("p (j e) -> p j e", j=J),
                                    c["bias1"][:].unsqueeze(1).to_broadcast([P, J, E]), ALU.add).then_inc(s["logits_used"], 1)
                    dve.wait_ge(s["logits_used"], 1)
                    top_two(v, dve, link, dict(prob=prob, small=small, rank=rank, gates=gates, cmp_a=cmp_a, cmp_b=cmp_b, c=c),
                            s, normalise=True)

                    def gated(n):
                        dve.wait_ge(s["u1_psum"], n + 1)
                        dve.wait_ge(s["silu1_ready"], n + 1)
                        v.tensor_tensor(hm[n], bk(2 * (n % 3) + 1), silu_g[n % 2], ALU.mult).then_inc(s["hm1_ready"], 1)
                    gated(0)
                    gated(1)
                    dve.wait_ge(s["gates_ready"], 1)
                    link(v.tensor_copy(gate16[:, :, 0:E], gates[:]))
                    v.tensor_copy(gate_parts[:, :, 0:E], gate16[:, :, 0:E])
                    link(v.tensor_tensor(gate_rest[:], gates[:], gate16[:, :, 0:E], ALU.subtract))
                    link(v.tensor_copy(gate16[:, :, E:], gate_rest[:]))
                    v.tensor_copy(gate_parts[:, :, E:2 * E], gate16[:, :, E:])
                    v.tensor_tensor(gate_parts[:, :, 2 * E:], gate_rest[:], gate16[:, :, E:], ALU.subtract).then_inc(s["parts_ready"], 1)
                    for n in range(2, MT + 1):
                        gated(n)
                    for n in range(MT):
                        dve.wait_ge(s["comb_psum"], n + 1)
                        dve.wait_ge(s["hm1_ready"], n + 1)
                        v.tensor_tensor(hm[n], hm[n], bk(n), ALU.mult).then_inc(s["hm_ready"], 1)
                    end_layer0(dve, link)
                    dve.wait_ge(s["moe_psum"], 1)
                    for h in range(2):
                        last = v.tensor_tensor(x2[:, 2 * h:2 * h + 2, :], x2[:, 2 * h:2 * h + 2, :], bank[2 + h][:, :, 0:P], ALU.add)
                    last.then_inc(s["moe_ready"], 1)
                    norm_rows(dve)
                    dve.wait_ge(s["silu_ready"], 1)
                    link(v.tensor_tensor(macc[:], srow[:], grow[:], ALU.mult))
                    v.tensor_tensor(macc[:], macc[:], xt[:], ALU.add).then_inc(s["out_ready"], 1)
                    scale_rows(dve)
            nc.all_engine_barrier(sems_to_clear=span(taken))


def shape_tables():
    rows = np.arange(P)
    lane = rows % 64
    freq = (1.0 / np.float32(100000.0) ** (np.arange(0, ROPE, 2, dtype=np.float32) / np.float32(ROPE))).astype(np.float32)
    angle = np.outer(np.arange(L, dtype=np.float32), freq).astype(np.float32)
    cos, sin = np.zeros((P, L), np.float32), np.zeros((P, L), np.float32)
    for r in rows:
        if lane[r] < ROPE:
            cos[r] = np.cos(angle[:, lane[r] // 2])
            sin[r] = np.sin(angle[:, lane[r] // 2]) * (1 if lane[r] % 2 else -1)
        elif lane[r] < ROPE + LAT:
            cos[r] = 1.0
        elif lane[r] == KD - 1:
            sin[r] = 1.0
    one_row = (lane == KD - 1).astype(np.float32)[:, None]
    part = np.arange(96) % 32
    sel_bc = part[:, None] == np.arange(32)[None, :]
    lower = np.tile((np.arange(E)[None, :] < np.arange(E)[:, None]).reshape(1, E * E), (P, 1))
    sel_den = rows[:, None] == 32 * np.arange(4)[None, :] + LAT
    tile_col = np.arange(MT * P)
    sel_comb = np.arange(3 * E)[:, None] % E == tile_col[None, :] // I1
    tables = {
        "ident": np.eye(P), "sel_bc": sel_bc, "mask": np.where(rows[None, :] > rows[:, None], MASKED, 0.0),
        "mask_t": np.where(rows[:, None] > rows[None, :], MASKED, 0.0), "cos": cos, "sin": sin, "one_row": one_row,
        "before": rows[:, None] < rows[None, :], "ones": np.ones((P, P)),
        "steps": np.tile(np.arange(T) * P, (P, 1)), "tiles": np.tile(np.arange(NT), (P, 1)),
        "lower": lower, "sel_den": sel_den, "sel_comb": sel_comb}
    return {k: np.ascontiguousarray(v.astype(np.float32)) for k, v in tables.items()}


def lay_out(i):
    def column(a):
        return a.reshape(-1, 1)

    def padded(a, width):
        return np.concatenate([a, np.zeros((*a.shape[:-1], width - a.shape[-1]), a.dtype)], axis=-1)
    swap = np.arange(ROPE) ^ 1
    wq = i["L1_ffn_Wq"].reshape(P, H, 64)
    rope = wq[:, :, 32:]
    wkva = i["L1_ffn_Wkva"]
    k_rope, k_lat = wkva[:, LAT:], wkva[:, :LAT]
    wkvb = i["L1_ffn_Wkvb"].reshape(LAT, H, 32)
    wo = i["L1_ffn_Wo"].reshape(H, 64, P)
    bc = np.concatenate([i["L0_attn_WB"], i["L0_attn_WC"]], axis=1)
    bbc = np.concatenate([i["L0_attn_bB"], i["L0_attn_bC"]])

    def experts_in(routed, shared):
        r = routed.transpose(1, 0, 2).reshape(P, E * I1)
        return np.concatenate([r, padded(shared[0], P)], axis=1)
    wexp = np.concatenate([i["L0_ffn_wg_w"].transpose(2, 0, 1), i["L0_ffn_w1_w"].transpose(2, 0, 1),
                           i["L0_ffn_w2_w"].reshape(E, P, FT, P).transpose(3, 0, 2, 1).reshape(P, E, FF)], axis=2)
    bexp = np.concatenate([i["L0_ffn_wg_b"], i["L0_ffn_w1_b"], i["L0_ffn_w2_b"]], axis=1)
    down = i["L1_ffn_Wd"].reshape(MT, P, P).transpose(1, 0, 2)
    down_shared = np.concatenate([i["L1_ffn_sWd"][0], np.zeros((P - I1, P), np.float32)])[:, None, :]
    return {
        "wz": i["L0_attn_Wz"], "wx": i["L0_attn_Wx"], "wdt": i["L0_attn_Wdt"], "wbc": np.concatenate([bc] * 3, axis=1),
        "a_log": i["L0_attn_A_log"], "wout": i["L0_attn_Wout"], "bz": column(i["L0_attn_bz"]), "bx": column(i["L0_attn_bx"]),
        "bdt": column(i["L0_attn_bdt"]), "bbc": column(np.concatenate([bbc] * 3)), "bout": i["L0_attn_bout"].reshape(1, P),
        "router0": i["L0_ffn_router_w"].T, "wexp": wexp.reshape(P, E * XW), "bexp": bexp.reshape(P, E * XB // P),
        "wq1": i["L1_attn_WQ"], "wk1": i["L1_attn_WK"], "wv1": i["L1_attn_WV"],
        "ln1": column(i["L1_ffn_w_ln1"]), "ln2": column(i["L1_ffn_w_ln2"]),
        "wq": padded(rope, 64).reshape(P, HP * P), "wq_swap": padded(rope[:, :, swap], 64).reshape(P, HP * P),
        "wk": np.concatenate([padded(np.concatenate([k_rope, k_lat], axis=1), 64)] * 2, axis=1),
        "wk_swap": np.concatenate([padded(k_rope[:, swap], 64)] * 2, axis=1),
        "wq_nope_t": wq[:, :, :32].transpose(2, 1, 0).reshape(32, H * P),
        "wkvb_t": wkvb.transpose(2, 1, 0).reshape(32, H * LAT),
        "wo_nope": wo[:, :32].transpose(1, 0, 2).reshape(32, H * P), "wlat": k_lat,
        "router1": i["L1_ffn_Wgate"], "bias1": i["L1_ffn_expert_bias"].reshape(1, E),
        "wg1": experts_in(i["L1_ffn_Wg"], i["L1_ffn_sWg"]), "wu1": experts_in(i["L1_ffn_Wu"], i["L1_ffn_sWu"]),
        "wd1": np.concatenate([down, down_shared], axis=1).reshape(P, (MT + 1) * P),
    }


def kernel(**inputs):
    import concourse.bacc as _bacc
    from concourse.bass_utils import run_bass_kernel_spmd as _run

    host = {k: np.asarray(v) for k, v in inputs.items()}
    x = np.ascontiguousarray(host["L0_attn_x"])
    given = {**shape_tables(), **lay_out(host)}
    nc = _bacc.Bacc("TRN2", target_bir_lowering=False, num_devices=1)
    padded_x = np.concatenate([x, np.zeros((1, *x.shape[1:]), x.dtype)])
    arrays = {"in_x": padded_x}
    x_ap = nc.dram_tensor("in_x", padded_x.shape, F32, kind="ExternalInput").ap()
    w = {}
    for name, _ in WEIGHTS:
        arrays["in_" + name] = np.ascontiguousarray(given[name])
        w[name] = nc.dram_tensor("in_" + name, given[name].shape, F32, kind="ExternalInput").ap()
    out = nc.dram_tensor("out", x.shape, F32, kind="ExternalOutput").ap()
    xs = nc.dram_tensor("sorted_in", (NT * P, P), F32, kind="Internal").ap()
    ys = nc.dram_tensor("sorted_out", (NT * P, P), F32, kind="Internal").ap()
    two_layers(nc, x_ap, w, out, xs, ys)
    r = _run(nc, [arrays], core_ids=[0])
    return r.results[0]["out"]
```
